# Optimizing a Trainium2 kernel written in Bass

```python
import numpy as np
import jax
import jax.numpy as jnp

def _softmax(x, axis=-1):
    return jax.nn.softmax(x, axis=axis)

def _gelu(x):
    return jax.nn.gelu(x, approximate=True)

def _silu(x):
    return jax.nn.silu(x)

def _sigmoid(x):
    return jax.nn.sigmoid(x)

def _layernorm(x, axis=-1, eps=1e-05):
    m = jnp.mean(x, axis=axis, keepdims=True)
    v = jnp.var(x, axis=axis, keepdims=True)
    return (x - m) / jnp.sqrt(v + eps)

def _scatter_add(tgt, idx, src, axis=0):
    return tgt.at[idx].add(src)

def _segment_sum(src, seg, n):
    return jax.ops.segment_sum(src, seg, n)
kernel_name = 'mk_adj_resnorm_d4_adj_r2_d11360'

def setup_inputs(seed: int=0):
    np.random.seed(seed)
    _w = jnp.asarray

    def _rec_inputs():
        import jax
        import jax.numpy as jnp
        _gk = jax.random.key(seed)
        x = 7.22e-05 + 1 * jax.random.normal(jax.random.fold_in(_gk, 1), (16, 512, 128), jnp.float32)
        _a = jax.random.bernoulli(jax.random.fold_in(_gk, 2), 0.00390625, (512, 512))
        _a = jnp.logical_or(_a, jnp.swapaxes(_a, -1, -2))
        _a = jnp.logical_or(_a, jnp.eye(512, dtype=bool))
        _af = _a.astype(jnp.float32)
        _af = _af * jax.random.uniform(jax.random.fold_in(_gk, 3), (512, 512), jnp.float32, 0.05, 0.000976562)
        adj = _af
        return (x, adj)
    x, adj = _rec_inputs()

    def _L0_gnn_setup():
        import jax, jax.numpy as jnp
        import numpy as np
        N_STEPS = 8
        SPATIAL_SCALE = 1.0
        key = jax.random.key(seed)
        ks = jax.random.split(key, 6)
        B, N, D = (32, 512, 128)
        x = jax.random.normal(ks[0], (B, N, D), dtype=jnp.float32)
        adj_mx = jax.random.uniform(ks[1], (N, N), dtype=jnp.float32) / N
        alpha_train = jnp.ones((N,), dtype=jnp.float32)
        w = jnp.eye(D, dtype=jnp.float32) + 0.01 * jax.random.normal(ks[2], (D, D), dtype=jnp.float32)
        d = jax.random.uniform(ks[3], (D,), dtype=jnp.float32)
        fc_in_w = jax.random.normal(ks[4], (D, D), dtype=jnp.float32) * (1.0 / np.sqrt(D))
        fc_in_b = jnp.zeros((D,), dtype=jnp.float32)
        return {'x': x, 'adj_mx': adj_mx, 'alpha_train': alpha_train, 'w': w, 'd': d, 'fc_in_w': fc_in_w, 'fc_in_b': fc_in_b, 'vt': 0}
    _L0_gnn_all = _L0_gnn_setup()
    _L0_gnn_in = {k: v for k, v in _L0_gnn_all.items() if k in ('alpha_train', 'w', 'd', 'fc_in_w', 'fc_in_b')}
    del _L0_gnn_all

    def _L1_gnn_setup():
        import jax, jax.numpy as jnp
        import numpy as np
        EPS = 1e-05

        def _batchnorm(x, gamma, beta):
            mu = jnp.mean(x, axis=0)
            var = jnp.var(x, axis=0)
            return (x - mu) * jax.lax.rsqrt(var + EPS) * gamma + beta
        key = jax.random.key(seed)
        ks = jax.random.split(key, 4)
        b, n, d, h, o = (32, 1024, 128, 256, 128)
        features = jax.random.normal(ks[0], (b, n, d), dtype=jnp.float32)
        A = jax.random.uniform(ks[1], (n, n), dtype=jnp.float32)
        lim1 = float(np.sqrt(6.0 / (d + h)))
        W1 = jax.random.uniform(ks[2], (h, d), minval=-lim1, maxval=lim1, dtype=jnp.float32)
        b1 = jnp.zeros((h,), jnp.float32)
        lim2 = float(np.sqrt(6.0 / (h + o)))
        W2 = jax.random.uniform(ks[3], (o, h), minval=-lim2, maxval=lim2, dtype=jnp.float32)
        b2 = jnp.zeros((o,), jnp.float32)
        g1 = jnp.ones((h,), jnp.float32)
        be1 = jnp.zeros((h,), jnp.float32)
        g2 = jnp.ones((o,), jnp.float32)
        be2 = jnp.zeros((o,), jnp.float32)
        return {'features': features, 'A': A, 'W1': W1, 'b1': b1, 'g1': g1, 'be1': be1, 'W2': W2, 'b2': b2, 'g2': g2, 'be2': be2}
    _L1_gnn_all = _L1_gnn_setup()
    _L1_gnn_in = {k: v for k, v in _L1_gnn_all.items() if k in ('W1', 'b1', 'g1', 'be1', 'W2', 'b2', 'g2', 'be2')}
    del _L1_gnn_all

    def _L2_gnn_setup():
        import jax, jax.numpy as jnp
        import numpy as np
        NEG = -1e+30
        key = jax.random.key(seed)
        ks = jax.random.split(key, 4)
        B, T, C = (4, 2048, 128)
        x = jax.random.normal(ks[0], (B, T, C), dtype=jnp.float32)
        adj_mask = jax.random.normal(ks[1], (T, T), dtype=jnp.float32)
        Wqkv = jax.random.normal(ks[2], (C, 3 * C), dtype=jnp.float32) * (1.0 / np.sqrt(C))
        Wo = jax.random.normal(ks[3], (C, C), dtype=jnp.float32) * (1.0 / np.sqrt(C))
        return {'x': x, 'adj_mask': adj_mask, 'Wqkv': Wqkv, 'Wo': Wo}
    _L2_gnn_all = _L2_gnn_setup()
    _L2_gnn_in = {k: v for k, v in _L2_gnn_all.items() if k in ('Wqkv', 'Wo')}
    del _L2_gnn_all

    def _L3_gnn_setup():
        import jax, jax.numpy as jnp
        import numpy as np
        B, T, D, H = (64, 1024, 128, 128)
        MAX_SKIP = 4

        def _lstm_last(Wih, Whh, bih, bhh, xs):
            N, _, Hd = xs.shape
            bias = bih + bhh

            def step(carry, x_t):
                h, c = carry
                g = x_t @ Wih.T + h @ Whh.T + bias
                i, f, gg, o = jnp.split(g, 4, axis=-1)
                c = jax.nn.sigmoid(f) * c + jax.nn.sigmoid(i) * jnp.tanh(gg)
                h = jax.nn.sigmoid(o) * jnp.tanh(c)
                return ((h, c), None)
            init = (jnp.zeros((N, Hd), xs.dtype), jnp.zeros((N, Hd), xs.dtype))
            (h_last, _), _ = jax.lax.scan(step, init, jnp.swapaxes(xs, 0, 1))
            return h_last
        key = jax.random.key(seed)
        ks = jax.random.split(key, 8)
        s = 0.05
        x = jax.random.normal(ks[0], (B, T, D), jnp.float32)
        adj = jax.random.uniform(ks[1], (T, T), jnp.float32) / T
        Wg0 = jax.random.normal(ks[2], (D, H), jnp.float32) * s
        bg0 = jnp.zeros((H,), jnp.float32)
        Wg1 = jax.random.normal(ks[3], (H, H), jnp.float32) * s
        bg1 = jnp.zeros((H,), jnp.float32)
        Wih = jax.random.normal(ks[4], (MAX_SKIP, 4 * H, H), jnp.float32) * s
        Whh = jax.random.normal(ks[5], (MAX_SKIP, 4 * H, H), jnp.float32) * s
        bih = jax.random.normal(ks[6], (MAX_SKIP, 4 * H), jnp.float32) * s
        bhh = jax.random.normal(ks[7], (MAX_SKIP, 4 * H), jnp.float32) * s
        return dict(x=x, adj=adj, Wg0=Wg0, bg0=bg0, Wg1=Wg1, bg1=bg1, Wih=Wih, Whh=Whh, bih=bih, bhh=bhh)
    _L3_gnn_all = _L3_gnn_setup()
    _L3_gnn_in = {k: v for k, v in _L3_gnn_all.items() if k in ('Wg0', 'bg0', 'Wg1', 'bg1', 'Wih', 'Whh', 'bih', 'bhh')}
    del _L3_gnn_all
    return {'x': x, 'adj': adj, 'L0_gnn_alpha_train': _L0_gnn_in['alpha_train'], 'L0_gnn_w': _L0_gnn_in['w'], 'L0_gnn_d': _L0_gnn_in['d'], 'L0_gnn_fc_in_w': _L0_gnn_in['fc_in_w'], 'L0_gnn_fc_in_b': _L0_gnn_in['fc_in_b'], 'L1_gnn_W1': _L1_gnn_in['W1'], 'L1_gnn_b1': _L1_gnn_in['b1'], 'L1_gnn_g1': _L1_gnn_in['g1'], 'L1_gnn_be1': _L1_gnn_in['be1'], 'L1_gnn_W2': _L1_gnn_in['W2'], 'L1_gnn_b2': _L1_gnn_in['b2'], 'L1_gnn_g2': _L1_gnn_in['g2'], 'L1_gnn_be2': _L1_gnn_in['be2'], 'L2_gnn_Wqkv': _L2_gnn_in['Wqkv'], 'L2_gnn_Wo': _L2_gnn_in['Wo'], 'L3_gnn_Wg0': _L3_gnn_in['Wg0'], 'L3_gnn_bg0': _L3_gnn_in['bg0'], 'L3_gnn_Wg1': _L3_gnn_in['Wg1'], 'L3_gnn_bg1': _L3_gnn_in['bg1'], 'L3_gnn_Wih': _L3_gnn_in['Wih'], 'L3_gnn_Whh': _L3_gnn_in['Whh'], 'L3_gnn_bih': _L3_gnn_in['bih'], 'L3_gnn_bhh': _L3_gnn_in['bhh']}

def reference(x, adj, L0_gnn_alpha_train, L0_gnn_w, L0_gnn_d, L0_gnn_fc_in_w, L0_gnn_fc_in_b, L1_gnn_W1, L1_gnn_b1, L1_gnn_g1, L1_gnn_be1, L1_gnn_W2, L1_gnn_b2, L1_gnn_g2, L1_gnn_be2, L2_gnn_Wqkv, L2_gnn_Wo, L3_gnn_Wg0, L3_gnn_bg0, L3_gnn_Wg1, L3_gnn_bg1, L3_gnn_Wih, L3_gnn_Whh, L3_gnn_bih, L3_gnn_bhh):
    import jax
    import jax.numpy as jnp

    def _L0_gnn_ref(x, adj_mx, alpha_train, w, d, fc_in_w, fc_in_b, vt):
        import jax, jax.numpy as jnp
        import numpy as np
        N_STEPS = 8
        SPATIAL_SCALE = 1.0
        x0 = jax.lax.stop_gradient(x)
        h = jnp.einsum('bnd,ed->bne', x, fc_in_w) + fc_in_b
        alph = jax.nn.sigmoid(alpha_train)[:, None]
        d_clamped = jnp.clip(d, 0.0, 1.0)
        w_eff = w * d_clamped @ w.T
        dt = jnp.float32(SPATIAL_SCALE / N_STEPS)

        def euler_step(h, _):
            ax = jnp.einsum('nm,bmd->bnd', adj_mx, h)
            f = alph * 0.5 * (ax - h) + h @ w_eff - h + x0
            return (h + dt * f, None)
        h, _ = jax.lax.scan(euler_step, h, None, length=N_STEPS)
        return h

    def _L1_gnn_ref(features, A, W1, b1, g1, be1, W2, b2, g2, be2):
        import jax, jax.numpy as jnp
        import numpy as np
        EPS = 1e-05

        def _batchnorm(x, gamma, beta):
            mu = jnp.mean(x, axis=0)
            var = jnp.var(x, axis=0)
            return (x - mu) * jax.lax.rsqrt(var + EPS) * gamma + beta
        b, n, d = features.shape
        A_norm = A + jnp.eye(n, dtype=A.dtype)
        deg = jnp.sum(A_norm, axis=0) + jnp.sum(A_norm, axis=1) - jnp.diagonal(A_norm)
        dinv = jax.lax.rsqrt(deg)
        A_hat = A_norm * dinv[:, None] * dinv[None, :]
        agg = jnp.einsum('nm,bmd->bnd', A_hat, features)
        x = agg.reshape(-1, d)
        h = jax.nn.relu(_batchnorm(x @ W1.T + b1, g1, be1))
        out = h @ W2.T + b2
        out = _batchnorm(out, g2, be2)
        return out.reshape(b, n, -1)

    def _L2_gnn_ref(x, adj_mask, Wqkv, Wo):
        import jax, jax.numpy as jnp
        import numpy as np
        NEG = -1e+30
        B, T, C = x.shape
        qkv = x @ Wqkv
        q, k, v = jnp.split(qkv, 3, axis=-1)
        scale = 1.0 / jnp.sqrt(jnp.asarray(C, dtype=x.dtype))
        scores = jnp.einsum('btd,bsd->bts', q, k) * scale + adj_mask
        causal = jnp.tril(jnp.ones((T, T), dtype=bool))
        scores = jnp.where(causal, scores, NEG)
        attn = jax.nn.softmax(scores, axis=-1)
        y = jnp.einsum('bts,bsd->btd', attn, v)
        return y @ Wo

    def _L3_gnn_ref(x, adj, Wg0, bg0, Wg1, bg1, Wih, Whh, bih, bhh):
        import jax, jax.numpy as jnp
        import numpy as np
        B, T, D, H = (64, 1024, 128, 128)
        MAX_SKIP = 4

        def _lstm_last(Wih, Whh, bih, bhh, xs):
            N, _, Hd = xs.shape
            bias = bih + bhh

            def step(carry, x_t):
                h, c = carry
                g = x_t @ Wih.T + h @ Whh.T + bias
                i, f, gg, o = jnp.split(g, 4, axis=-1)
                c = jax.nn.sigmoid(f) * c + jax.nn.sigmoid(i) * jnp.tanh(gg)
                h = jax.nn.sigmoid(o) * jnp.tanh(c)
                return ((h, c), None)
            init = (jnp.zeros((N, Hd), xs.dtype), jnp.zeros((N, Hd), xs.dtype))
            (h_last, _), _ = jax.lax.scan(step, init, jnp.swapaxes(xs, 0, 1))
            return h_last
        h = jax.nn.relu(jnp.einsum('ts,bsh->bth', adj, x @ Wg0 + bg0))
        h = jax.nn.relu(jnp.einsum('ts,bsh->bth', adj, h @ Wg1 + bg1))
        Bv, Tv, Hd = h.shape
        for p in range(1, MAX_SKIP + 1):
            nw = Tv // p
            wins = h[:, :nw * p, :].reshape(Bv * nw, p, Hd)
            last = _lstm_last(Wih[p - 1], Whh[p - 1], bih[p - 1], bhh[p - 1], wins)
            idx = jnp.arange(nw) * p + (p - 1)
            h = h.at[:, idx, :].set(last.reshape(Bv, nw, Hd))
        return h
    x = _layernorm(x + _L0_gnn_ref(x, adj, L0_gnn_alpha_train, L0_gnn_w, L0_gnn_d, L0_gnn_fc_in_w, L0_gnn_fc_in_b, 0), axis=-1)
    x = _layernorm(x + _L1_gnn_ref(x, adj, L1_gnn_W1, L1_gnn_b1, L1_gnn_g1, L1_gnn_be1, L1_gnn_W2, L1_gnn_b2, L1_gnn_g2, L1_gnn_be2), axis=-1)
    x = _layernorm(x + _L2_gnn_ref(x, adj, L2_gnn_Wqkv, L2_gnn_Wo), axis=-1)
    x = _layernorm(x + _L3_gnn_ref(x, adj, L3_gnn_Wg0, L3_gnn_bg0, L3_gnn_Wg1, L3_gnn_bg1, L3_gnn_Wih, L3_gnn_Whh, L3_gnn_bih, L3_gnn_bhh), axis=-1)
    return x

_drawn_inputs = setup_inputs


def setup_inputs(seed=0):
    import zlib

    import numpy as np

    out = dict(_drawn_inputs(seed))
    spreads = {'L0_gnn_alpha_train': (1.0, 0.6),
     'L0_gnn_fc_in_b': (0.0, 0.303),
     'L1_gnn_b1': (0.0, 0.8),
     'L1_gnn_g1': (1.0, 0.2),
     'L1_gnn_be1': (0.0, 0.1),
     'L1_gnn_b2': (0.0, 0.8),
     'L1_gnn_g2': (1.0, 0.2),
     'L1_gnn_be2': (0.0, 0.1),
     'L3_gnn_bg0': (0.0, 0.8),
     'L3_gnn_bg1': (0.0, 0.8)}
    factors = {'L3_gnn_Wg0': 8.0,
     'L3_gnn_Wg1': 8.0,
     'L3_gnn_Wih': 8.0,
     'L3_gnn_Whh': 8.0,
     'L3_gnn_bih': 2.85,
     'L3_gnn_bhh': 2.905}
    for name, (base, spread) in spreads.items():
        noise = np.random.default_rng([zlib.crc32(name.encode()), seed]).standard_normal(out[name].shape)
        drawn = base * np.exp(spread * noise) if base else spread * noise
        out[name] = jnp.asarray(drawn.astype(out[name].dtype))
    for name, factor in factors.items():
        out[name] = (out[name] * factor).astype(out[name].dtype)
    return out
```

```python
from contextlib import ExitStack

import concourse.bass as bass
from concourse import mybir

F32 = mybir.dt.float32
F32R = mybir.dt.float32r
ACT = mybir.ActivationFunctionType
ALU = mybir.AluOpType
AX = mybir.AxisListType

P = 128
B, N, D = 16, 512, 128
NT = N // P
GB = 4
GROUPS = B // GB
STEPS = 8
DT = 1.0 / STEPS
EI = STEPS + 1
HID = 256
HT = HID // P
SKIPS = 4
GATES = 4
EPS = 1e-5
NEG = -1e30

ROWPACK = {3: (0, 0), 2: (1, 0), 0: (1, 384), 1: (2, 0)}
ROWORDER = (3, 1, 2, 0)
COLPACK = {0: (0, 0), 1: (1, 0), 3: (1, 384), 2: (2, 0)}


def live(b):
    return not isinstance(b, int) or 0 <= b < B


def late(b, n=2):
    return not isinstance(b, int) or b >= n




def pipeline(eng, step, depth):
    head = 2 * ((depth + 3) // 2)
    for t in range(head):
        step(t, t % 2)
    with eng.Fori(head // 2, B // 2) as i:
        step(2 * i, 0)
        step(2 * i + 1, 1)
    for t in range(B, B + depth):
        step(t, t % 2)


def rounds(eng, count, body):
    body(0)
    with eng.Fori(1, count) as i:
        body(i)


def build(nc, ins, out, stop=99, dump=None):
    ctx = ExitStack()
    with ctx:
        def sem(name):
            return ctx.enter_context(nc.semaphore(name))

        def sb(name, shape, dt=F32, where=None):
            return (where or ctx).enter_context(nc.sbuf_tensor(name, shape, dt))

        ps = ctx.enter_context(nc.psum_tensor("banks", [P, 8, 512], F32))

        xn = sb("xn", [P, NT, B, D])
        adj = sb("adj_sb", [P, NT, N])
        ident = sb("ident", [P, P])
        ones = sb("ones", [P, 1])
        mhalf = sb("mhalf", [P, 16])
        w1t = sb("w1t", [P, HID])
        w2t = sb("w2t", [P, HT, P])
        wqk = sb("wqk", [P, P])
        wvo = sb("wvo", [P, P])
        wg0 = sb("wg0", [P, P])
        wg1 = sb("wg1", [P, P])
        cols = sb("cols", [P, 16])
        b1c, g1c, be1c = cols[:, 0:2], cols[:, 2:4], cols[:, 4:6]
        b2c, g2c, be2c = cols[:, 6:7], cols[:, 7:8], cols[:, 8:9]
        stats = sb("stats", [P, 2, 4, 6])
        mv = sb("mv", [P, 2, 4, 2])
        ve = sb("ve", [P, 2, 4])
        rstd = sb("rstd", [P, 2, 4])
        stats2 = sb("stats2", [P, 2, 4, 6])
        mv2 = sb("mv2", [P, 2, 4, 2])
        ve2 = sb("ve2", [P, 2, 4])
        rstd2 = sb("rstd2", [P, 2, 4])

        s0 = ExitStack()
        Mh = sb("Mh", [P, NT, N], F32R, s0)
        Ml = sb("Ml", [P, NT, N], F32R, s0)
        G = sb("G", [P, EI, NT, GB * D], F32, s0)
        Hh = sb("euh", [P, 2, NT, GB * D], F32R, s0)
        Hl = sb("eul", [P, 2, NT, GB * D], F32R, s0)
        tsum = sb("tsum", [P, 2, GB * D], F32, s0)
        Eh = sb("Eh", [P, 3, 3 * P], F32R, s0)
        El = sb("El", [P, 3, 3 * P], F32R, s0)
        Eb = sb("Eb", [P, 3, 3 * P], F32, s0)
        xs = sb("xs", [P, NT, GB, D], F32, s0)
        xTh = sb("xTh", [P, 2, GB * P], F32R, s0)
        xTl = sb("xTl", [P, 2, GB * P], F32R, s0)
        FW = P + 1
        gflat = G[:, :, :, :].rearrange("p i t n -> p (i t n)")
        F = [gflat[:, u * 10 * FW:(u + 1) * 10 * FW].rearrange("p (i n) -> p i n", n=FW) for u in range(2)]
        at = 20 * FW

        def carve(n):
            nonlocal at
            at += n
            return gflat[:, at - n:at]

        w_raw, wT, wTd, W = carve(P), carve(P), carve(P), carve(P)
        d_col, alpha_c, sig, cdt, dgm = carve(1), carve(4), carve(4), carve(4), carve(4)
        Mn = carve(NT * N).rearrange("p (t n) -> p t n", t=NT)
        w1_raw = carve(HT * P).rearrange("p (t n) -> p t n", t=HT)
        w2_raw, wqkv_raw, wo_raw = carve(HID), carve(3 * P), carve(P)
        wqT, wkT, wvT = carve(P), carve(P), carve(P)
        s0.close()

        s1 = ExitStack()
        bsc = sb("bsc", [P, 3], F32, s1)
        bsh = sb("bsh", [P, 3], F32, s1)
        y1 = sb("y1", [P, HT, B, N], F32, s1)
        s1b = ExitStack()
        Ah = sb("Ah", [P, NT, N], F32R, s1b)
        Al = sb("Al", [P, NT, N], F32R, s1b)
        A1 = sb("A1", [P, NT, N], F32, s1b)
        x1h = sb("x1h", [P, 2, NT, D], F32R, s1b)
        x1l = sb("x1l", [P, 2, NT, D], F32R, s1b)
        agg = sb("agg", [P, 2, N], F32, s1b)
        r1 = sb("r1", [P, 2, HT, N], F32, s1b)
        dg = sb("deg", [P, 6, 4], F32, s1b)
        dscr = sb("dscr", [P, P], F32, s1b)
        bst1 = sb("bst1", [P, HT, B, 6], F32, s1b)
        bst2 = sb("bst2", [P, B, 6], F32, s1b)
        bmv = sb("bmv", [P, 3, 2], F32, s1b)
        bve = sb("bve", [P, 3], F32, s1b)
        brs = sb("brs", [P, 3], F32, s1b)
        bms = sb("bms", [P, 3], F32, s1b)
        s1b.close()

        adjm = sb("adjm", [P, NT, N], F32, s1)
        zs = sb("zs", [P, 2, N], F32, s1)
        x2s = sb("x2s", [P, 2, NT, D], F32, s1)
        x2T = sb("x2T", [P, 2, N], F32, s1)
        qT = sb("qT", [P, 2, N], F32, s1)
        vs = sb("vs", [P, 2, NT, D], F32, s1)
        S = sb("S", [P, 2, 3, 512], F32, s1)
        pT = sb("pT", [P, 2, 3, 512], F32, s1)
        mx = sb("mx", [P, 2, 4], F32, s1)
        nmx = sb("nmx", [P, 2, 4], F32, s1)
        es = sb("es", [P, 2, 4], F32, s1)
        rs = sb("rs", [P, 2, 4], F32, s1)
        yb = sb("yb", [P, 2, NT, D], F32, s1)
        s1.close()

        s3 = ExitStack()
        H3h = sb("H3h", [P, B, N], F32R, s3)
        H3l = sb("H3l", [P, B, N], F32R, s3)
        s3a = ExitStack()
        Th = sb("Th", [P, NT, N], F32R, s3a)
        Tl = sb("Tl", [P, NT, N], F32R, s3a)
        Tf = sb("Tf", [P, NT, N], F32, s3a)
        Bm = sb("Bm", [P, N], F32, s3a)
        bg0r = sb("bg0r", [P, P], F32, s3a)
        bg1r = sb("bg1r", [P, NT, P], F32, s3a)
        x3h = sb("x3h", [P, 2, NT, D], F32R, s3a)
        x3l = sb("x3l", [P, 2, NT, D], F32R, s3a)
        a3 = sb("a3", [P, 2, N], F32, s3a)
        h1p = sb("h1p", [P, 2, N], F32, s3a)
        h1 = sb("h1", [P, 2, N], F32, s3a)
        zt = sb("zt", [P, 2, N], F32, s3a)
        zh = sb("zh", [P, 2, N], F32R, s3a)
        zl = sb("zl", [P, 2, N], F32R, s3a)
        s3a.close()
        wih = sb("wih_sb", [P, SKIPS, GATES, P], F32, s3)
        whh = sb("whh_sb", [P, SKIPS, GATES, P], F32, s3)
        LWh = sb("LWh", [P, SKIPS, 2, GATES * P], F32R, s3)
        LWl = sb("LWl", [P, SKIPS, 2, GATES * P], F32R, s3)
        lb = sb("lb", [P, 2, SKIPS, GATES], F32, s3)
        lbias = sb("lbias", [P, SKIPS, GATES], F32, s3)
        ga = sb("ga", [P, 2, GATES, 512], F32, s3)
        cc = sb("cc", [P, 2, 512], F32, s3)
        ig = sb("ig", [P, 2, 512], F32, s3)
        tc = sb("tc", [P, 2, 512], F32, s3)
        hb = sb("hb", [P, 2, 512], F32, s3)
        sth = sb("sth", [P, 2, 512], F32R, s3)
        stl = sb("stl", [P, 2, 512], F32R, s3)
        hs = sb("hs", [P, 2, N], F32, s3)
        fy = sb("fy", [P, 2, NT, D], F32, s3)
        s3.close()

        S_NAMES = """ld_adj ld_w ld_late ld_xs ld_l3 ld_lstm
            c_zero c_ident c_ones c_half c_rows c_fzero
            p_pe p_act p_dve f_mm f_add e_mm e_hi e_lo e_b m_sig m_row m_tr m_hi m_lo w_tr w_cp w_mm w_end
            g_tr g_hi g_lo g_mm g_ev eu_mm eu_sum eu_hi eu_lo
            ln_st ln_ag ln_ve ln_rs ln_ap
            d_row d_col d_dg d_deg d_inv d_a1 d_tr d_hi d_lo
            n_hi n_lo n_agg n_cp n_w1 n_y1 n_st n_r n_w2 n_y2 n_st2 bn_ag bn_ve bn_rs bn_ms bn_sc
            a_msk a_z a_t1 a_add a_x2 a_t2 a_x2T a_q a_v a_qT a_vs a_sc a_s a_nm a_p a_pt a_pts a_pv a_ri a_y
            l_st1 l_ag1 l_ve1 l_rs1 l_st2 l_ag2 l_ve2 l_rs2 a_x3
            t_tr t_hi t_lo t_cp t_bm t_bmc k_hi k_lo k_agg k_cp k_w0 k_add k_h1 k_z k_zt k_zh k_zl k_h2 k_h2h k_h2l
            lw_tr lw_hi lw_lo lw_b
            z_hs z_tr z_y z_st z_ag z_ve z_rs z_ap st_out""".split()
        s = {n: sem(n) for n in S_NAMES}
        lstm = {n: [sem(f"lstm_{n}{u}") for u in range(2)]
                for n in ("mm", "act", "ig", "fc", "c", "tc", "h", "hi", "lo")}

        def rows4(v):
            return [v[:, k * P:(k + 1) * P] for k in range(4)]

        def stage_done(eng, n):
            if n == 0:
                eng.wait_ge(s["ln_ap"], GROUPS * NT)
            elif n == 1:
                eng.wait_ge(s["bn_sc"], 4)
            elif n == 2:
                eng.wait_ge(s["a_x3"], B)
            elif n == 3:
                eng.wait_ge(s["k_h2l"], B)
            elif n == 4:
                for u in range(2):
                    eng.wait_ge(lstm["lo"][u], LSTM_STEPS)

        LB = [1, 2, 2, 4]
        PAIRS = [B // (2 * n) for n in LB]
        NG = [3 + 4 * p for p in range(SKIPS)]
        base_g = [sum(PAIRS[q] * NG[q] for q in range(p)) for p in range(SKIPS + 1)]
        base_s = [sum(PAIRS[q] * (q + 1) for q in range(p)) for p in range(SKIPS + 1)]
        base_r = [sum(PAIRS[q] * q for q in range(p)) for p in range(SKIPS + 1)]
        LSTM_STEPS = base_s[SKIPS]
        NW = [N // (p + 1) for p in range(SKIPS)]
        ORDER = [0, 2, 1, 3]
        FIRST = [0, 2, 3]

        x_v = ins["x"].rearrange("b (t p) d -> p t b d", p=P)
        out_v = out.rearrange("b (t p) d -> p t b d", p=P)

        block = ctx.enter_context(nc.Block())

        @block.sync
        def _(sp):
            def column(dst, src, name):
                sp.dma_start(dst, src.rearrange("(t p) -> p t", p=P), allow_slow_non_contiguous=True).then_inc(s[name], 16)

            sp.dma_start(w_raw, ins["L0_gnn_w"]).then_inc(s["ld_w"], 16)
            column(d_col, ins["L0_gnn_d"], "ld_w")
            sp.wait_ge(s["c_fzero"], 2)
            sp.dma_start(F[0][:, 1, 0:P], ins["L0_gnn_fc_in_w"]).then_inc(s["ld_w"], 16)
            column(F[0][:, 1, P:FW], ins["L0_gnn_fc_in_b"], "ld_w")
            sp.dma_start(adj[:, :, :], ins["adj"].rearrange("(t p) m -> p t m", p=P)).then_inc(s["ld_adj"], 16)
            column(alpha_c, ins["L0_gnn_alpha_train"], "ld_adj")

            def load_group(g):
                for t in range(NT):
                    sp.dma_start(xs[:, t, :, :], x_v[:, t, bass.ds(g * GB, GB), :]).then_inc(s["ld_xs"], 16)

            load_group(0)
            sp.dma_start(w1_raw, ins["L1_gnn_W1"].rearrange("(t p) d -> p t d", p=P)).then_inc(s["ld_late"], 16)
            sp.dma_start(w2_raw, ins["L1_gnn_W2"]).then_inc(s["ld_late"], 16)
            sp.dma_start(wqkv_raw, ins["L2_gnn_Wqkv"]).then_inc(s["ld_late"], 16)
            sp.dma_start(wo_raw, ins["L2_gnn_Wo"]).then_inc(s["ld_late"], 16)
            sp.dma_start(wg0[:, :], ins["L3_gnn_Wg0"]).then_inc(s["ld_late"], 16)
            sp.dma_start(wg1[:, :], ins["L3_gnn_Wg1"]).then_inc(s["ld_late"], 16)
            for dst, name in ((b1c, "b1"), (g1c, "g1"), (be1c, "be1"), (b2c, "b2"), (g2c, "g2"), (be2c, "be2")):
                column(dst, ins[f"L1_gnn_{name}"], "ld_late")
            with sp.Fori(1, GROUPS) as g:
                sp.wait_ge(s["g_tr"], 4 * g)
                load_group(g)
            if stop < 5:
                stage_done(sp, stop)
                for t in range(NT):
                    sp.dma_start(out_v[:, t, :, :], xn[:, t, :, :]).then_inc(s["st_out"], 16)
                sp.wait_ge(s["st_out"], 16 * NT)
                return
            stage_done(sp, 2)
            sp.dma_start(bg0r[:, :], ins["L3_gnn_bg0"].partition_broadcast(P)).then_inc(s["ld_l3"], 16)
            for t in range(NT):
                sp.dma_start(bg1r[:, t, :], ins["L3_gnn_bg1"].partition_broadcast(P)).then_inc(s["ld_l3"], 16)
            stage_done(sp, 3)
            for p in range(SKIPS):
                for dst, name in ((wih, "L3_gnn_Wih"), (whh, "L3_gnn_Whh")):
                    sp.dma_start(dst[:, p, :, :], ins[name][p].rearrange("(g r) h -> r g h", r=P))\
                      .then_inc(s["ld_lstm"], 16)
                for k, name in ((0, "L3_gnn_bih"), (1, "L3_gnn_bhh")):
                    sp.dma_start(lb[:, k, p, :], ins[name][p].rearrange("(g r) -> r g", r=P),
                                 allow_slow_non_contiguous=True)\
                      .then_inc(s["ld_lstm"], 16)
            with sp.Fori(0, B // 2) as i:
                for u in range(2):
                    b = 2 * i + u
                    sp.wait_ge(s["z_ap"], b + 1)
                    sp.dma_start(out_v[:, :, bass.ds(b, 1), :].rearrange("p t b d -> p t (b d)"), fy[:, u, :, :])\
                      .then_inc(s["st_out"], 16)
            sp.wait_ge(s["st_out"], 16 * B)

        @block.gpsimd
        def _(pool):
            pool.memset(ident[:, :], 0.0).then_inc(s["c_zero"], 1)
            for u in range(2):
                pool.memset(F[u], 0.0).then_inc(s["c_fzero"], 1)
            pool.memset(ones[:, :], 1.0).then_inc(s["c_ones"], 1)
            pool.memset(mhalf[:, :], -0.5).then_inc(s["c_half"], 1)
            pool.wait_ge(s["c_zero"], 1)
            pool.affine_select(out=ident[:, :], in_=ident[:, :], compare_op=ALU.not_equal, fill=1.0, base=0,
                               pattern=[[-1, P]], channel_multiplier=1).then_inc(s["c_ident"], 1)
            pool.wait_ge(s["c_half"], 1)

            def inv_sqrt(out_v, ve_v, var_v, eps, s_in, n, s_ve, s_rs, exponent=None):
                e = mhalf[:, 0:ve_v.shape[-1]]
                pool.wait_ge(s_in, n)
                pool.nop(nofuse=True)
                pool.tensor_scalar(ve_v, var_v, eps, None, ALU.add).then_inc(s_ve, 1)
                pool.wait_ge(s_ve, n)
                pool.tensor_tensor(out_v, ve_v, e, ALU.pow).then_inc(s_rs, 1)

            with pool.Fori(0, GROUPS) as g:
                for t in range(NT):
                    inv_sqrt(rstd[:, t % 2, :], ve[:, t % 2, :], mv[:, t % 2, :, 1], EPS,
                             s["ln_ag"], 4 * g + t + 1, s["ln_ve"], s["ln_rs"])
            if stop < 1:
                return
            pool.wait_ge(s["d_deg"], 3)
            pool.tensor_tensor(dg[:, 5, :], dg[:, 4, :], mhalf[:, 0:4], ALU.pow).then_inc(s["d_inv"], 1)
            pool.wait_ge(s["bn_ag"], 2)
            pool.tensor_scalar(bve[:, 0:2], bmv[:, 0:2, 1], EPS, None, ALU.add).then_inc(s["bn_ve"], 1)
            pool.wait_ge(s["bn_ve"], 1)
            pool.tensor_tensor(brs[:, 0:2], bve[:, 0:2], mhalf[:, 0:2], ALU.pow).then_inc(s["bn_rs"], 1)
            pool.wait_ge(s["bn_ag"], 3)
            pool.tensor_scalar(bve[:, 2:3], bmv[:, 2:3, 1], EPS, None, ALU.add).then_inc(s["bn_ve"], 1)
            pool.wait_ge(s["bn_ve"], 2)
            pool.tensor_tensor(brs[:, 2:3], bve[:, 2:3], mhalf[:, 0:1], ALU.pow).then_inc(s["bn_rs"], 1)
            if stop < 2:
                return
            for t in range(NT):
                blk = adjm[:, t, t * P:(t + 1) * P]
                pool.wait_ge(s["a_msk"], 1)
                pool.affine_select(out=blk, in_=blk, compare_op=ALU.is_ge, fill=NEG, base=0,
                                   pattern=[[-1, P]], channel_multiplier=1).then_inc(s["a_msk"], 1)

            def norms(t, u):
                if live(t):
                    inv_sqrt(rstd[:, u, :], ve[:, u, :], mv[:, u, :, 1], EPS, s["l_ag1"], t + 1,
                             s["l_ve1"], s["l_rs1"])
                if live(t - 2):
                    inv_sqrt(rstd2[:, u, :], ve2[:, u, :], mv2[:, u, :, 1], EPS, s["l_ag2"], t - 1,
                             s["l_ve2"], s["l_rs2"])

            pipeline(pool, norms, 2)
            if stop < 5:
                return
            stage_done(pool, 4)

            def last(t, u):
                if live(t):
                    if late(t):
                        pool.wait_ge(s["z_tr"], t - 1)
                    pool.tensor_tensor(hs[:, u, :], H3h[:, bass.ds(t, 1), :].rearrange("p b n -> p (b n)").bitcast(F32),
                                       H3l[:, bass.ds(t, 1), :].rearrange("p b n -> p (b n)").bitcast(F32), ALU.add)\
                        .then_inc(s["z_hs"], 1)
                if live(t - 1):
                    inv_sqrt(rstd[:, 1 - u, :], ve[:, 1 - u, :], mv[:, 1 - u, :, 1], EPS, s["z_ag"], t,
                             s["z_ve"], s["z_rs"])

            pipeline(pool, last, 1)

        @block.scalar
        def _(act):
            def copy(dst, src, name, **kw):
                act.activation(dst, src, ACT.Copy, **kw).then_inc(s[name], 1)

            act.wait_ge(s["ld_adj"], 32)
            act.activation(sig, alpha_c, ACT.Sigmoid).then_inc(s["m_sig"], 1)
            act.wait_ge(s["p_pe"], 1)
            copy(wT, ps[:, 0, 0:P], "p_act")
            act.wait_ge(s["p_pe"], 2)
            copy(W, ps[:, 1, 0:P], "p_act")
            for t in range(NT):
                act.wait_ge(s["m_tr"], t + 1)
                copy(Mh[:, t, :], ps[:, (5, 6, 7, 0)[t], :], "m_hi")
            act.wait_ge(s["w_tr"], 1)
            copy(w1t[:, :], ps[:, 1, 0:HID], "w_cp")
            copy(w2t[:, :, :], ps[:, 1, HID:2 * HID].rearrange("p (t o) -> p t o", t=HT), "w_cp")
            act.wait_ge(s["w_tr"], 2)
            for k, dst in enumerate((wqT, wkT, wvT)):
                copy(dst, ps[:, 5, k * P:(k + 1) * P], "w_cp")
            act.wait_ge(s["w_mm"], 1)
            copy(wqk[:, :], ps[:, 6, 0:P], "w_cp", scale=float(D) ** -0.5)
            copy(wvo[:, :], ps[:, 6, P:2 * P], "w_cp")
            act.wait_ge(s["e_mm"], 1)
            for c in range(3):
                copy(Eh[:, c, :], ps[:, 2 + c, 0:3 * P], "e_hi")
            act.wait_ge(s["e_mm"], 2)
            for c in range(3):
                copy(Eb[:, c, :], ps[:, (7, 0, 1)[c], 0:3 * P], "e_b")

            def euler(g):
                for t in range(NT):
                    act.wait_ge(s["g_tr"], 4 * g + t + 1)
                    if t >= 2:
                        act.wait_ge(s["g_mm"], 16 * g + 4 * (t - 1))
                    copy(xTh[:, t % 2, :], ps[:, 6 + t % 2, :], "g_hi")
                for t in range(NT):
                    act.wait_ge(s["g_ev"], 16 * g + 4 * (t + 1))
                    copy(Hh[:, 0, t, :], G[:, EI - 1, t, :], "eu_hi")
                for st in range(STEPS - 1):
                    for t in range(NT):
                        act.wait_ge(s["eu_sum"], 32 * g + 4 * st + t + 1)
                        copy(Hh[:, (st + 1) % 2, t, :], tsum[:, t % 2, :], "eu_hi")

            rounds(act, GROUPS, euler)
            if stop < 1:
                return
            for t in range(NT):
                act.wait_ge(s["d_tr"], t + 1)
                act.activation(Ah[:, t, :], ps[:, t, :], ACT.Copy, scale=dg[:, 5, t:t + 1]).then_inc(s["d_hi"], 1)

            def gcn(t, u):
                if live(t):
                    if late(t):
                        act.wait_ge(s["n_agg"], t - 1)
                    copy(x1h[:, u, :, :], xn[:, :, bass.ds(t, 1), :].rearrange("p t b d -> p t (b d)"), "n_hi")
                b = t - 1
                if live(b):
                    act.wait_ge(s["n_agg"], b + 1)
                    if late(b):
                        act.wait_ge(s["n_w1"], b - 1)
                    copy(agg[:, 1 - u, :], ps[:, 1 - u, :], "n_cp")
                b = t - 2
                if live(b):
                    act.wait_ge(s["n_w1"], b + 1)
                    for h in range(HT):
                        act.activation(y1[:, h, bass.ds(b, 1), :].rearrange("p b n -> p (b n)"),
                                       ps[:, 2 + 2 * u + h, :], ACT.Identity, bias=b1c[:, h:h + 1])\
                           .then_inc(s["n_y1"], 1)

            act.wait_ge(s["d_lo"], NT)
            pipeline(act, gcn, 2)
            act.wait_ge(s["bn_sc"], 2)

            def hidden(t, u):
                if late(t):
                    act.wait_ge(s["n_w2"], t - 1)
                for h in range(HT):
                    act.activation(r1[:, u, h, :], y1[:, h, bass.ds(t, 1), :].rearrange("p b n -> p (b n)"),
                                   ACT.Relu, scale=bsc[:, h:h + 1], bias=bsh[:, h:h + 1]).then_inc(s["n_r"], 1)

            pipeline(act, hidden, 0)
            if stop < 2:
                return
            stage_done(act, 1)
            copy(adjm[:, :, :], adj[:, :, :], "a_msk")

            def attention(t, u):
                if live(t):
                    if late(t):
                        act.wait_ge(s["a_t1"], t - 1)
                    act.activation(zs[:, u, :], y1[:, 0, bass.ds(t, 1), :].rearrange("p b n -> p (b n)"),
                                   ACT.Identity, scale=bsc[:, 2:3], bias=bsh[:, 2:3]).then_inc(s["a_z"], 1)
                b, v = t - 2, u
                if live(b):
                    act.wait_ge(s["a_nm"], b + 1)
                    for k in range(NT):
                        bank, c = ROWPACK[k]
                        sv = S[:, v, bank, c:c + (k + 1) * P]
                        act.activation(sv, sv, ACT.Exp, bias=nmx[:, v, k:k + 1], accum_out=es[:, v, k:k + 1])\
                           .then_inc(s["a_p"], 1)
                b, v = t - 1, 1 - u
                if live(b):
                    act.wait_ge(s["a_t2"], b + 1)
                    if late(b):
                        act.wait_ge(s["a_sc"], 4 * (b - 1))
                        act.wait_ge(s["a_v"], b - 1)
                    copy(x2T[:, v, :], ps[:, 6, :], "a_x2T")
                    act.wait_ge(s["a_q"], b + 1)
                    copy(qT[:, v, :], ps[:, 6, :], "a_qT")
                b, v = t - 2, u
                if live(b):
                    act.wait_ge(s["a_pt"], b + 1)
                    if late(b):
                        act.wait_ge(s["a_pv"], b - 1)
                    for k in range(3):
                        w = 256 if k == 2 else 512
                        copy(pT[:, v, k, 0:w], ps[:, 3 + k, 0:w], "a_pts")

            pipeline(act, attention, 2)
            if stop < 3:
                return
            stage_done(act, 2)
            for t in range(NT):
                act.wait_ge(s["t_tr"], t + 1)
                copy(Th[:, t, :], ps[:, t, :], "t_hi")
                copy(Tf[:, t, :], ps[:, t, :], "t_cp")
            act.wait_ge(s["t_bm"], 1)
            copy(Bm[:, :], ps[:, 4, :], "t_bmc")

            def gcn3(t, u):
                if live(t):
                    if late(t):
                        act.wait_ge(s["k_agg"], t - 1)
                    copy(x3h[:, u, :, :], xn[:, :, bass.ds(t, 1), :].rearrange("p t b d -> p t (b d)"), "k_hi")
                b, v = t - 2, u
                if live(b):
                    act.wait_ge(s["k_zt"], b + 1)
                    if late(b):
                        act.wait_ge(s["k_h2"], b - 1)
                    copy(zh[:, v, :], zt[:, v, :], "k_zh")
                b, v = t - 1, 1 - u
                if live(b):
                    act.wait_ge(s["k_agg"], b + 1)
                    if late(b):
                        act.wait_ge(s["k_w0"], b - 1)
                    copy(a3[:, v, :], ps[:, v, :], "k_cp")
                b, v = t - 2, u
                if live(b):
                    act.wait_ge(s["k_h2"], b + 1)
                    act.activation(H3h[:, bass.ds(b, 1), :].rearrange("p b n -> p (b n)"), ps[:, 6 + v, :],
                                   ACT.Relu).then_inc(s["k_h2h"], 1)
                b, v = t - 1, 1 - u
                if live(b):
                    act.wait_ge(s["k_add"], b + 1)
                    if late(b):
                        act.wait_ge(s["k_z"], b - 1)
                    act.activation(h1[:, v, :], h1p[:, v, :], ACT.Relu).then_inc(s["k_h1"], 1)

            pipeline(act, gcn3, 2)
            if stop < 4:
                return
            for j in range(2 * SKIPS):
                act.wait_ge(s["lw_tr"], j + 1)
                copy(LWh[:, j // 2, j % 2, :], ps[:, j, :], "lw_hi")
            act.wait_ge(s["lw_b"], 1)
            for p in range(SKIPS):
                cols_p = LB[p] * NW[p]
                def chunks_of_two(i):
                    for st in range(p + 1):
                        order = FIRST if st == 0 else ORDER
                        before = 0 if st == 0 else 3 + 4 * (st - 1)
                        for u in range(2):
                            act.wait_ge(lstm["h"][u], base_s[p] + i * (p + 1) + st)
                            for k, gt in enumerate(order):
                                act.wait_ge(lstm["mm"][u], base_g[p] + i * NG[p] + before + k + 1)
                                act.activation(ga[:, u, gt, 0:cols_p], ps[:, 4 * u + gt, 0:cols_p],
                                               ACT.Tanh if gt == 2 else ACT.Sigmoid,
                                               bias=lbias[:, p, gt:gt + 1]).then_inc(lstm["act"][u], 1)
                            act.wait_ge(lstm["c"][u], base_s[p] + i * (p + 1) + st + 1)
                            act.activation(tc[:, u, 0:cols_p], cc[:, u, 0:cols_p], ACT.Tanh)\
                               .then_inc(lstm["tc"][u], 1)

                rounds(act, PAIRS[p], chunks_of_two)

        @block.vector
        def _(dve):
            def sub(hi, lo, full, name):
                dve.tensor_tensor(lo, full, hi.bitcast(F32), ALU.subtract).then_inc(s[name], 1)

            def norm_stats(tiles, st, m, s_st, s_ag, n):
                dve.nop(nofuse=True)
                for k in range(4):
                    ins_ = dve.bn_stats(st[:, k, :], tiles[k])
                ins_.then_inc(s_st, 1)
                dve.wait_ge(s_st, n)
                dve.nop(nofuse=True)
                for k in range(4):
                    ins_ = dve.bn_aggr(m[:, k, :], st[:, k, :])
                ins_.then_inc(s_ag, 1)

            def normalise(dst, src, m, r, s_ap):
                for k in range(4):
                    ins_ = dve.tensor_scalar(dst[k], src[k], m[:, k, 0:1], r[:, k:k + 1], ALU.subtract, ALU.mult)
                ins_.then_inc(s_ap, 1)

            dve.wait_ge(s["ld_w"], 64)
            dve.tensor_scalar(d_col, d_col, 0.0, 1.0, ALU.max, ALU.min).then_inc(s["p_dve"], 1)
            dve.wait_ge(s["p_act"], 1)
            dve.wait_ge(s["p_dve"], 1)
            dve.tensor_scalar(wTd, wT, d_col, DT, ALU.mult, ALU.mult).then_inc(s["p_dve"], 1)
            dve.wait_ge(s["c_ident"], 1)
            dve.wait_ge(s["c_fzero"], 2)
            dve.tensor_scalar(F[0][:, 0, 0:P], ident[:, :], DT, None, ALU.mult).then_inc(s["p_dve"], 1)
            dve.tensor_scalar(F[1][:, 0, 0:P], ident[:, :], DT, None, ALU.mult).then_inc(s["p_dve"], 1)
            dve.wait_ge(s["m_sig"], 1)
            dve.tensor_scalar(cdt, sig, 0.5 * DT, None, ALU.mult).then_inc(s["m_row"], 1)
            dve.wait_ge(s["m_row"], 1)
            dve.tensor_scalar(dgm, cdt, -1.0, 1.0 - DT, ALU.mult, ALU.add).then_inc(s["m_row"], 1)
            for t in range(NT):
                dve.tensor_scalar(Mn[:, t, :], adj[:, t, :], cdt[:, t:t + 1], None, ALU.mult)\
                   .then_inc(s["m_row"], 1)
            dve.wait_ge(s["m_row"], 6)
            for t in range(NT):
                blk = Mn[:, t, t * P:(t + 1) * P]
                dve.scalar_tensor_tensor(blk, ident[:, :], dgm[:, t:t + 1], blk, ALU.mult, ALU.add)\
                   .then_inc(s["m_row"], 1)
            dve.wait_ge(s["p_dve"], 4)
            for k in range(STEPS):
                chunks = (k + 2 + 2) // 3
                dve.wait_ge(s["f_mm"], k + 1)
                if k:
                    dve.wait_ge(s["f_add"], k)
                old, new = F[k % 2], F[(k + 1) % 2]
                dve.tensor_tensor(
                    new[:, 1:1 + 3 * chunks, :].rearrange("p (c i) n -> p c (i n)", c=chunks),
                    ps[:, 2:2 + chunks, 0:3 * FW],
                    old[:, 0:3 * chunks, :].rearrange("p (c i) n -> p c (i n)", c=chunks), ALU.add)\
                    .then_inc(s["f_add"], 1)
            dve.wait_ge(s["f_add"], STEPS)
            dve.tensor_tensor(F[0][:, 1, 0:P], F[0][:, 1, 0:P], ident[:, :], ALU.add).then_inc(s["f_add"], 1)
            for t in range(NT):
                dve.wait_ge(s["m_hi"], t + 1)
                sub(Mh[:, t, :], Ml[:, t, :], ps[:, (5, 6, 7, 0)[t], :], "m_lo")
            for c in range(3):
                dve.wait_ge(s["e_hi"], c + 1)
                sub(Eh[:, c, :], El[:, c, :], ps[:, 2 + c, 0:3 * P], "e_lo")
            dve.wait_ge(s["e_b"], 3)
            dve.wait_ge(s["w_cp"], 7)

            def euler(g):
                def turn_lo(t):
                    dve.wait_ge(s["g_hi"], 4 * g + t + 1)
                    sub(xTh[:, t % 2, :], xTl[:, t % 2, :], ps[:, 6 + t % 2, :], "g_lo")

                turn_lo(0)
                for t in range(NT):
                    if t + 1 < NT:
                        turn_lo(t + 1)
                    for b in range(GB):
                        n = 4 * t + b
                        dve.wait_ge(s["g_mm"], 16 * g + n + 1)
                        dve.tensor_tensor(
                            G[:, :, t, b * D:(b + 1) * D].rearrange("p (c i) d -> p c i d", c=3),
                            ps[:, 3 * (n % 2):3 * (n % 2) + 3, 0:3 * P].rearrange("p c (i d) -> p c i d", i=3),
                            Eb[:, :, :].rearrange("p c (i d) -> p c i d", i=3), ALU.add).then_inc(s["g_ev"], 1)
                for t in range(NT):
                    dve.wait_ge(s["eu_hi"], 32 * g + t + 1)
                    sub(Hh[:, 0, t, :], Hl[:, 0, t, :], G[:, EI - 1, t, :], "eu_lo")
                for st in range(STEPS):
                    i = EI - 2 - st
                    last = st == STEPS - 1
                    dst = [xn[:, t, bass.ds(g * GB, GB), :].rearrange("p b d -> p (b d)") for t in range(NT)] \
                        if last else [tsum[:, t % 2, :] for t in range(NT)]

                    def total(t):
                        dve.wait_ge(s["eu_mm"], 32 * g + 4 * st + t + 1)
                        if t >= 2 and not last:
                            dve.wait_ge(s["eu_lo"], 32 * g + 4 * (st + 1) + t - 1)
                        dve.tensor_tensor(dst[t], ps[:, 4 * (st % 2) + t, :], G[:, i, t, :], ALU.add)\
                           .then_inc(s["eu_sum"], 1)

                    def low(t):
                        dve.wait_ge(s["eu_hi"], 32 * g + 4 * (st + 1) + t + 1)
                        sub(Hh[:, (st + 1) % 2, t, :], Hl[:, (st + 1) % 2, t, :], dst[t], "eu_lo")

                    def ln_a(t):
                        dve.wait_ge(s["eu_sum"], 32 * g + 4 * st + t + 1)
                        if t >= 2:
                            dve.wait_ge(s["ln_rs"], 4 * g + t - 1)
                        dve.wait_ge(s["ln_ap"], 4 * g + max(t - 1, 0))
                        norm_stats(rows4(dst[t]), stats[:, t % 2], mv[:, t % 2], s["ln_st"], s["ln_ag"],
                                   4 * g + t + 1)

                    def ln_b(t):
                        dve.wait_ge(s["ln_rs"], 4 * g + t + 1)
                        normalise(rows4(dst[t]), rows4(dst[t]), mv[:, t % 2], rstd[:, t % 2], s["ln_ap"])

                    if last:
                        total(0); ln_a(0); total(1); ln_a(1); ln_b(0); total(2); ln_a(2); ln_b(1)
                        total(3); ln_a(3); ln_b(2); ln_b(3)
                    else:
                        total(0); total(1); low(0); low(1); total(2); low(2); total(3); low(3)

            rounds(dve, GROUPS, euler)
            if stop < 1:
                return
            dve.wait_ge(s["ln_ap"], GROUPS * NT)
            dve.tensor_reduce(dg[:, 0, :], adj[:, :, :], AX.X, ALU.add).then_inc(s["d_row"], 1)
            for t in range(NT):
                if t:
                    dve.wait_ge(s["d_dg"], t)
                dve.tensor_tensor_reduce(dscr[:, :], adj[:, t, t * P:(t + 1) * P], ident[:, :], 1.0, 0.0,
                                         ALU.mult, ALU.add, dg[:, 1, t:t + 1]).then_inc(s["d_dg"], 1)
            dve.wait_ge(s["d_col"], 1)
            dve.wait_ge(s["d_row"], 1)
            dve.tensor_tensor(dg[:, 2, :], ps[:, 0, 0:4], dg[:, 0, :], ALU.add).then_inc(s["d_deg"], 1)
            dve.wait_ge(s["d_deg"], 1)
            dve.wait_ge(s["d_dg"], NT)
            dve.tensor_tensor(dg[:, 3, :], dg[:, 2, :], dg[:, 1, :], ALU.subtract).then_inc(s["d_deg"], 1)
            dve.wait_ge(s["d_deg"], 2)
            dve.tensor_scalar(dg[:, 4, :], dg[:, 3, :], 1.0, None, ALU.add).then_inc(s["d_deg"], 1)
            dve.wait_ge(s["d_inv"], 1)
            for t in range(NT):
                dve.tensor_scalar(A1[:, t, :], adj[:, t, :], dg[:, 5, t:t + 1], None, ALU.mult)\
                   .then_inc(s["d_a1"], 1)
            dve.wait_ge(s["d_a1"], NT)
            for t in range(NT):
                blk = A1[:, t, t * P:(t + 1) * P]
                dve.scalar_tensor_tensor(blk, ident[:, :], dg[:, 5, t:t + 1], blk, ALU.mult, ALU.add)\
                   .then_inc(s["d_a1"], 1)
            for t in range(NT):
                dve.wait_ge(s["d_hi"], t + 1)
                dve.scalar_tensor_tensor(Al[:, t, :], ps[:, t, :], dg[:, 5, t:t + 1], Ah[:, t, :].bitcast(F32),
                                         ALU.mult, ALU.subtract).then_inc(s["d_lo"], 1)

            def gcn(t, u):
                if live(t):
                    dve.wait_ge(s["n_hi"], t + 1)
                    sub(x1h[:, u, :, :], x1l[:, u, :, :],
                        xn[:, :, bass.ds(t, 1), :].rearrange("p t b d -> p t (b d)"), "n_lo")
                b = t - 2
                if live(b):
                    dve.wait_ge(s["n_y1"], 2 * (b + 1))
                    dve.nop(nofuse=True)
                    for h in range(HT):
                        dve.bn_stats(bst1[:, h, bass.ds(b, 1), :].rearrange("p b k -> p (b k)"),
                                     y1[:, h, bass.ds(b, 1), :].rearrange("p b n -> p (b n)"))\
                           .then_inc(s["n_st"], 1)

            def fold(a, z, gam, bet, n):
                dve.wait_ge(s["bn_rs"], n)
                dve.tensor_tensor(bsc[:, a:z], brs[:, a:z], gam, ALU.mult).then_inc(s["bn_sc"], 1)
                dve.wait_ge(s["bn_sc"], 2 * n - 1)
                dve.tensor_tensor(bms[:, a:z], bmv[:, a:z, 0], bsc[:, a:z], ALU.mult).then_inc(s["bn_ms"], 1)
                dve.wait_ge(s["bn_ms"], n)
                dve.tensor_tensor(bsh[:, a:z], bet, bms[:, a:z], ALU.subtract).then_inc(s["bn_sc"], 1)

            pipeline(dve, gcn, 2)
            dve.wait_ge(s["n_st"], 2 * B)
            for h in range(HT):
                dve.bn_aggr(bmv[:, h, :], bst1[:, h, :, :].rearrange("p b k -> p (b k)")).then_inc(s["bn_ag"], 1)
            fold(0, 2, g1c, be1c, 1)

            def outputs(t, u):
                dve.wait_ge(s["n_w2"], t + 1)
                y2 = y1[:, 0, bass.ds(t, 1), :].rearrange("p b n -> p (b n)")
                dve.tensor_scalar(y2, ps[:, u, :], b2c, None, ALU.add).then_inc(s["n_y2"], 1)
                dve.wait_ge(s["n_y2"], t + 1)
                dve.nop(nofuse=True)
                dve.bn_stats(bst2[:, bass.ds(t, 1), :].rearrange("p b k -> p (b k)"), y2).then_inc(s["n_st2"], 1)

            pipeline(dve, outputs, 0)
            dve.wait_ge(s["n_st2"], B)
            dve.bn_aggr(bmv[:, 2, :], bst2[:, :, :].rearrange("p b k -> p (b k)")).then_inc(s["bn_ag"], 1)
            fold(2, 3, g2c, be2c, 2)
            if stop < 2:
                return
            dve.wait_ge(s["bn_sc"], 4)
            dve.wait_ge(s["a_msk"], 1 + NT)

            def attention(t, u):
                b, v = t - 1, 1 - u
                if live(b):
                    for n, k in enumerate(ROWORDER):
                        bank, c = ROWPACK[k]
                        w = (k + 1) * P
                        dve.wait_ge(s["a_sc"], 4 * b + (n + 1 if n < 2 else 4))
                        if late(b) and n == 0:
                            dve.wait_ge(s["a_pt"], b - 1)
                        dve.nop(nofuse=True)
                        dve.tensor_tensor_reduce(S[:, v, bank, c:c + w], ps[:, bank, c:c + w], adjm[:, k, 0:w],
                                                 1.0, NEG, ALU.add, ALU.max, mx[:, v, k:k + 1])\
                           .then_inc(s["a_s"], 1)
                    dve.wait_ge(s["a_s"], 4 * (b + 1))
                    dve.tensor_scalar(nmx[:, v, :], mx[:, v, :], -1.0, None, ALU.mult).then_inc(s["a_nm"], 1)
                if live(t):
                    xv = xn[:, :, bass.ds(t, 1), :].rearrange("p t b d -> p t (b d)")
                    dve.wait_ge(s["a_t1"], t + 1)
                    if late(t):
                        dve.wait_ge(s["a_x2"], t - 1)
                    dve.tensor_tensor(yb[:, u, :, :], ps[:, 6, :].rearrange("p (t d) -> p t d", t=NT), xv, ALU.add)\
                       .then_inc(s["a_add"], 1)
                    dve.wait_ge(s["a_add"], t + 1)
                    norm_stats([yb[:, u, k, :] for k in range(4)], stats[:, u], mv[:, u], s["l_st1"], s["l_ag1"],
                               t + 1)
                b, v = t - 2, u
                if live(b):
                    dve.wait_ge(s["a_p"], 4 * (b + 1))
                    dve.reciprocal(rs[:, v, :], es[:, v, :]).then_inc(s["a_ri"], 1)
                    dve.wait_ge(s["a_ri"], b + 1)
                    dve.wait_ge(s["a_pv"], b + 1)
                    for k in range(4):
                        dve.scalar_tensor_tensor(
                            xn[:, k, bass.ds(b, 1), :].rearrange("p b d -> p (b d)"), ps[:, 7, k * P:(k + 1) * P],
                            rs[:, v, k:k + 1], x2s[:, v, k, :],
                            ALU.mult, ALU.add).then_inc(s["a_y"], 1)
                    dve.wait_ge(s["a_y"], 4 * (b + 1))
                    if late(b):
                        dve.wait_ge(s["a_x3"], b - 1)
                    norm_stats([xn[:, k, bass.ds(b, 1), :].rearrange("p b d -> p (b d)") for k in range(4)],
                               stats2[:, v], mv2[:, v], s["l_st2"], s["l_ag2"], b + 1)
                if live(t):
                    dve.wait_ge(s["l_rs1"], t + 1)
                    if late(t):
                        dve.wait_ge(s["a_t2"], t - 1)
                    normalise([x2s[:, u, k, :] for k in range(4)], [yb[:, u, k, :] for k in range(4)],
                              mv[:, u], rstd[:, u], s["a_x2"])
                    dve.wait_ge(s["a_x2"], t + 1)
                b, v = t - 2, u
                if live(b):
                    dve.wait_ge(s["l_rs2"], b + 1)
                    xb = [xn[:, k, bass.ds(b, 1), :].rearrange("p b d -> p (b d)") for k in range(4)]
                    normalise(xb, xb, mv2[:, v], rstd2[:, v], s["a_x3"])
                if live(t):
                    dve.wait_ge(s["a_v"], t + 1)
                    if late(t):
                        dve.wait_ge(s["a_pv"], t - 1)
                    dve.tensor_copy(vs[:, u, :, :], ps[:, 7, :].rearrange("p (t d) -> p t d", t=NT))\
                       .then_inc(s["a_vs"], 1)

            pipeline(dve, attention, 2)
            if stop < 3:
                return
            dve.wait_ge(s["a_x3"], B)
            for t in range(NT):
                dve.wait_ge(s["t_cp"], t + 1)
                sub(Th[:, t, :], Tl[:, t, :], ps[:, t, :], "t_lo")
            dve.wait_ge(s["t_bmc"], 1)
            dve.wait_ge(s["ld_l3"], 16 * (1 + NT))

            def gcn3(t, u):
                if live(t):
                    dve.wait_ge(s["k_hi"], t + 1)
                    sub(x3h[:, u, :, :], x3l[:, u, :, :],
                        xn[:, :, bass.ds(t, 1), :].rearrange("p t b d -> p t (b d)"), "k_lo")
                b, v = t - 2, u
                if live(b):
                    dve.wait_ge(s["k_z"], b + 1)
                    dve.tensor_tensor(zt[:, v, :], ps[:, 4 + v, :], bg1r[:, :, :].rearrange("p t d -> p (t d)"),
                                      ALU.add).then_inc(s["k_zt"], 1)
                    dve.wait_ge(s["k_zh"], b + 1)
                    sub(zh[:, v, :], zl[:, v, :], zt[:, v, :], "k_zl")
                    dve.wait_ge(s["k_h2h"], b + 1)
                    h3 = H3h[:, bass.ds(b, 1), :].rearrange("p b n -> p (b n)")
                    dve.scalar_tensor_tensor(H3l[:, bass.ds(b, 1), :].rearrange("p b n -> p (b n)"),
                                             ps[:, 6 + v, :], 0.0, h3.bitcast(F32), ALU.max, ALU.subtract)\
                       .then_inc(s["k_h2l"], 1)
                b, v = t - 1, 1 - u
                if live(b):
                    dve.wait_ge(s["k_w0"], b + 1)
                    if late(b):
                        dve.wait_ge(s["k_h1"], b - 1)
                    dve.tensor_tensor(h1p[:, v, :], ps[:, 2 + v, :], Bm[:, :], ALU.add).then_inc(s["k_add"], 1)

            pipeline(dve, gcn3, 2)
            if stop < 4:
                return
            dve.wait_ge(s["ld_lstm"], 16 * 4 * SKIPS)
            dve.tensor_tensor(lbias[:, :, :], lb[:, 0, :, :], lb[:, 1, :, :], ALU.add).then_inc(s["lw_b"], 1)
            for j in range(2 * SKIPS):
                dve.wait_ge(s["lw_hi"], j + 1)
                sub(LWh[:, j // 2, j % 2, :], LWl[:, j // 2, j % 2, :], ps[:, j, :], "lw_lo")
            for p in range(SKIPS):
                n = LB[p] * NW[p]
                def chunks_of_two(i):
                    for st in range(p + 1):
                        for u in range(2):
                            step = base_s[p] + i * (p + 1) + st
                            rec = base_r[p] + i * p + st - 1
                            acts = base_g[p] + i * NG[p] + (0 if st == 0 else 3 + 4 * (st - 1))
                            c, x1, t1, h = (v[:, u, 0:n] for v in (cc, ig, tc, hb))
                            g_i, g_f, g_g, g_o = (ga[:, u, k, 0:n] for k in range(4))
                            dve.wait_ge(lstm["act"][u], acts + 2)
                            if st == 0:
                                dve.tensor_tensor(c, g_i, g_g, ALU.mult).then_inc(lstm["c"][u], 1)
                            else:
                                dve.tensor_tensor(x1, g_i, g_g, ALU.mult).then_inc(lstm["ig"][u], 1)
                                dve.wait_ge(lstm["act"][u], acts + 3)
                                dve.tensor_tensor(c, g_f, c, ALU.mult).then_inc(lstm["fc"][u], 1)
                                dve.wait_ge(lstm["ig"][u], rec + 1)
                                dve.wait_ge(lstm["fc"][u], rec + 1)
                                dve.tensor_tensor(c, c, x1, ALU.add).then_inc(lstm["c"][u], 1)
                            dve.wait_ge(lstm["tc"][u], step + 1)
                            dve.tensor_tensor(h, g_o, t1, ALU.mult).then_inc(lstm["h"][u], 1)
                            if st < p:
                                dh, dl, hv = sth[:, u, 0:n], stl[:, u, 0:n], h
                            else:
                                dh, dl = (v[:, bass.ds((2 * i + u) * LB[p], LB[p]), p:p + (NW[p] - 1) * (p + 1) + 1:p + 1]
                                          for v in (H3h, H3l))
                                hv = h.rearrange("p (b w) -> p b w", b=LB[p])
                            dve.wait_ge(lstm["h"][u], step + 1)
                            dve.tensor_copy(dh, hv).then_inc(lstm["hi"][u], 1)
                            dve.wait_ge(lstm["hi"][u], step + 1)
                            dve.tensor_tensor(dl, hv, dh.bitcast(F32), ALU.subtract).then_inc(lstm["lo"][u], 1)

                rounds(dve, PAIRS[p], chunks_of_two)
            if stop < 5:
                return
            stage_done(dve, 4)

            def last(t, u):
                if live(t):
                    dve.wait_ge(s["z_tr"], t + 1)
                    if late(t):
                        dve.wait_ge(s["st_out"], 16 * (t - 1))
                    dve.tensor_tensor(fy[:, u, :, :], ps[:, u, :].rearrange("p (t d) -> p t d", t=NT),
                                      xn[:, :, bass.ds(t, 1), :].rearrange("p t b d -> p t (b d)"), ALU.add)\
                       .then_inc(s["z_y"], 1)
                    dve.wait_ge(s["z_y"], t + 1)
                    if late(t):
                        dve.wait_ge(s["z_ap"], t - 1)
                    norm_stats([fy[:, u, k, :] for k in range(4)], stats[:, u], mv[:, u], s["z_st"], s["z_ag"], t + 1)
                b, v = t - 1, 1 - u
                if live(b):
                    dve.wait_ge(s["z_rs"], b + 1)
                    tiles = [fy[:, v, k, :] for k in range(4)]
                    normalise(tiles, tiles, mv[:, v], rstd[:, v], s["z_ap"])

            pipeline(dve, last, 1)

        @block.tensor
        def _(pe):
            def turn(dst, src):
                return pe.transpose(dst, src, ident[:, :])

            def split(dst, pairs, name=None):
                for k, (lh, ll, rh, rl) in enumerate(pairs):
                    pe.matmul(dst, lh, rh, start=(k == 0), stop=False)
                    pe.matmul(dst, lh, rl, start=False, stop=False)
                    mm = pe.matmul(dst, ll, rh, start=False, stop=(k == len(pairs) - 1))
                return mm

            pe.wait_ge(s["c_ident"], 1)
            pe.wait_ge(s["ld_w"], 64)
            turn(ps[:, 0, 0:P], w_raw).then_inc(s["p_pe"], 1)
            pe.wait_ge(s["p_dve"], 2)
            pe.matmul(ps[:, 1, 0:P], wTd, wT, start=True, stop=True).then_inc(s["p_pe"], 1)
            pe.wait_ge(s["p_act"], 2)
            pe.wait_ge(s["p_dve"], 4)
            for k in range(STEPS):
                chunks = (k + 2 + 2) // 3
                pe.wait_ge(s["f_add"], k)
                for c in range(chunks):
                    mm = pe.matmul(ps[:, 2 + c, 0:3 * FW], W,
                                   F[k % 2][:, 1 + 3 * c:4 + 3 * c, :].rearrange("p i n -> p (i n)"),
                                   start=True, stop=True)
                mm.then_inc(s["f_mm"], 1)
            pe.wait_ge(s["m_row"], 10)
            for m in range(NT):
                for t in range(NT):
                    mm = turn(ps[:, (5, 6, 7, 0)[m], t * P:(t + 1) * P], Mn[:, t, m * P:(m + 1) * P])
                mm.then_inc(s["m_tr"], 1)
            pe.wait_ge(s["ld_late"], 16 * 12)
            for t in range(HT):
                turn(ps[:, 1, t * P:(t + 1) * P], w1_raw[:, t, :])
            for t in range(HT):
                mm = turn(ps[:, 1, HID + t * P:HID + (t + 1) * P], w2_raw[:, t * P:(t + 1) * P])
            mm.then_inc(s["w_tr"], 1)
            pe.wait_ge(s["m_lo"], NT)
            for k in range(3):
                mm = turn(ps[:, 5, k * P:(k + 1) * P], wqkv_raw[:, k * P:(k + 1) * P])
            mm.then_inc(s["w_tr"], 1)
            pe.wait_ge(s["w_cp"], 5)
            pe.matmul(ps[:, 6, 0:P], wqT, wkT, start=True, stop=True)
            pe.matmul(ps[:, 6, P:2 * P], wvT, wo_raw, start=True, stop=True).then_inc(s["w_mm"], 1)
            pe.wait_ge(s["f_add"], STEPS + 1)
            for k in range(EI):
                mm = turn(ps[:, 2 + k // 3, (k % 3) * P:(k % 3 + 1) * P], F[0][:, 1 + k, 0:P])
            mm.then_inc(s["e_mm"], 1)
            for k in range(EI):
                mm = pe.matmul(ps[:, (7, 0, 1)[k // 3], (k % 3) * P:(k % 3 + 1) * P],
                               F[0][:, 1 + k, P:FW].to_broadcast([P, P]), ident[:, :], start=True, stop=True)
            mm.then_inc(s["e_mm"], 1)
            pe.wait_ge(s["e_lo"], 3)
            pe.wait_ge(s["e_b"], 3)

            def euler(g):
                def turn_x(t):
                    if t >= 2:
                        pe.wait_ge(s["g_lo"], 4 * g + t - 1)
                    for b in range(GB):
                        mm = turn(ps[:, 6 + t % 2, b * P:(b + 1) * P], xs[:, t, b, :])
                    mm.then_inc(s["g_tr"], 1)

                pe.wait_ge(s["ld_xs"], 16 * NT * (g + 1))
                pe.wait_ge(s["eu_sum"], 32 * g)
                turn_x(0)
                turn_x(1)
                for t in range(NT):
                    pe.wait_ge(s["g_lo"], 4 * g + t + 1)
                    for b in range(GB):
                        n = 4 * t + b
                        if n >= 2:
                            pe.wait_ge(s["g_ev"], 16 * g + n - 1)
                        xh, xl = (v[:, t % 2, b * P:(b + 1) * P] for v in (xTh, xTl))
                        dst = [ps[:, 3 * (n % 2) + c, 0:3 * P] for c in range(3)]
                        for c in range(3):
                            pe.matmul(dst[c], xh, Eh[:, c, :], start=True, stop=False)
                            pe.matmul(dst[c], xh, El[:, c, :], start=False, stop=False)
                        for c in range(3):
                            mm = pe.matmul(dst[c], xl, Eh[:, c, :], start=False, stop=True)
                        mm.then_inc(s["g_mm"], 1)
                    if t + 2 < NT:
                        turn_x(t + 2)
                for st in range(STEPS):
                    u = st % 2
                    done = 32 * g + 4 * st

                    def part(t, ks):
                        dst = ps[:, 4 * u + t, :]
                        for k in ks:
                            pe.wait_ge(s["eu_lo"], done + k + 1)
                            mh, ml = (v[:, k, t * P:(t + 1) * P] for v in (Mh, Ml))
                            pe.matmul(dst, mh, Hh[:, u, k, :], start=(k == 0), stop=False)
                            pe.matmul(dst, mh, Hl[:, u, k, :], start=False, stop=False)
                            mm = pe.matmul(dst, ml, Hh[:, u, k, :], start=False, stop=(k == NT - 1))
                        return mm

                    part(0, range(3))
                    part(1, range(3))
                    for t in range(2):
                        part(t, [3]).then_inc(s["eu_mm"], 1)
                    for t in range(2, NT):
                        part(t, range(NT)).then_inc(s["eu_mm"], 1)

            rounds(pe, GROUPS, euler)
            if stop < 1:
                return
            pe.wait_ge(s["c_ones"], 1)
            stage_done(pe, 0)
            for m in range(NT):
                for t in range(NT):
                    mm = pe.matmul(ps[:, 0, m:m + 1], adj[:, t, m * P:(m + 1) * P], ones[:, :],
                                   start=(t == 0), stop=(t == NT - 1))
            mm.then_inc(s["d_col"], 1)
            pe.wait_ge(s["d_a1"], 2 * NT)
            for m in range(NT):
                for t in range(NT):
                    mm = turn(ps[:, m, t * P:(t + 1) * P], A1[:, t, m * P:(m + 1) * P])
                mm.then_inc(s["d_tr"], 1)
            pe.wait_ge(s["d_lo"], NT)

            def gcn(t, u):
                if live(t):
                    pe.wait_ge(s["n_lo"], t + 1)
                    if late(t):
                        pe.wait_ge(s["n_cp"], t - 1)
                    split(ps[:, u, :], [(x1h[:, u, k, :], x1l[:, u, k, :], Ah[:, k, :], Al[:, k, :])
                                        for k in range(NT)]).then_inc(s["n_agg"], 1)
                b, v = t - 1, 1 - u
                if live(b):
                    pe.wait_ge(s["n_cp"], b + 1)
                    if late(b):
                        pe.wait_ge(s["n_y1"], 2 * (b - 1))
                    for h in range(HT):
                        mm = pe.matmul(ps[:, 2 + 2 * v + h, :], w1t[:, h * P:(h + 1) * P], agg[:, v, :],
                                       start=True, stop=True)
                    mm.then_inc(s["n_w1"], 1)

            pipeline(pe, gcn, 1)

            def outputs(t, u):
                pe.wait_ge(s["n_r"], 2 * (t + 1))
                if late(t):
                    pe.wait_ge(s["n_y2"], t - 1)
                for h in range(HT):
                    mm = pe.matmul(ps[:, u, :], w2t[:, h, :], r1[:, u, h, :], start=(h == 0), stop=(h == HT - 1))
                mm.then_inc(s["n_w2"], 1)

            pipeline(pe, outputs, 0)
            if stop < 2:
                return
            stage_done(pe, 1)

            def attention(t, u):
                b, v = t - 1, 1 - u
                if live(b):
                    pe.wait_ge(s["a_qT"], b + 1)
                    pe.wait_ge(s["a_s"], 4 * b)
                    for k in ROWORDER:
                        bank, c = ROWPACK[k]
                        w = (k + 1) * P
                        pe.matmul(ps[:, bank, c:c + w], qT[:, v, k * P:(k + 1) * P], x2T[:, v, 0:w],
                                  start=True, stop=True).then_inc(s["a_sc"], 1)
                if live(t):
                    pe.wait_ge(s["a_z"], t + 1)
                    pe.wait_ge(s["a_qT"], t)
                    for k in range(NT):
                        mm = turn(ps[:, 6, k * P:(k + 1) * P], zs[:, u, k * P:(k + 1) * P])
                    mm.then_inc(s["a_t1"], 1)
                b, v = t - 2, u
                if live(b):
                    pe.wait_ge(s["a_pts"], 3 * (b + 1))
                    pe.wait_ge(s["a_vs"], b + 2 if live(b + 1) else b + 1)
                    pe.wait_ge(s["a_y"], 4 * b)
                    for k in range(NT):
                        for j in range(k + 1):
                            bank, c = COLPACK[j]
                            c += (k - j) * P
                            mm = pe.matmul(ps[:, 7, k * P:(k + 1) * P], pT[:, v, bank, c:c + P], vs[:, v, j, :],
                                           start=(j == 0), stop=(j == k))
                    mm.then_inc(s["a_pv"], 1)
                if live(t):
                    pe.wait_ge(s["a_x2"], t + 1)
                    for k in range(NT):
                        mm = turn(ps[:, 6, k * P:(k + 1) * P], x2s[:, u, k, :])
                    mm.then_inc(s["a_t2"], 1)
                    pe.wait_ge(s["a_x2T"], t + 1)
                    pe.matmul(ps[:, 6, :], wqk[:, :], x2T[:, u, :], start=True, stop=True).then_inc(s["a_q"], 1)
                    if late(t):
                        pe.wait_ge(s["a_y"], 4 * (t - 1))
                    for k in range(NT):
                        mm = pe.matmul(ps[:, 7, k * P:(k + 1) * P], x2T[:, u, k * P:(k + 1) * P], wvo[:, :],
                                       start=True, stop=True)
                    mm.then_inc(s["a_v"], 1)
                b, v = t - 1, 1 - u
                if live(b):
                    pe.wait_ge(s["a_p"], 4 * (b + 1))
                    pe.wait_ge(s["a_pts"], 3 * b)
                    for j in range(NT):
                        ob, oc = COLPACK[j]
                        for k in range(j, NT):
                            ib, ic = ROWPACK[k]
                            mm = turn(ps[:, 3 + ob, oc + (k - j) * P:oc + (k - j + 1) * P],
                                      S[:, v, ib, ic + j * P:ic + (j + 1) * P])
                    mm.then_inc(s["a_pt"], 1)

            pipeline(pe, attention, 2)
            if stop < 3:
                return
            stage_done(pe, 2)
            for m in range(NT):
                for t in range(NT):
                    mm = turn(ps[:, m, t * P:(t + 1) * P], adj[:, t, m * P:(m + 1) * P])
                mm.then_inc(s["t_tr"], 1)
            pe.wait_ge(s["ld_l3"], 16 * (1 + NT))
            pe.wait_ge(s["t_cp"], NT)
            for m in range(NT):
                mm = pe.matmul(ps[:, 4, :], bg0r[:, :], Tf[:, m, :], start=(m == 0), stop=(m == NT - 1))
            mm.then_inc(s["t_bm"], 1)
            pe.wait_ge(s["t_lo"], NT)
            pe.wait_ge(s["t_bmc"], 1)

            def gcn3(t, u):
                b, v = t - 1, 1 - u
                if live(b):
                    pe.wait_ge(s["k_h1"], b + 1)
                    if late(b):
                        pe.wait_ge(s["k_zt"], b - 1)
                    for k in range(NT):
                        mm = pe.matmul(ps[:, 4 + v, k * P:(k + 1) * P], h1[:, v, k * P:(k + 1) * P], wg1[:, :],
                                       start=True, stop=True)
                    mm.then_inc(s["k_z"], 1)
                if live(t):
                    pe.wait_ge(s["k_lo"], t + 1)
                    if late(t):
                        pe.wait_ge(s["k_cp"], t - 1)
                    split(ps[:, u, :], [(x3h[:, u, k, :], x3l[:, u, k, :], Th[:, k, :], Tl[:, k, :])
                                        for k in range(NT)]).then_inc(s["k_agg"], 1)
                if live(b):
                    pe.wait_ge(s["k_zl"], b + 1)
                    if late(b):
                        pe.wait_ge(s["k_h2l"], b - 1)
                    split(ps[:, 6 + v, :], [(zh[:, v, k * P:(k + 1) * P], zl[:, v, k * P:(k + 1) * P],
                                             Th[:, k, :], Tl[:, k, :]) for k in range(NT)]).then_inc(s["k_h2"], 1)
                if live(t):
                    pe.wait_ge(s["k_cp"], t + 1)
                    if late(t):
                        pe.wait_ge(s["k_add"], t - 1)
                    pe.matmul(ps[:, 2 + u, :], wg0[:, :], a3[:, u, :], start=True, stop=True)\
                      .then_inc(s["k_w0"], 1)

            pipeline(pe, gcn3, 1)
            if stop < 4:
                return
            stage_done(pe, 3)
            pe.wait_ge(s["ld_lstm"], 16 * 4 * SKIPS)
            for j in range(2 * SKIPS):
                for k in range(GATES):
                    mm = turn(ps[:, j, k * P:(k + 1) * P], (wih, whh)[j % 2][:, j // 2, k, :])
                mm.then_inc(s["lw_tr"], 1)
            pe.wait_ge(s["lw_lo"], 2 * SKIPS)
            for p in range(SKIPS):
                n = LB[p] * NW[p]
                for u in range(2):
                    pe.wait_ge(lstm["lo"][u], base_s[p])
                def chunks_of_two(i):
                    for st in range(p + 1):
                        for u in range(2):
                            xh, xl = (v[:, bass.ds((2 * i + u) * LB[p], LB[p]),
                                        st:st + (NW[p] - 1) * (p + 1) + 1:p + 1] for v in (H3h, H3l))
                            before = 0 if st == 0 else 3 + 4 * (st - 1)
                            pe.wait_ge(lstm["act"][u], base_g[p] + i * NG[p] + before)
                            pe.wait_ge(lstm["lo"][u], base_s[p] + i * (p + 1) + st)
                            for gt in (FIRST if st == 0 else ORDER):
                                w = [(LWh[:, p, q, gt * P:(gt + 1) * P], LWl[:, p, q, gt * P:(gt + 1) * P])
                                     for q in range(2)]
                                dst = ps[:, 4 * u + gt, 0:n]
                                dst3 = dst.rearrange("p (b w) -> p b w", b=LB[p])
                                pe.matmul(dst3, w[0][0], xh, start=True, stop=False)
                                pe.matmul(dst3, w[0][0], xl, start=False, stop=False)
                                mm = pe.matmul(dst3, w[0][1], xh, start=False, stop=(st == 0))
                                if st:
                                    pe.matmul(dst, w[1][0], sth[:, u, 0:n], start=False, stop=False)
                                    pe.matmul(dst, w[1][0], stl[:, u, 0:n], start=False, stop=False)
                                    mm = pe.matmul(dst, w[1][1], sth[:, u, 0:n], start=False, stop=True)
                                mm.then_inc(lstm["mm"][u], 1)

                rounds(pe, PAIRS[p], chunks_of_two)
            if stop < 5:
                return
            def last(t, u):
                pe.wait_ge(s["z_hs"], t + 1)
                if late(t):
                    pe.wait_ge(s["z_y"], t - 1)
                for k in range(NT):
                    mm = turn(ps[:, u, k * P:(k + 1) * P], hs[:, u, k * P:(k + 1) * P])
                mm.then_inc(s["z_tr"], 1)

            stage_done(pe, 4)
            pipeline(pe, last, 0)


_INS = ["x", "adj", "L0_gnn_alpha_train", "L0_gnn_w", "L0_gnn_d", "L0_gnn_fc_in_w", "L0_gnn_fc_in_b",
        "L1_gnn_W1", "L1_gnn_b1", "L1_gnn_g1", "L1_gnn_be1", "L1_gnn_W2", "L1_gnn_b2", "L1_gnn_g2",
        "L1_gnn_be2", "L2_gnn_Wqkv", "L2_gnn_Wo", "L3_gnn_Wg0", "L3_gnn_bg0", "L3_gnn_Wg1", "L3_gnn_bg1",
        "L3_gnn_Wih", "L3_gnn_Whh", "L3_gnn_bih", "L3_gnn_bhh"]


def kernel(**inputs):
    import numpy as _np
    import concourse.bacc as _bacc
    from concourse.bass_utils import run_bass_kernel_spmd as _run

    nc = _bacc.Bacc("TRN2", target_bir_lowering=False, num_devices=1)
    arrays, args = {}, {}
    for name in _INS:
        a = _np.ascontiguousarray(inputs[name])
        arrays[f"in_{name}"] = a
        args[name] = nc.dram_tensor(f"in_{name}", a.shape, mybir.dt.from_np(a.dtype), kind="ExternalInput").ap()
    out = nc.dram_tensor("out_0", (B, N, D), F32, kind="ExternalOutput").ap()
    build(nc, args, out)
    r = _run(nc, [arrays], core_ids=[0])
    return r.results[0]["out_0"]
```

```python
from contextlib import ExitStack

import concourse.bass as bass
from concourse import mybir

F32 = mybir.dt.float32
F32R = mybir.dt.float32r
ACT = mybir.ActivationFunctionType
ALU = mybir.AluOpType
AX = mybir.AxisListType

P = 128
B, N, D = 16, 512, 128
NT = N // P
GB = 4
GROUPS = B // GB
STEPS = 8
DT = 1.0 / STEPS
EI = STEPS + 1
HID = 256
HT = HID // P
SKIPS = 4
GATES = 4
EPS = 1e-5
NEG = -1e30

ROWPACK = {3: (0, 0), 2: (1, 0), 0: (1, 384), 1: (2, 0)}
ROWORDER = (3, 1, 2, 0)
COLPACK = {0: (0, 0), 1: (1, 0), 3: (1, 384), 2: (2, 0)}


def live(b):
    return not isinstance(b, int) or 0 <= b < B


def late(b, n=2):
    return not isinstance(b, int) or b >= n




def pipeline(eng, step, depth):
    head = 2 * ((depth + 3) // 2)
    for t in range(head):
        step(t, t % 2)
    with eng.Fori(head // 2, B // 2) as i:
        step(2 * i, 0)
        step(2 * i + 1, 1)
    for t in range(B, B + depth):
        step(t, t % 2)


def rounds(eng, count, body):
    body(0)
    with eng.Fori(1, count) as i:
        body(i)


def build(nc, ins, out, stop=99, dump=None):
    ctx = ExitStack()
    with ctx:
        def sem(name):
            return ctx.enter_context(nc.semaphore(name))

        def sb(name, shape, dt=F32, where=None):
            return (where or ctx).enter_context(nc.sbuf_tensor(name, shape, dt))

        ps = ctx.enter_context(nc.psum_tensor("banks", [P, 8, 512], F32))

        xn = sb("xn", [P, NT, B, D])
        adj = sb("adj_sb", [P, NT, N])
        ident = sb("ident", [P, P])
        ones = sb("ones", [P, 1])
        mhalf = sb("mhalf", [P, 16])
        w1t = sb("w1t", [P, HID])
        w2t = sb("w2t", [P, HT, P])
        wqk = sb("wqk", [P, P])
        wvo = sb("wvo", [P, P])
        wg0 = sb("wg0", [P, P])
        wg1 = sb("wg1", [P, P])
        cols = sb("cols", [P, 16])
        b1c, g1c, be1c = cols[:, 0:2], cols[:, 2:4], cols[:, 4:6]
        b2c, g2c, be2c = cols[:, 6:7], cols[:, 7:8], cols[:, 8:9]
        stats = sb("stats", [P, 2, 4, 6])
        mv = sb("mv", [P, 2, 4, 2])
        ve = sb("ve", [P, 2, 4])
        rstd = sb("rstd", [P, 2, 4])
        stats2 = sb("stats2", [P, 2, 4, 6])
        mv2 = sb("mv2", [P, 2, 4, 2])
        ve2 = sb("ve2", [P, 2, 4])
        rstd2 = sb("rstd2", [P, 2, 4])
        nmr = sb("nmr", [P, 2, 4])
        bsc = sb("bsc", [P, 3])
        bsh = sb("bsh", [P, 3])

        s0 = ExitStack()
        Mh = sb("Mh", [P, NT, N], F32R, s0)
        Ml = sb("Ml", [P, NT, N], F32R, s0)
        G = sb("G", [P, EI, NT, GB * D], F32, s0)
        Hh = sb("euh", [P, 2, NT, GB * D], F32R, s0)
        Hl = sb("eul", [P, 2, NT, GB * D], F32R, s0)
        tsum = sb("tsum", [P, 2, GB * D], F32, s0)
        Eh = sb("Eh", [P, 3, 3 * P], F32R, s0)
        El = sb("El", [P, 3, 3 * P], F32R, s0)
        Eb = sb("Eb", [P, 3, 3 * P], F32, s0)
        xs = sb("xs", [P, NT, GB, D], F32, s0)
        xTh = sb("xTh", [P, 2, GB * P], F32R, s0)
        xTl = sb("xTl", [P, 2, GB * P], F32R, s0)
        FW = P + 1
        gflat = G[:, :, :, :].rearrange("p i t n -> p (i t n)")
        F = [gflat[:, u * 10 * FW:(u + 1) * 10 * FW].rearrange("p (i n) -> p i n", n=FW) for u in range(2)]
        at = 20 * FW

        def carve(n):
            nonlocal at
            at += n
            return gflat[:, at - n:at]

        w_raw, wT, wTd, W = carve(P), carve(P), carve(P), carve(P)
        d_col, alpha_c, sig, cdt, dgm = carve(1), carve(4), carve(4), carve(4), carve(4)
        Mn = carve(NT * N).rearrange("p (t n) -> p t n", t=NT)
        w1_raw = carve(HT * P).rearrange("p (t n) -> p t n", t=HT)
        w2_raw, wqkv_raw, wo_raw = carve(HID), carve(3 * P), carve(P)
        wqT, wkT, wvT = carve(P), carve(P), carve(P)
        s0.close()

        s1 = ExitStack()
        y1 = sb("y1", [P, HT, B, N], F32, s1)
        s1b = ExitStack()
        Ah = sb("Ah", [P, NT, N], F32R, s1b)
        Al = sb("Al", [P, NT, N], F32R, s1b)
        A1 = sb("A1", [P, NT, N], F32, s1b)
        x1h = sb("x1h", [P, 2, NT, D], F32R, s1b)
        x1l = sb("x1l", [P, 2, NT, D], F32R, s1b)
        agg = sb("agg", [P, 2, N], F32, s1b)
        r1 = sb("r1", [P, 2, HT, N], F32, s1b)
        dg = sb("deg", [P, 6, 4], F32, s1b)
        dscr = sb("dscr", [P, P], F32, s1b)
        bst1 = sb("bst1", [P, HT, B, 6], F32, s1b)
        bst2 = sb("bst2", [P, B, 6], F32, s1b)
        bmv = sb("bmv", [P, 3, 2], F32, s1b)
        bve = sb("bve", [P, 3], F32, s1b)
        brs = sb("brs", [P, 3], F32, s1b)
        bms = sb("bms", [P, 3], F32, s1b)
        s1b.close()
        s1.close()

        s3 = ExitStack()
        H3h = sb("H3h", [P, B, N], F32R, s3)
        H3l = sb("H3l", [P, B, N], F32R, s3)
        s3a = ExitStack()
        wih = sb("wih_sb", [P, SKIPS, GATES, P], F32, s3)
        whh = sb("whh_sb", [P, SKIPS, GATES, P], F32, s3)
        lb = sb("lb", [P, 2, SKIPS, GATES], F32, s3)
        Th = sb("Th", [P, NT, N], F32R, s3a)
        Tl = sb("Tl", [P, NT, N], F32R, s3a)
        Tf = sb("Tf", [P, NT, N], F32, s3a)
        Bm = sb("Bm", [P, N], F32, s3a)
        bg0r = sb("bg0r", [P, P], F32, s3a)
        bg1r = sb("bg1r", [P, NT, P], F32, s3a)
        zs = sb("zs", [P, N], F32, s3a)
        x2s = sb("x2s", [P, NT, D], F32, s3a)
        x2T = sb("x2T", [P, N], F32, s3a)
        qT = sb("qT", [P, N], F32, s3a)
        vs = sb("vs", [P, 2, NT, D], F32, s3a)
        S = sb("S", [P, 3, 512], F32, s3a)
        pT = sb("pT", [P, 3, 512], F32, s3a)
        nmx = sb("nmx", [P, 2, 4], F32, s3a)
        es = sb("es", [P, 2, 4], F32, s3a)
        rs = sb("rs", [P, 2, 4], F32, s3a)
        yb = sb("yb", [P, NT, D], F32, s3a)
        x3h = sb("x3h", [P, 2, NT, D], F32R, s3a)
        x3l = sb("x3l", [P, 2, NT, D], F32R, s3a)
        a3 = sb("a3", [P, N], F32, s3a)
        h1 = sb("h1", [P, N], F32, s3a)
        zt = sb("zt", [P, N], F32, s3a)
        zh = sb("zh", [P, N], F32R, s3a)
        zl = sb("zl", [P, N], F32R, s3a)
        s3a.close()

        LWh = sb("LWh", [P, SKIPS, 2, GATES * P], F32R, s3)
        LWl = sb("LWl", [P, SKIPS, 2, GATES * P], F32R, s3)
        lbias = sb("lbias", [P, SKIPS, GATES], F32, s3)
        ga = sb("ga", [P, 2, GATES, 512], F32, s3)
        cc = sb("cc", [P, 2, 512], F32, s3)
        ig = sb("ig", [P, 2, 512], F32, s3)
        tc = sb("tc", [P, 2, 512], F32, s3)
        hb = sb("hb", [P, 2, 512], F32, s3)
        sth = sb("sth", [P, 2, 512], F32R, s3)
        stl = sb("stl", [P, 2, 512], F32R, s3)
        hs = sb("hs", [P, 2, N], F32, s3)
        s3.close()

        S_NAMES = """ld_adj ld_w ld_late ld_xs ld_l3 ld_lstm
            c_zero c_ident c_ones c_half c_rows c_fzero
            p_pe p_act p_dve f_mm f_add e_mm e_hi e_lo e_b m_sig m_row m_tr m_hi m_lo w_tr w_cp w_mm w_end
            g_tr g_hi g_lo g_mm g_ev eu_mm eu_sum eu_hi eu_lo
            ln_st ln_ag ln_ve ln_rs ln_ap
            d_row d_col d_dg d_deg d_inv d_a1 d_tr d_hi d_lo
            n_hi n_lo n_agg n_cp n_w1 n_y1 n_st n_r n_w2 n_y2 n_st2 bn_ag bn_ve bn_rs bn_ms bn_sc
            a_msk a_z a_t1 a_add a_x2 a_t2 a_x2T a_q a_v a_qT a_vs a_sc a_s a_p a_pt a_pts a_pv a_ri a_y a_x2c
            l_st1 l_ag1 l_ve1 l_rs1 l_st2 l_ag2 l_ve2 l_rs2 a_x3
            t_tr t_hi t_lo t_cp t_bm t_bmc k_hi k_lo k_agg k_cp k_w0 k_add k_h1 k_z k_zt k_zh k_zl k_h2 k_h2h k_h2l
            lw_tr lw_hi lw_lo lw_b
            z_hs z_tr z_y z_st z_ag z_ve z_rs z_nb z_ap st_out""".split()
        s = {n: sem(n) for n in S_NAMES}
        lstm = {n: [sem(f"lstm_{n}{u}") for u in range(2)]
                for n in ("mm", "act", "ig", "fc", "c", "tc", "h", "hi", "lo")}

        def rows4(v):
            return [v[:, k * P:(k + 1) * P] for k in range(4)]

        def batch(v, b):
            return v[:, :, bass.ds(b, 1), :].rearrange("p t b d -> p t (b d)")

        def feat(v, b):
            return v[:, bass.ds(b, 1), :].rearrange("p b n -> p (b n)")

        def stage_done(eng, n):
            if n == 0:
                eng.wait_ge(s["ln_ap"], GROUPS * NT)
            elif n == 1:
                eng.wait_ge(s["bn_sc"], 4)
            elif n == 3:
                eng.wait_ge(s["k_h2l"], B)
            elif n == 4:
                for u in range(2):
                    eng.wait_ge(lstm["lo"][u], LSTM_STEPS)

        LB = [1, 2, 2, 4]
        PAIRS = [B // (2 * n) for n in LB]
        NG = [3 + 4 * p for p in range(SKIPS)]
        base_g = [sum(PAIRS[q] * NG[q] for q in range(p)) for p in range(SKIPS + 1)]
        base_s = [sum(PAIRS[q] * (q + 1) for q in range(p)) for p in range(SKIPS + 1)]
        base_r = [sum(PAIRS[q] * q for q in range(p)) for p in range(SKIPS + 1)]
        LSTM_STEPS = base_s[SKIPS]
        NW = [N // (p + 1) for p in range(SKIPS)]
        ORDER = [0, 2, 1, 3]
        FIRST = [0, 2, 3]

        x_v = ins["x"].rearrange("b (t p) d -> p t b d", p=P)
        out_v = out.rearrange("b (t p) d -> p t b d", p=P)

        block = ctx.enter_context(nc.Block())

        @block.sync
        def _(sp):
            def column(dst, src, name):
                sp.dma_start(dst, src.rearrange("(t p) -> p t", p=P), allow_slow_non_contiguous=True).then_inc(s[name], 16)

            sp.dma_start(w_raw, ins["L0_gnn_w"]).then_inc(s["ld_w"], 16)
            column(d_col, ins["L0_gnn_d"], "ld_w")
            sp.wait_ge(s["c_fzero"], 2)
            sp.dma_start(F[0][:, 1, 0:P], ins["L0_gnn_fc_in_w"]).then_inc(s["ld_w"], 16)
            column(F[0][:, 1, P:FW], ins["L0_gnn_fc_in_b"], "ld_w")
            sp.dma_start(adj[:, :, :], ins["adj"].rearrange("(t p) m -> p t m", p=P)).then_inc(s["ld_adj"], 16)
            column(alpha_c, ins["L0_gnn_alpha_train"], "ld_adj")

            def load_group(g):
                for t in range(NT):
                    sp.dma_start(xs[:, t, :, :], x_v[:, t, bass.ds(g * GB, GB), :]).then_inc(s["ld_xs"], 16)

            load_group(0)
            sp.dma_start(w1_raw, ins["L1_gnn_W1"].rearrange("(t p) d -> p t d", p=P)).then_inc(s["ld_late"], 16)
            sp.dma_start(w2_raw, ins["L1_gnn_W2"]).then_inc(s["ld_late"], 16)
            sp.dma_start(wqkv_raw, ins["L2_gnn_Wqkv"]).then_inc(s["ld_late"], 16)
            sp.dma_start(wo_raw, ins["L2_gnn_Wo"]).then_inc(s["ld_late"], 16)
            sp.dma_start(wg0[:, :], ins["L3_gnn_Wg0"]).then_inc(s["ld_late"], 16)
            sp.dma_start(wg1[:, :], ins["L3_gnn_Wg1"]).then_inc(s["ld_late"], 16)
            for dst, name in ((b1c, "b1"), (g1c, "g1"), (be1c, "be1"), (b2c, "b2"), (g2c, "g2"), (be2c, "be2")):
                column(dst, ins[f"L1_gnn_{name}"], "ld_late")
            with sp.Fori(1, GROUPS) as g:
                sp.wait_ge(s["g_tr"], 4 * g)
                load_group(g)
            stage_done(sp, 1)
            sp.dma_start(bg0r[:, :], ins["L3_gnn_bg0"].partition_broadcast(P)).then_inc(s["ld_l3"], 16)
            for t in range(NT):
                sp.dma_start(bg1r[:, t, :], ins["L3_gnn_bg1"].partition_broadcast(P)).then_inc(s["ld_l3"], 16)
            for p in range(SKIPS):
                for dst, name in ((wih, "L3_gnn_Wih"), (whh, "L3_gnn_Whh")):
                    sp.dma_start(dst[:, p, :, :], ins[name][p].rearrange("(g r) h -> r g h", r=P))\
                      .then_inc(s["ld_lstm"], 16)
                for k, name in ((0, "L3_gnn_bih"), (1, "L3_gnn_bhh")):
                    sp.dma_start(lb[:, k, p, :], ins[name][p].rearrange("(g r) -> r g", r=P),
                                 allow_slow_non_contiguous=True).then_inc(s["ld_lstm"], 16)
            with sp.Fori(0, B // 2) as i:
                for u in range(2):
                    b = 2 * i + u
                    sp.wait_ge(s["z_ap"], b + 1)
                    sp.dma_start(out_v[:, :, bass.ds(b, 1), :].rearrange("p t b d -> p t (b d)"), batch(xn, b))\
                      .then_inc(s["st_out"], 16)
            sp.wait_ge(s["st_out"], 16 * B)

        @block.gpsimd
        def _(pool):
            pool.memset(ident[:, :], 0.0).then_inc(s["c_zero"], 1)
            for u in range(2):
                pool.memset(F[u], 0.0).then_inc(s["c_fzero"], 1)
            pool.memset(ones[:, :], 1.0).then_inc(s["c_ones"], 1)
            pool.memset(mhalf[:, :], -0.5).then_inc(s["c_half"], 1)
            pool.wait_ge(s["c_zero"], 1)
            pool.affine_select(out=ident[:, :], in_=ident[:, :], compare_op=ALU.not_equal, fill=1.0, base=0,
                               pattern=[[-1, P]], channel_multiplier=1).then_inc(s["c_ident"], 1)
            pool.wait_ge(s["c_half"], 1)

            def inv_sqrt(out_v, ve_v, var_v, eps, s_in, n, s_ve, s_rs, exponent=None):
                e = mhalf[:, 0:ve_v.shape[-1]]
                pool.wait_ge(s_in, n)
                pool.nop(nofuse=True)
                pool.tensor_scalar(ve_v, var_v, eps, None, ALU.add).then_inc(s_ve, 1)
                pool.wait_ge(s_ve, n)
                pool.tensor_tensor(out_v, ve_v, e, ALU.pow).then_inc(s_rs, 1)

            with pool.Fori(0, GROUPS) as g:
                for t in range(NT):
                    inv_sqrt(rstd[:, t % 2, :], ve[:, t % 2, :], mv[:, t % 2, :, 1], EPS,
                             s["ln_ag"], 4 * g + t + 1, s["ln_ve"], s["ln_rs"])
            if stop < 1:
                return
            pool.wait_ge(s["d_deg"], 3)
            pool.tensor_tensor(dg[:, 5, :], dg[:, 4, :], mhalf[:, 0:4], ALU.pow).then_inc(s["d_inv"], 1)
            pool.wait_ge(s["bn_ag"], 2)
            pool.tensor_scalar(bve[:, 0:2], bmv[:, 0:2, 1], EPS, None, ALU.add).then_inc(s["bn_ve"], 1)
            pool.wait_ge(s["bn_ve"], 1)
            pool.tensor_tensor(brs[:, 0:2], bve[:, 0:2], mhalf[:, 0:2], ALU.pow).then_inc(s["bn_rs"], 1)
            pool.wait_ge(s["bn_ag"], 3)
            pool.tensor_scalar(bve[:, 2:3], bmv[:, 2:3, 1], EPS, None, ALU.add).then_inc(s["bn_ve"], 1)
            pool.wait_ge(s["bn_ve"], 2)
            pool.tensor_tensor(brs[:, 2:3], bve[:, 2:3], mhalf[:, 0:1], ALU.pow).then_inc(s["bn_rs"], 1)
            if stop < 2:
                return
            pool.wait_ge(s["t_tr"], NT)
            for t in range(NT):
                blk = adj[:, t, t * P:(t + 1) * P]
                pool.affine_select(out=blk, in_=blk, compare_op=ALU.is_ge, fill=NEG, base=0,
                                   pattern=[[-1, P]], channel_multiplier=1).then_inc(s["a_msk"], 1)

            def norms(t, u):
                if live(t):
                    inv_sqrt(rstd[:, u, :], ve[:, u, :], mv[:, u, :, 1], EPS, s["l_ag1"], t + 1,
                             s["l_ve1"], s["l_rs1"])
                    pool.wait_ge(s["a_x2"], t + 1)
                    pool.nop(nofuse=True)
                    pool.tensor_copy(batch(xn, t), x2s[:, :, :]).then_inc(s["a_x2c"], 1)
                if live(t - 2):
                    inv_sqrt(rstd2[:, u, :], ve2[:, u, :], mv2[:, u, :, 1], EPS, s["l_ag2"], t - 1,
                             s["l_ve2"], s["l_rs2"])

            pipeline(pool, norms, 2)
            stage_done(pool, 4)

            def last(t, u):
                if live(t):
                    if late(t):
                        pool.wait_ge(s["z_tr"], t - 1)
                    pool.tensor_tensor(hs[:, u, :], H3h[:, bass.ds(t, 1), :].rearrange("p b n -> p (b n)").bitcast(F32),
                                       H3l[:, bass.ds(t, 1), :].rearrange("p b n -> p (b n)").bitcast(F32), ALU.add)\
                        .then_inc(s["z_hs"], 1)
                if live(t - 2):
                    inv_sqrt(rstd[:, u, :], ve[:, u, :], mv[:, u, :, 1], EPS, s["z_ag"], t - 1,
                             s["z_ve"], s["z_rs"])

            pipeline(pool, last, 2)

        @block.scalar
        def _(act):
            def copy(dst, src, name, **kw):
                act.activation(dst, src, ACT.Copy, **kw).then_inc(s[name], 1)

            act.wait_ge(s["ld_adj"], 32)
            act.activation(sig, alpha_c, ACT.Sigmoid).then_inc(s["m_sig"], 1)
            act.wait_ge(s["p_pe"], 1)
            copy(wT, ps[:, 0, 0:P], "p_act")
            act.wait_ge(s["p_pe"], 2)
            copy(W, ps[:, 1, 0:P], "p_act")
            for t in range(NT):
                act.wait_ge(s["m_tr"], t + 1)
                copy(Mh[:, t, :], ps[:, (5, 6, 7, 0)[t], :], "m_hi")
            act.wait_ge(s["w_tr"], 1)
            copy(w1t[:, :], ps[:, 1, 0:HID], "w_cp")
            copy(w2t[:, :, :], ps[:, 1, HID:2 * HID].rearrange("p (t o) -> p t o", t=HT), "w_cp")
            act.wait_ge(s["w_tr"], 2)
            for k, dst in enumerate((wqT, wkT, wvT)):
                copy(dst, ps[:, 5, k * P:(k + 1) * P], "w_cp")
            act.wait_ge(s["w_mm"], 1)
            copy(wqk[:, :], ps[:, 6, 0:P], "w_cp", scale=float(D) ** -0.5)
            copy(wvo[:, :], ps[:, 6, P:2 * P], "w_cp")
            act.wait_ge(s["e_mm"], 1)
            for c in range(3):
                copy(Eh[:, c, :], ps[:, 2 + c, 0:3 * P], "e_hi")
            act.wait_ge(s["e_mm"], 2)
            for c in range(3):
                copy(Eb[:, c, :], ps[:, (7, 0, 1)[c], 0:3 * P], "e_b")

            def euler(g):
                for t in range(NT):
                    act.wait_ge(s["g_tr"], 4 * g + t + 1)
                    if t >= 2:
                        act.wait_ge(s["g_mm"], 16 * g + 4 * (t - 1))
                    copy(xTh[:, t % 2, :], ps[:, 6 + t % 2, :], "g_hi")
                for t in range(NT):
                    act.wait_ge(s["g_ev"], 16 * g + 4 * (t + 1))
                    copy(Hh[:, 0, t, :], G[:, EI - 1, t, :], "eu_hi")
                for st in range(STEPS - 1):
                    for t in range(NT):
                        act.wait_ge(s["eu_sum"], 32 * g + 4 * st + t + 1)
                        copy(Hh[:, (st + 1) % 2, t, :], tsum[:, t % 2, :], "eu_hi")

            rounds(act, GROUPS, euler)
            if stop < 1:
                return
            for t in range(NT):
                act.wait_ge(s["d_tr"], t + 1)
                act.activation(Ah[:, t, :], ps[:, t, :], ACT.Copy, scale=dg[:, 5, t:t + 1]).then_inc(s["d_hi"], 1)

            def gcn(t, u):
                if live(t):
                    if late(t):
                        act.wait_ge(s["n_agg"], t - 1)
                    copy(x1h[:, u, :, :], batch(xn, t), "n_hi")
                b = t - 1
                if live(b):
                    act.wait_ge(s["n_agg"], b + 1)
                    if late(b):
                        act.wait_ge(s["n_w1"], b - 1)
                    copy(agg[:, 1 - u, :], ps[:, 1 - u, :], "n_cp")
                b = t - 2
                if live(b):
                    act.wait_ge(s["n_w1"], b + 1)
                    for h in range(HT):
                        act.activation(y1[:, h, bass.ds(b, 1), :].rearrange("p b n -> p (b n)"),
                                       ps[:, 2 + 2 * u + h, :], ACT.Identity, bias=b1c[:, h:h + 1])\
                           .then_inc(s["n_y1"], 1)

            act.wait_ge(s["d_lo"], NT)
            pipeline(act, gcn, 2)
            act.wait_ge(s["bn_sc"], 2)

            def hidden(t, u):
                if late(t):
                    act.wait_ge(s["n_w2"], t - 1)
                for h in range(HT):
                    act.activation(r1[:, u, h, :], y1[:, h, bass.ds(t, 1), :].rearrange("p b n -> p (b n)"),
                                   ACT.Relu, scale=bsc[:, h:h + 1], bias=bsh[:, h:h + 1]).then_inc(s["n_r"], 1)

            pipeline(act, hidden, 0)
            if stop < 2:
                return
            stage_done(act, 1)
            for t in range(NT):
                act.wait_ge(s["t_tr"], t + 1)
                copy(Th[:, t, :], ps[:, t, :], "t_hi")
                copy(Tf[:, t, :], ps[:, t, :], "t_cp")
            act.wait_ge(s["t_bm"], 1)
            copy(Bm[:, :], ps[:, 4, :], "t_bmc")

            def blocks(t, u):
                b, v = t - 2, u
                if live(b):
                    for n, k in enumerate(ROWORDER):
                        bank, c = ROWPACK[k]
                        sv = S[:, bank, c:c + (k + 1) * P]
                        act.wait_ge(s["a_s"], 4 * b + n + 1)
                        act.activation(sv, sv, ACT.Exp, scale=-1.0, bias=nmx[:, v, k:k + 1],
                                       accum_out=es[:, v, k:k + 1])\
                           .then_inc(s["a_p"], 1)
                b = t - 6
                if live(b):
                    act.wait_ge(s["k_h2"], b + 1)
                    act.activation(feat(H3h, b), ps[:, 4, :], ACT.Relu).then_inc(s["k_h2h"], 1)
                b = t - 1
                if live(b):
                    act.wait_ge(s["a_t2"], b + 1)
                    act.wait_ge(s["a_sc"], 4 * b)
                    copy(x2T[:, :], ps[:, 6, :], "a_x2T")
                b = t - 5
                if live(b):
                    act.wait_ge(s["k_add"], b + 1)
                    act.activation(h1[:, :], h1[:, :], ACT.Relu).then_inc(s["k_h1"], 1)
                b, v = t - 1, 1 - u
                if live(b):
                    act.wait_ge(s["a_q"], b + 1)
                    copy(qT[:, :], ps[:, 6, :], "a_qT")
                    act.wait_ge(s["a_v"], b + 1)
                    if late(b):
                        act.wait_ge(s["a_pv"], b - 1)
                    copy(vs[:, v, :, :], ps[:, 7, :].rearrange("p (t d) -> p t d", t=NT), "a_vs")
                if live(t):
                    act.wait_ge(s["a_t1"], t)
                    act.activation(zs[:, :], feat(y1[:, 0, :, :], t), ACT.Identity, scale=bsc[:, 2:3],
                                   bias=bsh[:, 2:3]).then_inc(s["a_z"], 1)
                b = t - 5
                if live(b):
                    act.wait_ge(s["k_zt"], b + 1)
                    act.wait_ge(s["k_h2"], b)
                    copy(zh[:, :], zt[:, :], "k_zh")
                b = t - 2
                if live(b):
                    act.wait_ge(s["a_pt"], b + 1)
                    act.wait_ge(s["a_pv"], b)
                    for k in range(3):
                        w = 256 if k == 2 else 512
                        copy(pT[:, k, 0:w], ps[:, k, 0:w], "a_pts")
                b, v = t - 3, 1 - u
                if live(b):
                    act.wait_ge(s["a_x3"], b + 1)
                    if late(b):
                        act.wait_ge(s["k_agg"], b - 1)
                    copy(x3h[:, v, :, :], batch(xn, b), "k_hi")
                b = t - 4
                if live(b):
                    act.wait_ge(s["k_agg"], b + 1)
                    act.wait_ge(s["k_w0"], b)
                    copy(a3[:, :], ps[:, 4, :], "k_cp")

            pipeline(act, blocks, 6)
            if stop < 4:
                return
            for j in range(2 * SKIPS):
                act.wait_ge(s["lw_tr"], j + 1)
                copy(LWh[:, j // 2, j % 2, :], ps[:, j, :], "lw_hi")
            act.wait_ge(s["lw_b"], 1)
            for p in range(SKIPS):
                n = LB[p] * NW[p]

                def cell(u, count):
                    act.wait_ge(lstm["c"][u], count)
                    act.activation(tc[:, u, 0:n], cc[:, u, 0:n], ACT.Tanh).then_inc(lstm["tc"][u], 1)

                def chunks_of_two(i):
                    for st in range(p + 1):
                        before = 0 if st == 0 else 3 + 4 * (st - 1)
                        step = base_s[p] + i * (p + 1) + st
                        for u in range(2):
                            for k, gt in enumerate(FIRST if st == 0 else ORDER):
                                act.wait_ge(lstm["mm"][u], base_g[p] + i * NG[p] + before + k + 1)
                                if gt == 3:
                                    act.wait_ge(lstm["h"][u], step)
                                act.activation(ga[:, u, gt, 0:n], ps[:, 4 * u + gt, 0:n],
                                               ACT.Tanh if gt == 2 else ACT.Sigmoid,
                                               bias=lbias[:, p, gt:gt + 1]).then_inc(lstm["act"][u], 1)
                                if p == 0 and k == 0 and u == 1:
                                    cell(0, step + 1)
                                elif p == 0 and k == 0 and not (isinstance(i, int) and i == 0):
                                    cell(1, step)
                            if p:
                                cell(u, step + 1)

                rounds(act, PAIRS[p], chunks_of_two)
                if p == 0:
                    cell(1, base_s[p + 1])
            if stop < 5:
                return
            def last(t, u):
                act.wait_ge(s["z_nb"], t + 1)
                for k in range(NT):
                    xb = xn[:, k, bass.ds(t, 1), :].rearrange("p b d -> p (b d)")
                    ins_ = act.activation(xb, xb, ACT.Identity, scale=rstd[:, u, k:k + 1], bias=nmr[:, u, k:k + 1])
                ins_.then_inc(s["z_ap"], 1)

            pipeline(act, last, 0)

        @block.vector
        def _(dve):
            def sub(hi, lo, full, name):
                dve.tensor_tensor(lo, full, hi.bitcast(F32), ALU.subtract).then_inc(s[name], 1)

            def norm_stats(tiles, st, m, s_st, s_ag, n):
                dve.nop(nofuse=True)
                for k in range(4):
                    ins_ = dve.bn_stats(st[:, k, :], tiles[k])
                ins_.then_inc(s_st, 1)
                dve.wait_ge(s_st, n)
                dve.nop(nofuse=True)
                for k in range(4):
                    ins_ = dve.bn_aggr(m[:, k, :], st[:, k, :])
                ins_.then_inc(s_ag, 1)

            def normalise(dst, src, m, r, s_ap):
                for k in range(4):
                    ins_ = dve.tensor_scalar(dst[k], src[k], m[:, k, 0:1], r[:, k:k + 1], ALU.subtract, ALU.mult)
                ins_.then_inc(s_ap, 1)

            dve.wait_ge(s["ld_w"], 64)
            dve.tensor_scalar(d_col, d_col, 0.0, 1.0, ALU.max, ALU.min).then_inc(s["p_dve"], 1)
            dve.wait_ge(s["p_act"], 1)
            dve.wait_ge(s["p_dve"], 1)
            dve.tensor_scalar(wTd, wT, d_col, DT, ALU.mult, ALU.mult).then_inc(s["p_dve"], 1)
            dve.wait_ge(s["c_ident"], 1)
            dve.wait_ge(s["c_fzero"], 2)
            dve.tensor_scalar(F[0][:, 0, 0:P], ident[:, :], DT, None, ALU.mult).then_inc(s["p_dve"], 1)
            dve.tensor_scalar(F[1][:, 0, 0:P], ident[:, :], DT, None, ALU.mult).then_inc(s["p_dve"], 1)
            dve.wait_ge(s["m_sig"], 1)
            dve.tensor_scalar(cdt, sig, 0.5 * DT, None, ALU.mult).then_inc(s["m_row"], 1)
            dve.wait_ge(s["m_row"], 1)
            dve.tensor_scalar(dgm, cdt, -1.0, 1.0 - DT, ALU.mult, ALU.add).then_inc(s["m_row"], 1)
            for t in range(NT):
                dve.tensor_scalar(Mn[:, t, :], adj[:, t, :], cdt[:, t:t + 1], None, ALU.mult)\
                   .then_inc(s["m_row"], 1)
            dve.wait_ge(s["m_row"], 6)
            for t in range(NT):
                blk = Mn[:, t, t * P:(t + 1) * P]
                dve.scalar_tensor_tensor(blk, ident[:, :], dgm[:, t:t + 1], blk, ALU.mult, ALU.add)\
                   .then_inc(s["m_row"], 1)
            dve.wait_ge(s["p_dve"], 4)
            for k in range(STEPS):
                chunks = (k + 2 + 2) // 3
                dve.wait_ge(s["f_mm"], k + 1)
                if k:
                    dve.wait_ge(s["f_add"], k)
                old, new = F[k % 2], F[(k + 1) % 2]
                dve.tensor_tensor(
                    new[:, 1:1 + 3 * chunks, :].rearrange("p (c i) n -> p c (i n)", c=chunks),
                    ps[:, 2:2 + chunks, 0:3 * FW],
                    old[:, 0:3 * chunks, :].rearrange("p (c i) n -> p c (i n)", c=chunks), ALU.add)\
                    .then_inc(s["f_add"], 1)
            dve.wait_ge(s["f_add"], STEPS)
            dve.tensor_tensor(F[0][:, 1, 0:P], F[0][:, 1, 0:P], ident[:, :], ALU.add).then_inc(s["f_add"], 1)
            for t in range(NT):
                dve.wait_ge(s["m_hi"], t + 1)
                sub(Mh[:, t, :], Ml[:, t, :], ps[:, (5, 6, 7, 0)[t], :], "m_lo")
            for c in range(3):
                dve.wait_ge(s["e_hi"], c + 1)
                sub(Eh[:, c, :], El[:, c, :], ps[:, 2 + c, 0:3 * P], "e_lo")
            dve.wait_ge(s["e_b"], 3)
            dve.wait_ge(s["w_cp"], 7)

            def euler(g):
                def turn_lo(t):
                    dve.wait_ge(s["g_hi"], 4 * g + t + 1)
                    sub(xTh[:, t % 2, :], xTl[:, t % 2, :], ps[:, 6 + t % 2, :], "g_lo")

                turn_lo(0)
                for t in range(NT):
                    if t + 1 < NT:
                        turn_lo(t + 1)
                    for b in range(GB):
                        n = 4 * t + b
                        dve.wait_ge(s["g_mm"], 16 * g + n + 1)
                        dve.tensor_tensor(
                            G[:, :, t, b * D:(b + 1) * D].rearrange("p (c i) d -> p c i d", c=3),
                            ps[:, 3 * (n % 2):3 * (n % 2) + 3, 0:3 * P].rearrange("p c (i d) -> p c i d", i=3),
                            Eb[:, :, :].rearrange("p c (i d) -> p c i d", i=3), ALU.add).then_inc(s["g_ev"], 1)
                for t in range(NT):
                    dve.wait_ge(s["eu_hi"], 32 * g + t + 1)
                    sub(Hh[:, 0, t, :], Hl[:, 0, t, :], G[:, EI - 1, t, :], "eu_lo")
                for st in range(STEPS):
                    i = EI - 2 - st
                    last = st == STEPS - 1
                    dst = [xn[:, t, bass.ds(g * GB, GB), :].rearrange("p b d -> p (b d)") for t in range(NT)] \
                        if last else [tsum[:, t % 2, :] for t in range(NT)]

                    def total(t):
                        dve.wait_ge(s["eu_mm"], 32 * g + 4 * st + t + 1)
                        if t >= 2 and not last:
                            dve.wait_ge(s["eu_lo"], 32 * g + 4 * (st + 1) + t - 1)
                        dve.tensor_tensor(dst[t], ps[:, 4 * (st % 2) + t, :], G[:, i, t, :], ALU.add)\
                           .then_inc(s["eu_sum"], 1)

                    def low(t):
                        dve.wait_ge(s["eu_hi"], 32 * g + 4 * (st + 1) + t + 1)
                        sub(Hh[:, (st + 1) % 2, t, :], Hl[:, (st + 1) % 2, t, :], dst[t], "eu_lo")

                    def ln_a(t):
                        dve.wait_ge(s["eu_sum"], 32 * g + 4 * st + t + 1)
                        if t >= 2:
                            dve.wait_ge(s["ln_rs"], 4 * g + t - 1)
                        dve.wait_ge(s["ln_ap"], 4 * g + max(t - 1, 0))
                        norm_stats(rows4(dst[t]), stats[:, t % 2], mv[:, t % 2], s["ln_st"], s["ln_ag"],
                                   4 * g + t + 1)

                    def ln_b(t):
                        dve.wait_ge(s["ln_rs"], 4 * g + t + 1)
                        normalise(rows4(dst[t]), rows4(dst[t]), mv[:, t % 2], rstd[:, t % 2], s["ln_ap"])

                    if last:
                        total(0); ln_a(0); total(1); ln_a(1); ln_b(0); total(2); ln_a(2); ln_b(1)
                        total(3); ln_a(3); ln_b(2); ln_b(3)
                    else:
                        total(0); total(1); low(0); low(1); total(2); low(2); total(3); low(3)

            rounds(dve, GROUPS, euler)
            if stop < 1:
                return
            dve.wait_ge(s["ln_ap"], GROUPS * NT)
            dve.tensor_reduce(dg[:, 0, :], adj[:, :, :], AX.X, ALU.add).then_inc(s["d_row"], 1)
            for t in range(NT):
                if t:
                    dve.wait_ge(s["d_dg"], t)
                dve.tensor_tensor_reduce(dscr[:, :], adj[:, t, t * P:(t + 1) * P], ident[:, :], 1.0, 0.0,
                                         ALU.mult, ALU.add, dg[:, 1, t:t + 1]).then_inc(s["d_dg"], 1)
            dve.wait_ge(s["d_col"], 1)
            dve.wait_ge(s["d_row"], 1)
            dve.tensor_tensor(dg[:, 2, :], ps[:, 0, 0:4], dg[:, 0, :], ALU.add).then_inc(s["d_deg"], 1)
            dve.wait_ge(s["d_deg"], 1)
            dve.wait_ge(s["d_dg"], NT)
            dve.tensor_tensor(dg[:, 3, :], dg[:, 2, :], dg[:, 1, :], ALU.subtract).then_inc(s["d_deg"], 1)
            dve.wait_ge(s["d_deg"], 2)
            dve.tensor_scalar(dg[:, 4, :], dg[:, 3, :], 1.0, None, ALU.add).then_inc(s["d_deg"], 1)
            dve.wait_ge(s["d_inv"], 1)
            for t in range(NT):
                dve.tensor_scalar(A1[:, t, :], adj[:, t, :], dg[:, 5, t:t + 1], None, ALU.mult)\
                   .then_inc(s["d_a1"], 1)
            dve.wait_ge(s["d_a1"], NT)
            for t in range(NT):
                blk = A1[:, t, t * P:(t + 1) * P]
                dve.scalar_tensor_tensor(blk, ident[:, :], dg[:, 5, t:t + 1], blk, ALU.mult, ALU.add)\
                   .then_inc(s["d_a1"], 1)
            for t in range(NT):
                dve.wait_ge(s["d_hi"], t + 1)
                dve.scalar_tensor_tensor(Al[:, t, :], ps[:, t, :], dg[:, 5, t:t + 1], Ah[:, t, :].bitcast(F32),
                                         ALU.mult, ALU.subtract).then_inc(s["d_lo"], 1)

            def gcn(t, u):
                if live(t):
                    dve.wait_ge(s["n_hi"], t + 1)
                    sub(x1h[:, u, :, :], x1l[:, u, :, :],
                        batch(xn, t), "n_lo")
                b = t - 2
                if live(b):
                    dve.wait_ge(s["n_y1"], 2 * (b + 1))
                    dve.nop(nofuse=True)
                    for h in range(HT):
                        dve.bn_stats(bst1[:, h, bass.ds(b, 1), :].rearrange("p b k -> p (b k)"),
                                     y1[:, h, bass.ds(b, 1), :].rearrange("p b n -> p (b n)"))\
                           .then_inc(s["n_st"], 1)

            def fold(a, z, gam, bet, n):
                dve.wait_ge(s["bn_rs"], n)
                dve.tensor_tensor(bsc[:, a:z], brs[:, a:z], gam, ALU.mult).then_inc(s["bn_sc"], 1)
                dve.wait_ge(s["bn_sc"], 2 * n - 1)
                dve.tensor_tensor(bms[:, a:z], bmv[:, a:z, 0], bsc[:, a:z], ALU.mult).then_inc(s["bn_ms"], 1)
                dve.wait_ge(s["bn_ms"], n)
                dve.tensor_tensor(bsh[:, a:z], bet, bms[:, a:z], ALU.subtract).then_inc(s["bn_sc"], 1)

            pipeline(dve, gcn, 2)
            dve.wait_ge(s["n_st"], 2 * B)
            for h in range(HT):
                dve.bn_aggr(bmv[:, h, :], bst1[:, h, :, :].rearrange("p b k -> p (b k)")).then_inc(s["bn_ag"], 1)
            fold(0, 2, g1c, be1c, 1)

            def outputs(t, u):
                dve.wait_ge(s["n_w2"], t + 1)
                y2 = y1[:, 0, bass.ds(t, 1), :].rearrange("p b n -> p (b n)")
                dve.tensor_scalar(y2, ps[:, u, :], b2c, None, ALU.add).then_inc(s["n_y2"], 1)
                dve.wait_ge(s["n_y2"], t + 1)
                dve.nop(nofuse=True)
                dve.bn_stats(bst2[:, bass.ds(t, 1), :].rearrange("p b k -> p (b k)"), y2).then_inc(s["n_st2"], 1)

            pipeline(dve, outputs, 0)
            dve.wait_ge(s["n_st2"], B)
            dve.bn_aggr(bmv[:, 2, :], bst2[:, :, :].rearrange("p b k -> p (b k)")).then_inc(s["bn_ag"], 1)
            fold(2, 3, g2c, be2c, 2)
            if stop < 2:
                return
            dve.wait_ge(s["bn_sc"], 4)
            for t in range(NT):
                dve.wait_ge(s["t_cp"], t + 1)
                sub(Th[:, t, :], Tl[:, t, :], ps[:, t, :], "t_lo")
            dve.wait_ge(s["t_bmc"], 1)
            dve.wait_ge(s["ld_l3"], 16 * (1 + NT))
            dve.wait_ge(s["a_msk"], NT)

            def blocks(t, u):
                if live(t):
                    dve.wait_ge(s["a_t1"], t + 1)
                    dve.wait_ge(s["a_x2"], t)
                    dve.tensor_tensor(yb[:, :, :], ps[:, 6, :].rearrange("p (t d) -> p t d", t=NT), batch(xn, t),
                                      ALU.add).then_inc(s["a_add"], 1)
                    dve.wait_ge(s["a_add"], t + 1)
                    norm_stats([yb[:, k, :] for k in range(4)], stats[:, u], mv[:, u], s["l_st1"], s["l_ag1"],
                               t + 1)
                b, v = t - 1, 1 - u
                if live(b):
                    dve.wait_ge(s["a_pt"], b)
                    for n, k in enumerate(ROWORDER):
                        bank, c = ROWPACK[k]
                        w = (k + 1) * P
                        dve.wait_ge(s["a_sc"], 4 * b + (n + 1 if n < 2 else 4))
                        dve.nop(nofuse=True)
                        dve.tensor_tensor_reduce(S[:, bank, c:c + w], ps[:, bank, c:c + w], adj[:, k, 0:w],
                                                 -1.0, -NEG, ALU.add, ALU.min, nmx[:, v, k:k + 1])\
                           .then_inc(s["a_s"], 1)
                if live(t):
                    dve.wait_ge(s["l_rs1"], t + 1)
                    dve.wait_ge(s["a_t2"], t)
                    dve.wait_ge(s["a_x2c"], t)
                    normalise([x2s[:, k, :] for k in range(4)], [yb[:, k, :] for k in range(4)],
                              mv[:, u], rstd[:, u], s["a_x2"])
                b = t - 4
                if live(b):
                    dve.wait_ge(s["k_w0"], b + 1)
                    dve.wait_ge(s["k_z"], b)
                    dve.tensor_tensor(h1[:, :], ps[:, 5, :], Bm[:, :], ALU.add).then_inc(s["k_add"], 1)
                b = t - 5
                if live(b):
                    dve.wait_ge(s["k_h2h"], b + 1)
                    dve.scalar_tensor_tensor(feat(H3l, b), ps[:, 4, :], 0.0, feat(H3h, b).bitcast(F32),
                                             ALU.max, ALU.subtract).then_inc(s["k_h2l"], 1)
                b, v = t - 2, u
                if live(b):
                    dve.wait_ge(s["a_p"], 4 * (b + 1))
                    dve.reciprocal(rs[:, v, :], es[:, v, :]).then_inc(s["a_ri"], 1)
                    dve.wait_ge(s["a_ri"], b + 1)
                    dve.wait_ge(s["a_pv"], b + 1)
                    dve.wait_ge(s["a_x2c"], b + 1)
                    xb = [xn[:, k, bass.ds(b, 1), :].rearrange("p b d -> p (b d)") for k in range(4)]
                    for k in range(4):
                        dve.scalar_tensor_tensor(xb[k], ps[:, 3, k * P:(k + 1) * P], rs[:, v, k:k + 1], xb[k],
                                                 ALU.mult, ALU.add).then_inc(s["a_y"], 1)
                    dve.wait_ge(s["a_y"], 4 * (b + 1))
                    if late(b):
                        dve.wait_ge(s["a_x3"], b - 1)
                    norm_stats(xb, stats2[:, v], mv2[:, v], s["l_st2"], s["l_ag2"], b + 1)
                b = t - 4
                if live(b):
                    dve.wait_ge(s["k_z"], b + 1)
                    dve.wait_ge(s["k_zl"], b)
                    dve.tensor_tensor(zt[:, :], ps[:, 5, :], bg1r[:, :, :].rearrange("p t d -> p (t d)"),
                                      ALU.add).then_inc(s["k_zt"], 1)
                b, v = t - 2, u
                if live(b):
                    dve.wait_ge(s["l_rs2"], b + 1)
                    normalise(xb, xb, mv2[:, v], rstd2[:, v], s["a_x3"])
                b = t - 4
                if live(b):
                    dve.wait_ge(s["k_zh"], b + 1)
                    sub(zh[:, :], zl[:, :], zt[:, :], "k_zl")
                b, v = t - 2, u
                if live(b):
                    dve.wait_ge(s["k_hi"], b + 1)
                    sub(x3h[:, v, :, :], x3l[:, v, :, :], batch(xn, b), "k_lo")

            pipeline(dve, blocks, 5)
            if stop < 4:
                return
            dve.wait_ge(s["ld_lstm"], 16 * 4 * SKIPS)
            dve.tensor_tensor(lbias[:, :, :], lb[:, 0, :, :], lb[:, 1, :, :], ALU.add).then_inc(s["lw_b"], 1)
            for j in range(2 * SKIPS):
                dve.wait_ge(s["lw_hi"], j + 1)
                sub(LWh[:, j // 2, j % 2, :], LWl[:, j // 2, j % 2, :], ps[:, j, :], "lw_lo")
            for p in range(SKIPS):
                n = LB[p] * NW[p]
                def chunks_of_two(i):
                    for st in range(p + 1):
                        for u in range(2):
                            step = base_s[p] + i * (p + 1) + st
                            rec = base_r[p] + i * p + st - 1
                            acts = base_g[p] + i * NG[p] + (0 if st == 0 else 3 + 4 * (st - 1))
                            c, x1, t1, h = (v[:, u, 0:n] for v in (cc, ig, tc, hb))
                            g_i, g_f, g_g, g_o = (ga[:, u, k, 0:n] for k in range(4))
                            dve.wait_ge(lstm["act"][u], acts + 2)
                            if st == 0:
                                dve.tensor_tensor(c, g_i, g_g, ALU.mult).then_inc(lstm["c"][u], 1)
                            else:
                                dve.tensor_tensor(x1, g_i, g_g, ALU.mult).then_inc(lstm["ig"][u], 1)
                                dve.wait_ge(lstm["act"][u], acts + 3)
                                dve.tensor_tensor(c, g_f, c, ALU.mult).then_inc(lstm["fc"][u], 1)
                                dve.wait_ge(lstm["ig"][u], rec + 1)
                                dve.wait_ge(lstm["fc"][u], rec + 1)
                                dve.tensor_tensor(c, c, x1, ALU.add).then_inc(lstm["c"][u], 1)
                            dve.wait_ge(lstm["tc"][u], step + 1)
                            dve.tensor_tensor(h, g_o, t1, ALU.mult).then_inc(lstm["h"][u], 1)
                            if st < p:
                                dh, dl, hv = sth[:, u, 0:n], stl[:, u, 0:n], h
                            else:
                                dh, dl = (v[:, bass.ds((2 * i + u) * LB[p], LB[p]), p:p + (NW[p] - 1) * (p + 1) + 1:p + 1]
                                          for v in (H3h, H3l))
                                hv = h.rearrange("p (b w) -> p b w", b=LB[p])
                            dve.wait_ge(lstm["h"][u], step + 1)
                            dve.tensor_copy(dh, hv).then_inc(lstm["hi"][u], 1)
                            dve.wait_ge(lstm["hi"][u], step + 1)
                            dve.tensor_tensor(dl, hv, dh.bitcast(F32), ALU.subtract).then_inc(lstm["lo"][u], 1)

                rounds(dve, PAIRS[p], chunks_of_two)
            if stop < 5:
                return
            def last(t, u):
                if live(t):
                    dve.wait_ge(s["z_tr"], t + 1)
                    xb = [xn[:, k, bass.ds(t, 1), :].rearrange("p b d -> p (b d)") for k in range(4)]
                    dve.tensor_tensor(batch(xn, t), ps[:, u, :].rearrange("p (t d) -> p t d", t=NT), batch(xn, t),
                                      ALU.add).then_inc(s["z_y"], 1)
                    dve.wait_ge(s["z_y"], t + 1)
                    if late(t):
                        dve.wait_ge(s["z_ap"], t - 1)
                    norm_stats(xb, stats[:, u], mv[:, u], s["z_st"], s["z_ag"], t + 1)
                b, v = t - 1, 1 - u
                if live(b):
                    dve.wait_ge(s["z_rs"], b + 1)
                    if late(b):
                        dve.wait_ge(s["z_ap"], b - 1)
                    dve.scalar_tensor_tensor(nmr[:, v, :], mv[:, v, :, 0], -1.0, rstd[:, v, :], ALU.mult, ALU.mult)\
                       .then_inc(s["z_nb"], 1)

            pipeline(dve, last, 1)

        @block.tensor
        def _(pe):
            def turn(dst, src):
                return pe.transpose(dst, src, ident[:, :])

            def split(dst, pairs, name=None):
                for k, (lh, ll, rh, rl) in enumerate(pairs):
                    pe.matmul(dst, lh, rh, start=(k == 0), stop=False)
                    pe.matmul(dst, lh, rl, start=False, stop=False)
                    mm = pe.matmul(dst, ll, rh, start=False, stop=(k == len(pairs) - 1))
                return mm

            pe.wait_ge(s["c_ident"], 1)
            pe.wait_ge(s["ld_w"], 64)
            turn(ps[:, 0, 0:P], w_raw).then_inc(s["p_pe"], 1)
            pe.wait_ge(s["p_dve"], 2)
            pe.matmul(ps[:, 1, 0:P], wTd, wT, start=True, stop=True).then_inc(s["p_pe"], 1)
            pe.wait_ge(s["p_act"], 2)
            pe.wait_ge(s["p_dve"], 4)
            for k in range(STEPS):
                chunks = (k + 2 + 2) // 3
                pe.wait_ge(s["f_add"], k)
                for c in range(chunks):
                    mm = pe.matmul(ps[:, 2 + c, 0:3 * FW], W,
                                   F[k % 2][:, 1 + 3 * c:4 + 3 * c, :].rearrange("p i n -> p (i n)"),
                                   start=True, stop=True)
                mm.then_inc(s["f_mm"], 1)
            pe.wait_ge(s["m_row"], 10)
            for m in range(NT):
                for t in range(NT):
                    mm = turn(ps[:, (5, 6, 7, 0)[m], t * P:(t + 1) * P], Mn[:, t, m * P:(m + 1) * P])
                mm.then_inc(s["m_tr"], 1)
            pe.wait_ge(s["ld_late"], 16 * 12)
            for t in range(HT):
                turn(ps[:, 1, t * P:(t + 1) * P], w1_raw[:, t, :])
            for t in range(HT):
                mm = turn(ps[:, 1, HID + t * P:HID + (t + 1) * P], w2_raw[:, t * P:(t + 1) * P])
            mm.then_inc(s["w_tr"], 1)
            pe.wait_ge(s["m_lo"], NT)
            for k in range(3):
                mm = turn(ps[:, 5, k * P:(k + 1) * P], wqkv_raw[:, k * P:(k + 1) * P])
            mm.then_inc(s["w_tr"], 1)
            pe.wait_ge(s["w_cp"], 5)
            pe.matmul(ps[:, 6, 0:P], wqT, wkT, start=True, stop=True)
            pe.matmul(ps[:, 6, P:2 * P], wvT, wo_raw, start=True, stop=True).then_inc(s["w_mm"], 1)
            pe.wait_ge(s["f_add"], STEPS + 1)
            for k in range(EI):
                mm = turn(ps[:, 2 + k // 3, (k % 3) * P:(k % 3 + 1) * P], F[0][:, 1 + k, 0:P])
            mm.then_inc(s["e_mm"], 1)
            for k in range(EI):
                mm = pe.matmul(ps[:, (7, 0, 1)[k // 3], (k % 3) * P:(k % 3 + 1) * P],
                               F[0][:, 1 + k, P:FW].to_broadcast([P, P]), ident[:, :], start=True, stop=True)
            mm.then_inc(s["e_mm"], 1)
            pe.wait_ge(s["e_lo"], 3)
            pe.wait_ge(s["e_b"], 3)

            def euler(g):
                def turn_x(t):
                    if t >= 2:
                        pe.wait_ge(s["g_lo"], 4 * g + t - 1)
                    for b in range(GB):
                        mm = turn(ps[:, 6 + t % 2, b * P:(b + 1) * P], xs[:, t, b, :])
                    mm.then_inc(s["g_tr"], 1)

                pe.wait_ge(s["ld_xs"], 16 * NT * (g + 1))
                pe.wait_ge(s["eu_sum"], 32 * g)
                turn_x(0)
                turn_x(1)
                for t in range(NT):
                    pe.wait_ge(s["g_lo"], 4 * g + t + 1)
                    for b in range(GB):
                        n = 4 * t + b
                        if n >= 2:
                            pe.wait_ge(s["g_ev"], 16 * g + n - 1)
                        xh, xl = (v[:, t % 2, b * P:(b + 1) * P] for v in (xTh, xTl))
                        dst = [ps[:, 3 * (n % 2) + c, 0:3 * P] for c in range(3)]
                        for c in range(3):
                            pe.matmul(dst[c], xh, Eh[:, c, :], start=True, stop=False)
                            pe.matmul(dst[c], xh, El[:, c, :], start=False, stop=False)
                        for c in range(3):
                            mm = pe.matmul(dst[c], xl, Eh[:, c, :], start=False, stop=True)
                        mm.then_inc(s["g_mm"], 1)
                    if t + 2 < NT:
                        turn_x(t + 2)
                for st in range(STEPS):
                    u = st % 2
                    done = 32 * g + 4 * st

                    def part(t, ks):
                        dst = ps[:, 4 * u + t, :]
                        for k in ks:
                            pe.wait_ge(s["eu_lo"], done + k + 1)
                            mh, ml = (v[:, k, t * P:(t + 1) * P] for v in (Mh, Ml))
                            pe.matmul(dst, mh, Hh[:, u, k, :], start=(k == 0), stop=False)
                            pe.matmul(dst, mh, Hl[:, u, k, :], start=False, stop=False)
                            mm = pe.matmul(dst, ml, Hh[:, u, k, :], start=False, stop=(k == NT - 1))
                        return mm

                    part(0, range(3))
                    part(1, range(3))
                    for t in range(2):
                        part(t, [3]).then_inc(s["eu_mm"], 1)
                    for t in range(2, NT):
                        part(t, range(NT)).then_inc(s["eu_mm"], 1)

            rounds(pe, GROUPS, euler)
            if stop < 1:
                return
            pe.wait_ge(s["c_ones"], 1)
            stage_done(pe, 0)
            for m in range(NT):
                for t in range(NT):
                    mm = pe.matmul(ps[:, 0, m:m + 1], adj[:, t, m * P:(m + 1) * P], ones[:, :],
                                   start=(t == 0), stop=(t == NT - 1))
            mm.then_inc(s["d_col"], 1)
            pe.wait_ge(s["d_a1"], 2 * NT)
            for m in range(NT):
                for t in range(NT):
                    mm = turn(ps[:, m, t * P:(t + 1) * P], A1[:, t, m * P:(m + 1) * P])
                mm.then_inc(s["d_tr"], 1)
            pe.wait_ge(s["d_lo"], NT)

            def gcn(t, u):
                if live(t):
                    pe.wait_ge(s["n_lo"], t + 1)
                    if late(t):
                        pe.wait_ge(s["n_cp"], t - 1)
                    split(ps[:, u, :], [(x1h[:, u, k, :], x1l[:, u, k, :], Ah[:, k, :], Al[:, k, :])
                                        for k in range(NT)]).then_inc(s["n_agg"], 1)
                b, v = t - 1, 1 - u
                if live(b):
                    pe.wait_ge(s["n_cp"], b + 1)
                    if late(b):
                        pe.wait_ge(s["n_y1"], 2 * (b - 1))
                    for h in range(HT):
                        mm = pe.matmul(ps[:, 2 + 2 * v + h, :], w1t[:, h * P:(h + 1) * P], agg[:, v, :],
                                       start=True, stop=True)
                    mm.then_inc(s["n_w1"], 1)

            pipeline(pe, gcn, 1)

            def outputs(t, u):
                pe.wait_ge(s["n_r"], 2 * (t + 1))
                if late(t):
                    pe.wait_ge(s["n_y2"], t - 1)
                for h in range(HT):
                    mm = pe.matmul(ps[:, u, :], w2t[:, h, :], r1[:, u, h, :], start=(h == 0), stop=(h == HT - 1))
                mm.then_inc(s["n_w2"], 1)

            pipeline(pe, outputs, 0)
            if stop < 2:
                return
            stage_done(pe, 1)
            for m in range(NT):
                for t in range(NT):
                    mm = turn(ps[:, m, t * P:(t + 1) * P], adj[:, t, m * P:(m + 1) * P])
                mm.then_inc(s["t_tr"], 1)
            pe.wait_ge(s["ld_l3"], 16 * (1 + NT))
            pe.wait_ge(s["t_cp"], NT)
            for m in range(NT):
                mm = pe.matmul(ps[:, 4, :], bg0r[:, :], Tf[:, m, :], start=(m == 0), stop=(m == NT - 1))
            mm.then_inc(s["t_bm"], 1)
            pe.wait_ge(s["t_lo"], NT)
            pe.wait_ge(s["t_bmc"], 1)

            def blocks(t, u):
                if live(t):
                    pe.wait_ge(s["a_z"], t + 1)
                    pe.wait_ge(s["a_qT"], t)
                    for k in range(NT):
                        mm = turn(ps[:, 6, k * P:(k + 1) * P], zs[:, k * P:(k + 1) * P])
                    mm.then_inc(s["a_t1"], 1)
                b = t - 1
                if live(b):
                    pe.wait_ge(s["a_qT"], b + 1)
                    pe.wait_ge(s["a_pts"], 3 * b)
                    for k in ROWORDER:
                        bank, c = ROWPACK[k]
                        w = (k + 1) * P
                        pe.matmul(ps[:, bank, c:c + w], qT[:, k * P:(k + 1) * P], x2T[:, 0:w],
                                  start=True, stop=True).then_inc(s["a_sc"], 1)
                b = t - 4
                if live(b):
                    pe.wait_ge(s["k_cp"], b + 1)
                    pe.wait_ge(s["k_zt"], b)
                    pe.matmul(ps[:, 5, :], wg0[:, :], a3[:, :], start=True, stop=True).then_inc(s["k_w0"], 1)
                b = t - 5
                if live(b):
                    pe.wait_ge(s["k_zl"], b + 1)
                    pe.wait_ge(s["k_cp"], b + 2 if live(b + 1) else b + 1)
                    pe.wait_ge(s["k_h2l"], b)
                    split(ps[:, 4, :], [(zh[:, k * P:(k + 1) * P], zl[:, k * P:(k + 1) * P], Th[:, k, :], Tl[:, k, :])
                                        for k in range(NT)]).then_inc(s["k_h2"], 1)
                if live(t):
                    pe.wait_ge(s["a_x2"], t + 1)
                    for k in range(NT):
                        mm = turn(ps[:, 6, k * P:(k + 1) * P], x2s[:, k, :])
                    mm.then_inc(s["a_t2"], 1)
                b, v = t - 2, u
                if live(b):
                    pe.wait_ge(s["a_pts"], 3 * (b + 1))
                    pe.wait_ge(s["a_vs"], b + 1)
                    pe.wait_ge(s["a_y"], 4 * b)
                    for k in range(NT):
                        for j in range(k + 1):
                            bank, c = COLPACK[j]
                            c += (k - j) * P
                            mm = pe.matmul(ps[:, 3, k * P:(k + 1) * P], pT[:, bank, c:c + P], vs[:, v, j, :],
                                           start=(j == 0), stop=(j == k))
                    mm.then_inc(s["a_pv"], 1)
                b = t - 4
                if live(b):
                    pe.wait_ge(s["k_h1"], b + 1)
                    for k in range(NT):
                        mm = pe.matmul(ps[:, 5, k * P:(k + 1) * P], h1[:, k * P:(k + 1) * P], wg1[:, :],
                                       start=True, stop=True)
                    mm.then_inc(s["k_z"], 1)
                if live(t):
                    pe.wait_ge(s["a_x2T"], t + 1)
                    pe.matmul(ps[:, 6, :], wqk[:, :], x2T[:, :], start=True, stop=True).then_inc(s["a_q"], 1)
                    pe.wait_ge(s["a_vs"], t)
                    for k in range(NT):
                        mm = pe.matmul(ps[:, 7, k * P:(k + 1) * P], x2T[:, k * P:(k + 1) * P], wvo[:, :],
                                       start=True, stop=True)
                    mm.then_inc(s["a_v"], 1)
                b = t - 1
                if live(b):
                    pe.wait_ge(s["a_p"], 4 * (b + 1))
                    for j in range(NT):
                        ob, oc = COLPACK[j]
                        for k in range(j, NT):
                            ib, ic = ROWPACK[k]
                            mm = turn(ps[:, ob, oc + (k - j) * P:oc + (k - j + 1) * P],
                                      S[:, ib, ic + j * P:ic + (j + 1) * P])
                    mm.then_inc(s["a_pt"], 1)
                b, v = t - 3, 1 - u
                if live(b):
                    pe.wait_ge(s["k_lo"], b + 1)
                    if not isinstance(b, int) or b >= 2:
                        pe.wait_ge(s["k_h2l"], b - 1)
                    split(ps[:, 4, :], [(x3h[:, v, k, :], x3l[:, v, k, :], Th[:, k, :], Tl[:, k, :])
                                        for k in range(NT)]).then_inc(s["k_agg"], 1)

            pipeline(pe, blocks, 5)
            if stop < 4:
                return
            stage_done(pe, 3)
            pe.wait_ge(s["ld_lstm"], 16 * 4 * SKIPS)
            for j in range(2 * SKIPS):
                for k in range(GATES):
                    mm = turn(ps[:, j, k * P:(k + 1) * P], (wih, whh)[j % 2][:, j // 2, k, :])
                mm.then_inc(s["lw_tr"], 1)
            pe.wait_ge(s["lw_lo"], 2 * SKIPS)
            for p in range(SKIPS):
                n = LB[p] * NW[p]
                def chunks_of_two(i):
                    if p:
                        for u in range(2):
                            pe.wait_ge(lstm["lo"][u], base_s[p - 1] + (i + 1) * (LB[p] // LB[p - 1]) * p)
                    for st in range(p + 1):
                        for u in range(2):
                            xh, xl = (v[:, bass.ds((2 * i + u) * LB[p], LB[p]),
                                        st:st + (NW[p] - 1) * (p + 1) + 1:p + 1] for v in (H3h, H3l))
                            before = 0 if st == 0 else 3 + 4 * (st - 1)
                            pe.wait_ge(lstm["act"][u], base_g[p] + i * NG[p] + before)
                            if st:
                                pe.wait_ge(lstm["lo"][u], base_s[p] + i * (p + 1) + st)
                            for gt in (FIRST if st == 0 else ORDER):
                                w = [(LWh[:, p, q, gt * P:(gt + 1) * P], LWl[:, p, q, gt * P:(gt + 1) * P])
                                     for q in range(2)]
                                dst = ps[:, 4 * u + gt, 0:n]
                                dst3 = dst.rearrange("p (b w) -> p b w", b=LB[p])
                                pe.matmul(dst3, w[0][0], xh, start=True, stop=False)
                                pe.matmul(dst3, w[0][0], xl, start=False, stop=False)
                                mm = pe.matmul(dst3, w[0][1], xh, start=False, stop=(st == 0))
                                if st:
                                    pe.matmul(dst, w[1][0], sth[:, u, 0:n], start=False, stop=False)
                                    pe.matmul(dst, w[1][0], stl[:, u, 0:n], start=False, stop=False)
                                    mm = pe.matmul(dst, w[1][1], sth[:, u, 0:n], start=False, stop=True)
                                mm.then_inc(lstm["mm"][u], 1)

                rounds(pe, PAIRS[p], chunks_of_two)
            if stop < 5:
                return
            def last(t, u):
                pe.wait_ge(s["z_hs"], t + 1)
                if late(t):
                    pe.wait_ge(s["z_y"], t - 1)
                for k in range(NT):
                    mm = turn(ps[:, u, k * P:(k + 1) * P], hs[:, u, k * P:(k + 1) * P])
                mm.then_inc(s["z_tr"], 1)

            stage_done(pe, 4)
            pipeline(pe, last, 0)


_INS = ["x", "adj", "L0_gnn_alpha_train", "L0_gnn_w", "L0_gnn_d", "L0_gnn_fc_in_w", "L0_gnn_fc_in_b",
        "L1_gnn_W1", "L1_gnn_b1", "L1_gnn_g1", "L1_gnn_be1", "L1_gnn_W2", "L1_gnn_b2", "L1_gnn_g2",
        "L1_gnn_be2", "L2_gnn_Wqkv", "L2_gnn_Wo", "L3_gnn_Wg0", "L3_gnn_bg0", "L3_gnn_Wg1", "L3_gnn_bg1",
        "L3_gnn_Wih", "L3_gnn_Whh", "L3_gnn_bih", "L3_gnn_bhh"]


def kernel(**inputs):
    import numpy as _np
    import concourse.bacc as _bacc
    from concourse.bass_utils import run_bass_kernel_spmd as _run

    nc = _bacc.Bacc("TRN2", target_bir_lowering=False, num_devices=1)
    arrays, args = {}, {}
    for name in _INS:
        a = _np.ascontiguousarray(inputs[name])
        arrays[f"in_{name}"] = a
        args[name] = nc.dram_tensor(f"in_{name}", a.shape, mybir.dt.from_np(a.dtype), kind="ExternalInput").ap()
    out = nc.dram_tensor("out_0", (B, N, D), F32, kind="ExternalOutput").ap()
    build(nc, args, out)
    r = _run(nc, [arrays], core_ids=[0])
    return r.results[0]["out_0"]
```

```python
from contextlib import ExitStack

import concourse.bass as bass
from concourse import mybir

F32 = mybir.dt.float32
F32R = mybir.dt.float32r
ACT = mybir.ActivationFunctionType
ALU = mybir.AluOpType
AX = mybir.AxisListType

P = 128
B, N, D = 16, 512, 128
NT = N // P
GB = 4
GROUPS = B // GB
STEPS = 8
DT = 1.0 / STEPS
EI = STEPS + 1
BABY = 3
GIANT = EI // BABY
HID = 256
HT = HID // P
SKIPS = 4
GATES = 4
EPS = 1e-5
NEG = -1e30

ROWPACK = {3: (0, 0), 2: (1, 0), 0: (1, 384), 1: (2, 0)}
MBANK = (5, 6, 7, 0)
WBANK = (0, 1, 2, 6, 7, 0, 1, 2)
TBANK = (6, 7, 0, 1)
ROWORDER = (3, 1, 2, 0)
COLPACK = {0: (0, 0), 1: (1, 0), 3: (1, 384), 2: (2, 0)}


def live(b):
    return not isinstance(b, int) or 0 <= b < B


def weights_after(t, first):
    return {first: (0, 1, 2), first + 1: (3, 4, 5), first + 2: (6, 7)}.get(t, ())


def late(b, n=2):
    return not isinstance(b, int) or b >= n




def pipeline(eng, step, depth, after=None):
    head = 2 * ((depth + 3) // 2)
    for t in range(head):
        step(t, t % 2)
    with eng.Fori(head // 2, B // 2) as i:
        step(2 * i, 0)
        step(2 * i + 1, 1)
    for t in range(B, B + depth):
        step(t, t % 2)
        if after:
            after(t)


def rounds(eng, count, body):
    body(0)
    with eng.Fori(1, count) as i:
        body(i)


def live_group(g):
    return not isinstance(g, int) or g < GROUPS


def g_before(g):
    return not isinstance(g, int) or g > 0


def groups(eng, body):
    body(0)
    body(1)
    with eng.Fori(2, GROUPS) as g:
        body(g)
    body(GROUPS)


def build(nc, ins, out):
    ctx = ExitStack()
    with ctx:
        def sem(name):
            return ctx.enter_context(nc.semaphore(name))

        def sb(name, shape, dt=F32, where=None):
            return (where or ctx).enter_context(nc.sbuf_tensor(name, shape, dt))

        ps = ctx.enter_context(nc.psum_tensor("banks", [P, 8, 512], F32))

        xn = sb("xn", [P, NT, B, D])
        adj = sb("adj_sb", [P, NT, N])
        ident = sb("ident", [P, P])
        ones = sb("ones", [P, 1])
        mhalf = sb("mhalf", [P, 16])
        w1t = sb("w1t", [P, HID])
        w2t = sb("w2t", [P, HT, P])
        wqk = sb("wqk", [P, P])
        wvo = sb("wvo", [P, P])
        wg0 = sb("wg0", [P, P])
        wg1 = sb("wg1", [P, P])
        cols = sb("cols", [P, 16])
        b1c, g1c, be1c = cols[:, 0:2], cols[:, 2:4], cols[:, 4:6]
        b2c, g2c, be2c = cols[:, 6:7], cols[:, 7:8], cols[:, 8:9]
        bg0c = cols[:, 9:10]
        stats = sb("stats", [P, 2, 4, 6])
        mv = sb("mv", [P, 2, 4, 2])
        ve = sb("ve", [P, 2, 4])
        rstd = sb("rstd", [P, 2, 4])
        stats2 = sb("stats2", [P, 2, 4, 6])
        mv2 = sb("mv2", [P, 2, 4, 2])
        ve2 = sb("ve2", [P, 2, 4])
        rstd2 = sb("rstd2", [P, 2, 4])
        zst = sb("zst", [P, 4, 4, 6])
        zmv = sb("zmv", [P, 4, 4, 2])
        zve = sb("zve", [P, 4, 4])
        zrs = sb("zrs", [P, 4, 4])
        znm = sb("znm", [P, 4, 4])
        dg = sb("deg", [P, 6, 4])
        dscr = sb("dscr", [P, P])
        lb = sb("lb", [P, 2, SKIPS, GATES])
        bsc = sb("bsc", [P, 3])
        bsh = sb("bsh", [P, 3])

        s0 = ExitStack()
        Mh = sb("Mh", [P, 3, NT, N], F32R, s0)
        Ml = sb("Ml", [P, 3, NT, N], F32R, s0)
        Eh = sb("Eh", [P, BABY, GIANT * P], F32R, s0)
        El = sb("El", [P, BABY, GIANT * P], F32R, s0)
        tsum = sb("tsum", [P, 2, GB * D], F32, s0)
        Cb = sb("Cb", [P, NT, GIANT * P], F32, s0)
        xs = sb("xs", [P, GB, NT, D], F32, s0)
        xh = sb("xh", [P, 2, NT, D], F32R, s0)
        xl = sb("xl", [P, 2, NT, D], F32R, s0)
        Vh = sb("Vh", [P, 2, BABY, N], F32R, s0)
        Vl = sb("Vl", [P, 2, BABY, N], F32R, s0)
        early_bytes = ExitStack()
        early = sb("early", [P, 3 * NT * GB * D * 2], F32, early_bytes)
        early_bytes.close()
        S12 = sb("S12", [P, NT, 2, GB, D], F32, s0)
        S2h = sb("S2h", [P, NT, GB * D], F32R, s0)
        S2l = sb("S2l", [P, NT, GB * D], F32R, s0)
        leaph = sb("leaph", [P, NT, GB * D], F32R, s0)
        leapl = sb("leapl", [P, NT, GB * D], F32R, s0)
        FW = P + 1
        at = 0

        def carve(n):
            nonlocal at
            at += n
            assert at <= early.shape[-1]
            return early[:, at - n:at]

        F = [carve(10 * FW).rearrange("p (i n) -> p i n", n=FW) for u in range(2)]
        w_raw, wT, wTd, W = carve(P), carve(P), carve(P), carve(P)
        d_col, alpha_c, sig, cdt, dgm = carve(1), carve(4), carve(4), carve(4), carve(4)
        urow = carve(2 * NT).rearrange("p (r t) -> p r t", r=2)
        Mn = carve(NT * N).rearrange("p (t n) -> p t n", t=NT)
        w1_raw = carve(HT * P).rearrange("p (t n) -> p t n", t=HT)
        w2_raw, wqkv_raw, wo_raw = carve(HID), carve(3 * P), carve(P)
        wqT, wkT, wvT = carve(P), carve(P), carve(P)
        Eb = carve(BABY * GIANT * P).rearrange("p (r n) -> p r n", r=BABY)
        Mnh = Vh[:, :, :, :].rearrange("p u r n -> p (u r) n")[:, 0:NT, :]
        Mnl = Vl[:, :, :, :].rearrange("p u r n -> p (u r) n")[:, 0:NT, :]
        s0.close()

        s1 = ExitStack()
        y1 = sb("y1", [P, HT, B, N], F32, s1)
        s1b = ExitStack()
        r1 = sb("r1", [P, 2, HT, N], F32, s1b)
        x1h = sb("x1h", [P, 2, NT, D], F32R, s1b)
        x1l = sb("x1l", [P, 2, NT, D], F32R, s1b)
        Ah = sb("Ah", [P, NT, N], F32R, s1b)
        Al = sb("Al", [P, NT, N], F32R, s1b)
        A1 = sb("A1", [P, NT, N], F32, s1b)
        agg = sb("agg", [P, 2, N], F32, s1b)
        bst1 = sb("bst1", [P, HT, B, 6], F32, s1b)
        bst2 = sb("bst2", [P, B, 6], F32, s1b)
        bmv = sb("bmv", [P, 3, 2], F32, s1b)
        bve = sb("bve", [P, 3], F32, s1b)
        brs = sb("brs", [P, 3], F32, s1b)
        bms = sb("bms", [P, 3], F32, s1b)
        s1b.close()
        s1.close()

        s3 = ExitStack()
        H3h = sb("H3h", [P, B, N], F32R, s3)
        H3l = sb("H3l", [P, B, N], F32R, s3)
        s3a = ExitStack()
        raw = ExitStack()
        wih = sb("wih_sb", [P, SKIPS, GATES, P], F32, raw)
        whh = sb("whh_sb", [P, SKIPS, GATES, P], F32, raw)
        raw.close()
        hs = sb("hs", [P, B // 2, N], F32, s3)
        Th = sb("Th", [P, NT, N], F32R, s3a)
        Tl = sb("Tl", [P, NT, N], F32R, s3a)
        zs = sb("zs", [P, N], F32, s3a)
        x2s = sb("x2s", [P, NT, D], F32, s3a)
        x2T = sb("x2T", [P, N], F32, s3a)
        qT = sb("qT", [P, N], F32, s3a)
        vs = sb("vs", [P, 2, NT, D], F32, s3a)
        S = sb("S", [P, 3, 512], F32, s3a)
        pT = sb("pT", [P, 3, 512], F32, s3a)
        yb = sb("yb", [P, NT, D], F32, s3a)
        x3h = sb("x3h", [P, 2, NT, D], F32R, s3a)
        x3l = sb("x3l", [P, 2, NT, D], F32R, s3a)
        nmx = sb("nmx", [P, 2, 4], F32, s3a)
        es = sb("es", [P, 2, 4], F32, s3a)
        rs = sb("rs", [P, 2, 4], F32, s3a)
        Bm = sb("Bm", [P, N], F32, s3a)
        a3 = sb("a3", [P, N], F32, s3a)
        h1 = sb("h1", [P, N], F32, s3a)
        zt = sb("zt", [P, N], F32, s3a)
        zh = sb("zh", [P, N], F32R, s3a)
        zl = sb("zl", [P, N], F32R, s3a)
        bg1r = sb("bg1r", [P, NT, P], F32, s3a)
        s3a.close()

        ga = sb("ga", [P, GATES, 2, 512], F32, s3)
        LWh = sb("LWh", [P, SKIPS, 2, GATES * P], F32R, s3)
        LWl = sb("LWl", [P, SKIPS, 2, GATES * P], F32R, s3)
        lbias = sb("lbias", [P, SKIPS, GATES], F32, s3)
        cc = sb("cc", [P, 2, 512], F32, s3)
        ig = sb("ig", [P, 2, 512], F32, s3)
        tc = sb("tc", [P, 2, 512], F32, s3)
        hb = sb("hb", [P, 2, 512], F32, s3)
        sth = sb("sth", [P, 2, 512], F32R, s3)
        stl = sb("stl", [P, 2, 512], F32R, s3)
        s3.close()

        S_NAMES = """
            ld_adj ld_w ld_late ld_l3 ld_lstm
            c_ident c_const c_fzero
            p_pe p_act p_dve f_mm f_add e_mm e_hi e_lo e_b
            m_sig m_row m_mm m_hi m_lo mn_hi mn_lo u_mm u_cp c_b w_tr w_cp w_mm
            x_hi x_lo v_mm v_hi v_lo g_mm g_ev s2_hi s2_lo eu_mm eu_sum eu_hi eu_lo
            ln_st ln_ag ln_ve ln_rs ln_nb ln_ap
            d_row d_col d_dg d_deg d_inv d_a1 d_tr d_hi d_lo
            n_hi n_lo n_agg n_cp n_w1 n_y1 n_st n_r n_w2 n_y2 bn_ag bn_ve bn_rs bn_ms bn_sc
            a_msk a_z a_t1 a_add a_x2 a_t2 a_x2T a_q a_v a_qT a_vs a_sc a_s a_p a_pt a_pts a_pv a_ri a_y a_x2c
            l_st1 l_ag1 l_ve1 l_rs1 l_st2 l_ag2 l_ve2 l_rs2 a_x3
            t_tr t_lo t_cp t_bm t_bmc
            k_hi k_lo k_agg k_cp k_w0 k_add k_h1 k_z k_zt k_zh k_zl k_h2 k_h2h k_h2l
            lw_tr lw_hi lw_lo lw_b
            z_hs z_hd z_tr z_st z_ag z_ve z_rs z_nb z_ap st_out""".split()
        s = {n: sem(n) for n in S_NAMES}
        ld_x = [sem(f"ld_x{u}") for u in range(GB)]
        lstm = {n: [sem(f"lstm_{n}{u}") for u in range(2)]
                for n in ("mm", "act", "ig", "fc", "c", "tc", "h", "hi", "lo")}

        def rows4(v):
            return [v[:, k * P:(k + 1) * P] for k in range(4)]

        def batch(v, b):
            return v[:, :, bass.ds(b, 1), :].rearrange("p t b d -> p t (b d)")

        def feat(v, b):
            return v[:, bass.ds(b, 1), :].rearrange("p b n -> p (b n)")

        def stage_done(eng, n):
            if n == 0:
                eng.wait_ge(s["ln_ap"], GROUPS * NT)
            elif n == 1:
                eng.wait_ge(s["bn_sc"], 4)
            elif n == 3:
                eng.wait_ge(s["k_h2l"], B)
            elif n == 4:
                for u in range(2):
                    eng.wait_ge(lstm["lo"][u], base_s[u][SKIPS])

        LB = [1, 2, 2, 4]
        PAIRS = [B // (2 * n) for n in LB]
        NG = [3 + 4 * p for p in range(SKIPS)]
        base_g = [[sum(PAIRS[q] * NG[q] for q in range(u, p)) for p in range(SKIPS + 1)] for u in range(2)]
        base_s = [[sum(PAIRS[q] * (q + 1) for q in range(u, p)) for p in range(SKIPS + 1)] for u in range(2)]
        base_r = [sum(PAIRS[q] * q for q in range(p)) for p in range(SKIPS + 1)]
        NW = [N // (p + 1) for p in range(SKIPS)]
        ORDER = [0, 2, 1, 3]
        FIRST = [0, 2, 3]

        x_v = ins["x"].rearrange("b (t p) d -> p t b d", p=P)
        out_v = out.rearrange("b (t p) d -> p t b d", p=P)

        block = ctx.enter_context(nc.Block())

        @block.sync
        def _(sp):
            def column(dst, src, name):
                sp.dma_start(dst, src.rearrange("(t p) -> p t", p=P), allow_slow_non_contiguous=True).then_inc(s[name], 16)

            sp.dma_start(w_raw, ins["L0_gnn_w"]).then_inc(s["ld_w"], 16)
            column(d_col, ins["L0_gnn_d"], "ld_w")
            sp.wait_ge(s["c_fzero"], 2)
            sp.dma_start(F[0][:, 1, 0:P], ins["L0_gnn_fc_in_w"]).then_inc(s["ld_w"], 16)
            column(F[0][:, 1, P:FW], ins["L0_gnn_fc_in_b"], "ld_w")
            sp.dma_start(adj[:, :, :], ins["adj"].rearrange("(t p) m -> p t m", p=P)).then_inc(s["ld_adj"], 16)
            column(alpha_c, ins["L0_gnn_alpha_train"], "ld_adj")

            def load_x(u, b):
                sp.dma_start(xs[:, u, :, :], x_v[:, :, bass.ds(b, 1), :].rearrange("p t b d -> p t (b d)"))\
                  .then_inc(ld_x[u], 16)

            for b in range(GB):
                load_x(b, b)
            sp.dma_start(w1_raw, ins["L1_gnn_W1"].rearrange("(t p) d -> p t d", p=P)).then_inc(s["ld_late"], 16)
            sp.dma_start(w2_raw, ins["L1_gnn_W2"]).then_inc(s["ld_late"], 16)
            sp.dma_start(wqkv_raw, ins["L2_gnn_Wqkv"]).then_inc(s["ld_late"], 16)
            sp.dma_start(wo_raw, ins["L2_gnn_Wo"]).then_inc(s["ld_late"], 16)
            sp.dma_start(wg0[:, :], ins["L3_gnn_Wg0"]).then_inc(s["ld_late"], 16)
            sp.dma_start(wg1[:, :], ins["L3_gnn_Wg1"]).then_inc(s["ld_late"], 16)
            for dst, name in ((b1c, "b1"), (g1c, "g1"), (be1c, "be1"), (b2c, "b2"), (g2c, "g2"), (be2c, "be2")):
                column(dst, ins[f"L1_gnn_{name}"], "ld_late")
            column(bg0c, ins["L3_gnn_bg0"], "ld_late")
            with sp.Fori(1, GROUPS) as g:
                for u in range(GB):
                    n = GB * g + u
                    sp.wait_ge(s["v_mm"], 3 * (n - GB) + 1)
                    sp.nop(nofuse=True)
                    sp.wait_ge(s["x_lo"], n - GB + 1)
                    sp.nop(nofuse=True)
                    load_x(u, n)
            stage_done(sp, 0)
            for t in range(NT):
                sp.dma_start(bg1r[:, t, :], ins["L3_gnn_bg1"].partition_broadcast(P)).then_inc(s["ld_l3"], 16)
            stage_done(sp, 1)
            for p in range(SKIPS):
                for dst, name in ((wih, "L3_gnn_Wih"), (whh, "L3_gnn_Whh")):
                    sp.dma_start(dst[:, p, :, :], ins[name][p].rearrange("(g r) h -> r g h", r=P))\
                      .then_inc(s["ld_lstm"], 16)
                for k, name in ((0, "L3_gnn_bih"), (1, "L3_gnn_bhh")):
                    sp.dma_start(lb[:, k, p, :], ins[name][p].rearrange("(g r) -> r g", r=P),
                                 allow_slow_non_contiguous=True).then_inc(s["ld_lstm"], 16)
            with sp.Fori(0, B // 2) as i:
                for u in range(2):
                    b = 2 * i + u
                    sp.wait_ge(s["z_ap"], b + 1)
                    sp.dma_start(out_v[:, :, bass.ds(b, 1), :].rearrange("p t b d -> p t (b d)"), batch(xn, b))\
                      .then_inc(s["st_out"], 16)
            sp.wait_ge(s["st_out"], 16 * B)

        @block.gpsimd
        def _(pool):
            pool.memset(ident[:, :], 0.0).then_inc(s["c_ident"], 1)
            for u in range(2):
                pool.memset(F[u], 0.0).then_inc(s["c_fzero"], 1)
            pool.memset(ones[:, :], 1.0).then_inc(s["c_const"], 1)
            pool.memset(mhalf[:, :], -0.5).then_inc(s["c_const"], 1)
            pool.wait_ge(s["c_ident"], 1)
            pool.affine_select(out=ident[:, :], in_=ident[:, :], compare_op=ALU.not_equal, fill=1.0, base=0,
                               pattern=[[-1, P]], channel_multiplier=1).then_inc(s["c_ident"], 1)
            pool.wait_ge(s["c_const"], 2)

            def inv_sqrt(out_v, ve_v, var_v, eps, s_in, n, s_ve, s_rs):
                e = mhalf[:, 0:ve_v.shape[-1]]
                pool.wait_ge(s_in, n)
                pool.nop(nofuse=True)
                pool.tensor_scalar(ve_v, var_v, eps, None, ALU.add).then_inc(s_ve, 1)
                pool.wait_ge(s_ve, n)
                pool.tensor_tensor(out_v, ve_v, e, ALU.pow).then_inc(s_rs, 1)

            pool.wait_ge(s["d_deg"], 3)
            pool.tensor_tensor(dg[:, 5, :], dg[:, 4, :], mhalf[:, 0:4], ALU.pow).then_inc(s["d_inv"], 1)
            with pool.Fori(0, GROUPS) as g:
                for t in range(NT):
                    inv_sqrt(zrs[:, t, :], zve[:, t, :], zmv[:, t, :, 1], EPS,
                             s["ln_ag"], 4 * g + t + 1, s["ln_ve"], s["ln_rs"])
            pool.wait_ge(s["bn_ag"], 2)
            pool.tensor_scalar(bve[:, 0:2], bmv[:, 0:2, 1], EPS, None, ALU.add).then_inc(s["bn_ve"], 1)
            pool.wait_ge(s["bn_ve"], 1)
            pool.tensor_tensor(brs[:, 0:2], bve[:, 0:2], mhalf[:, 0:2], ALU.pow).then_inc(s["bn_rs"], 1)
            pool.wait_ge(s["t_tr"], NT)
            for t in range(NT):
                blk = adj[:, t, t * P:(t + 1) * P]
                pool.affine_select(out=blk, in_=blk, compare_op=ALU.is_ge, fill=NEG, base=0,
                                   pattern=[[-1, P]], channel_multiplier=1).then_inc(s["a_msk"], 1)
            pool.wait_ge(s["bn_ag"], 3)
            pool.tensor_scalar(bve[:, 2:3], bmv[:, 2:3, 1], EPS, None, ALU.add).then_inc(s["bn_ve"], 1)
            pool.wait_ge(s["bn_ve"], 2)
            pool.tensor_tensor(brs[:, 2:3], bve[:, 2:3], mhalf[:, 0:1], ALU.pow).then_inc(s["bn_rs"], 1)
            def norms(t, u):
                if live(t):
                    inv_sqrt(rstd[:, u, :], ve[:, u, :], mv[:, u, :, 1], EPS, s["l_ag1"], t + 1,
                             s["l_ve1"], s["l_rs1"])
                    pool.wait_ge(s["a_x2"], t + 1)
                    pool.nop(nofuse=True)
                    pool.tensor_copy(batch(xn, t), x2s[:, :, :]).then_inc(s["a_x2c"], 1)
                if live(t - 2):
                    inv_sqrt(rstd2[:, u, :], ve2[:, u, :], mv2[:, u, :, 1], EPS, s["l_ag2"], t - 1,
                             s["l_ve2"], s["l_rs2"])

            pipeline(pool, norms, 2)
            def state(k, b):
                pool.tensor_tensor(hs[:, k, :], feat(H3h, b).bitcast(F32), feat(H3l, b).bitcast(F32), ALU.add)\
                    .then_inc(s["z_hs"], 1)

            def deviation(t, k):
                inv_sqrt(zrs[:, k % 4, :], zve[:, k % 4, :], zmv[:, k % 4, :, 1], EPS, s["z_ag"], t + 1,
                         s["z_ve"], s["z_rs"])

            for u in range(2):
                pool.wait_ge(lstm["lo"][u], base_s[u][SKIPS] - SKIPS)
            for k in range(B // 2):
                state(k, k)
            stage_done(pool, 4)
            for k in range(B // 2):
                if k % 2 == 0:
                    pool.wait_ge(s["z_tr"], k + 1)
                    state(k, B // 2 + k)
                deviation(k, k)
            for k in range(B // 2):
                deviation(B // 2 + k, k)

        @block.scalar
        def _(act):
            def copy(dst, src, name, **kw):
                act.activation(dst, src, ACT.Copy, **kw).then_inc(s[name], 1)

            act.wait_ge(s["ld_adj"], 32)
            act.activation(sig, alpha_c, ACT.Sigmoid).then_inc(s["m_sig"], 1)
            act.wait_ge(s["p_pe"], 1)
            copy(wT, ps[:, 0, 0:P], "p_act")
            act.wait_ge(s["p_pe"], 2)
            copy(W, ps[:, 1, 0:P], "p_act")
            act.wait_ge(s["m_row"], 10)
            for t in range(NT):
                copy(Mnh[:, t, :], Mn[:, t, :], "mn_hi")

            def power_hi(q, t):
                act.wait_ge(s["m_mm"], NT * q + t + 1)
                copy(Mh[:, q, t, :], ps[:, MBANK[t], :], "m_hi")

            for t in range(NT):
                power_hi(0, t)
            for t in range(NT):
                power_hi(1, t)
            act.wait_ge(ld_x[0], 16)
            copy(xh[:, 0, :, :], xs[:, 0, :, :], "x_hi")
            for t in range(NT):
                power_hi(2, t)
            act.wait_ge(s["w_tr"], 1)
            copy(w1t[:, :], ps[:, 1, 0:HID], "w_cp")
            copy(w2t[:, :, :], ps[:, 1, HID:2 * HID].rearrange("p (t o) -> p t o", t=HT), "w_cp")
            act.wait_ge(s["w_tr"], 2)
            for k, dst in enumerate((wqT, wkT, wvT)):
                copy(dst, ps[:, 5, k * P:(k + 1) * P], "w_cp")
            act.wait_ge(s["w_mm"], 1)
            copy(wqk[:, :], ps[:, 6, 0:P], "w_cp", scale=float(D) ** -0.5)
            copy(wvo[:, :], ps[:, 6, P:2 * P], "w_cp")
            act.wait_ge(s["e_mm"], 1)
            for c in range(3):
                copy(Eh[:, c, :], ps[:, 2 + c, 0:GIANT * P], "e_hi")
            act.wait_ge(s["e_mm"], 2)
            for c in range(3):
                copy(Eb[:, c, :], ps[:, (7, 0, 1)[c], 0:GIANT * P], "e_b")

            def euler(g):
                def x_hi(u):
                    n = GB * g + u
                    act.wait_ge(ld_x[u], 16 * (g + 1))
                    if late(n):
                        act.wait_ge(s["v_mm"], 3 * (n - 1))
                    copy(xh[:, u % 2, :, :], xs[:, u, :, :], "x_hi")

                def v_hi(u, r):
                    n = GB * g + u
                    act.wait_ge(s["v_mm"], 3 * n + r + 1)
                    if late(n):
                        act.wait_ge(s["g_mm"], NT * (n - 1))
                    copy(Vh[:, u % 2, r, :], ps[:, r, :], "v_hi")

                def s2_hi(h, u):
                    n = GB * h + u
                    act.wait_ge(s["g_ev"], NT * (n + 1))
                    if not isinstance(h, int) or h:
                        act.wait_ge(s["eu_mm"], 8 * h - 4)
                    copy(S2h[:, :, u * D:(u + 1) * D], S12[:, :, 1, u, :], "s2_hi")

                def normalise(h, t):
                    act.wait_ge(s["ln_nb"], NT * h + t + 1)
                    for b in range(GB):
                        row = xn[:, t, bass.ds(h * GB + b, 1), :].rearrange("p b d -> p (b d)")
                        ins_ = act.activation(row, row, ACT.Identity, scale=zrs[:, t, b:b + 1],
                                              bias=znm[:, t, b:b + 1])
                    ins_.then_inc(s["ln_ap"], 1)

                if live_group(g) and g_before(g):
                    x_hi(0)
                if g_before(g - 1):
                    normalise(g - 2, 3)
                if g_before(g):
                    s2_hi(g - 1, 2)
                if live_group(g):
                    v_hi(0, 0)
                    v_hi(0, 1)
                    x_hi(1)
                    v_hi(0, 2)
                if g_before(g):
                    s2_hi(g - 1, 3)
                if live_group(g):
                    v_hi(1, 0)
                    v_hi(1, 1)
                    x_hi(2)
                    v_hi(1, 2)
                if g_before(g):
                    for t in range(NT):
                        act.wait_ge(s["eu_sum"], 8 * (g - 1) + t + 1)
                        copy(leaph[:, t, :], tsum[:, t % 2, :], "eu_hi")
                if live_group(g):
                    s2_hi(g, 0)
                    v_hi(2, 0)
                    v_hi(2, 1)
                    x_hi(3)
                    v_hi(2, 2)
                    s2_hi(g, 1)
                    for r in range(BABY):
                        v_hi(3, r)
                if isinstance(g, int) and g == GROUPS:
                    for t in range(NT):
                        act.wait_ge(s["d_tr"], t + 1)
                        act.activation(Ah[:, t, :], ps[:, t, :], ACT.Copy, scale=dg[:, 5, t:t + 1])\
                           .then_inc(s["d_hi"], 1)
                    act.wait_ge(s["ln_ap"], NT)
                    for b in range(2):
                        copy(x1h[:, b, :, :], batch(xn, b), "n_hi")
                if g_before(g):
                    for t in range(NT if isinstance(g, int) and g == GROUPS else NT - 1):
                        normalise(g - 1, t)

            groups(act, euler)
            def gcn(t, u):
                if live(t) and late(t):
                    act.wait_ge(s["n_agg"], t - 1)
                    copy(x1h[:, u, :, :], batch(xn, t), "n_hi")
                b = t - 1
                if live(b):
                    act.wait_ge(s["n_agg"], b + 1)
                    if late(b):
                        act.wait_ge(s["n_w1"], b - 1)
                    copy(agg[:, 1 - u, :], ps[:, 1 - u, :], "n_cp")
                b = t - 2
                if live(b):
                    act.wait_ge(s["n_w1"], b + 1)
                    for h in range(HT):
                        act.activation(y1[:, h, bass.ds(b, 1), :].rearrange("p b n -> p (b n)"),
                                       ps[:, 2 + 2 * u + h, :], ACT.Identity, bias=b1c[:, h:h + 1])\
                           .then_inc(s["n_y1"], 1)

            act.wait_ge(s["ln_ap"], GROUPS * NT)
            pipeline(act, gcn, 2)
            for k, t in enumerate(TBANK):
                act.wait_ge(s["t_tr"], k + 1)
                copy(Th[:, k, :], ps[:, t, :], "t_cp")
            act.wait_ge(s["t_bm"], 1)
            copy(Bm[:, :], ps[:, 4, :], "t_bmc", scale=bg0c)
            act.wait_ge(s["bn_sc"], 2)

            def hidden(t, u):
                if late(t):
                    act.wait_ge(s["n_w2"], t - 1)
                for h in range(HT):
                    act.activation(r1[:, u, h, :], y1[:, h, bass.ds(t, 1), :].rearrange("p b n -> p (b n)"),
                                   ACT.Relu, scale=bsc[:, h:h + 1], bias=bsh[:, h:h + 1]).then_inc(s["n_r"], 1)

            pipeline(act, hidden, 0)
            stage_done(act, 1)
            def blocks(t, u):
                b, v = t - 2, u
                if live(b):
                    for n, k in enumerate(ROWORDER):
                        bank, c = ROWPACK[k]
                        sv = S[:, bank, c:c + (k + 1) * P]
                        act.wait_ge(s["a_s"], 4 * b + n + 1)
                        act.activation(sv, sv, ACT.Exp, scale=-1.0, bias=nmx[:, v, k:k + 1],
                                       accum_out=es[:, v, k:k + 1])\
                           .then_inc(s["a_p"], 1)
                b = t - 6
                if live(b):
                    act.wait_ge(s["k_h2"], b + 1)
                    act.activation(feat(H3h, b), ps[:, 4, :], ACT.Relu).then_inc(s["k_h2h"], 1)
                b = t - 1
                if live(b):
                    act.wait_ge(s["a_t2"], b + 1)
                    act.wait_ge(s["a_sc"], 4 * b)
                    copy(x2T[:, :], ps[:, 6, :], "a_x2T")
                b = t - 5
                if live(b):
                    act.wait_ge(s["k_add"], b + 1)
                    act.activation(h1[:, :], h1[:, :], ACT.Relu).then_inc(s["k_h1"], 1)
                b, v = t - 1, 1 - u
                if live(b):
                    act.wait_ge(s["a_q"], b + 1)
                    copy(qT[:, :], ps[:, 6, :], "a_qT")
                    act.wait_ge(s["a_v"], b + 1)
                    if late(b):
                        act.wait_ge(s["a_pv"], b - 1)
                    copy(vs[:, v, :, :], ps[:, 7, :].rearrange("p (t d) -> p t d", t=NT), "a_vs")
                if live(t):
                    act.wait_ge(s["a_t1"], t)
                    act.activation(zs[:, :], feat(y1[:, 0, :, :], t), ACT.Identity, scale=bsc[:, 2:3],
                                   bias=bsh[:, 2:3]).then_inc(s["a_z"], 1)
                b = t - 5
                if live(b):
                    act.wait_ge(s["k_zt"], b + 1)
                    act.wait_ge(s["k_h2"], b)
                    copy(zh[:, :], zt[:, :], "k_zh")
                b = t - 2
                if live(b):
                    act.wait_ge(s["a_pt"], b + 1)
                    act.wait_ge(s["a_pv"], b)
                    for k in range(3):
                        w = 256 if k == 2 else 512
                        copy(pT[:, k, 0:w], ps[:, k, 0:w], "a_pts")
                b, v = t - 3, 1 - u
                if live(b):
                    act.wait_ge(s["a_x3"], b + 1)
                    if late(b):
                        act.wait_ge(s["k_agg"], b - 1)
                    copy(x3h[:, v, :, :], batch(xn, b), "k_hi")
                b = t - 4
                if live(b):
                    act.wait_ge(s["k_agg"], b + 1)
                    act.wait_ge(s["k_w0"], b)
                    copy(a3[:, :], ps[:, 4, :], "k_cp")

            def weights(t):
                for j in weights_after(t, B + 3):
                    act.wait_ge(s["lw_tr"], j + 1)
                    copy(LWh[:, j // 2, j % 2, :], ps[:, WBANK[j], :], "lw_hi")

            pipeline(act, blocks, 6, weights)
            act.wait_ge(s["lw_b"], 1)

            def first_lstm(i):
                for k, gt in enumerate(FIRST):
                    act.wait_ge(lstm["mm"][0], NG[0] * i + k + 1)
                    if k == 0:
                        act.wait_ge(lstm["c"][0], i)
                    if gt == 3:
                        act.wait_ge(lstm["h"][0], i)
                    act.activation(ga[:, gt, :, :], ps[:, 2 * k:2 * k + 2, :], ACT.Tanh if gt == 2 else ACT.Sigmoid,
                                   bias=lbias[:, 0, gt:gt + 1]).then_inc(lstm["act"][0], 1)
                act.wait_ge(lstm["c"][0], i + 1)
                act.activation(tc[:, :, :], cc[:, :, :], ACT.Tanh).then_inc(lstm["tc"][0], 1)

            rounds(act, PAIRS[0], first_lstm)
            for p in range(1, SKIPS):
                n = LB[p] * NW[p]

                def chunks_of_two(i):
                    for st in range(p + 1):
                        for u in range(2):
                            step = base_s[u][p] + i * (p + 1) + st
                            before = base_g[u][p] + i * NG[p] + (0 if st == 0 else 3 + 4 * (st - 1))
                            for k, gt in enumerate(FIRST if st == 0 else ORDER):
                                act.wait_ge(lstm["mm"][u], before + k + 1)
                                if gt == 3:
                                    act.wait_ge(lstm["h"][u], step)
                                act.activation(ga[:, gt, u, 0:n], ps[:, 4 * u + gt, 0:n],
                                               ACT.Tanh if gt == 2 else ACT.Sigmoid,
                                               bias=lbias[:, p, gt:gt + 1]).then_inc(lstm["act"][u], 1)
                            act.wait_ge(lstm["c"][u], step + 1)
                            act.activation(tc[:, u, 0:n], cc[:, u, 0:n], ACT.Tanh).then_inc(lstm["tc"][u], 1)

                rounds(act, PAIRS[p], chunks_of_two)
            with act.Fori(0, B // 4) as q:
                for k in range(4):
                    b = 4 * q + k
                    act.wait_ge(s["z_nb"], b + 1)
                    for t in range(NT):
                        ins_ = act.activation(xn[:, t, bass.ds(b, 1), :].rearrange("p b d -> p (b d)"),
                                              ps[:, k, t * P:(t + 1) * P], ACT.Identity,
                                              scale=zrs[:, k, t:t + 1], bias=znm[:, k, t:t + 1])
                    ins_.then_inc(s["z_ap"], 1)

        @block.vector
        def _(dve):
            def sub(hi, lo, full, name):
                dve.tensor_tensor(lo, full, hi.bitcast(F32), ALU.subtract).then_inc(s[name], 1)

            def norm_stats(tiles, st, m, s_st, s_ag, n):
                dve.nop(nofuse=True)
                for k in range(4):
                    ins_ = dve.bn_stats(st[:, k, :], tiles[k])
                ins_.then_inc(s_st, 1)
                dve.wait_ge(s_st, n)
                dve.nop(nofuse=True)
                for k in range(4):
                    ins_ = dve.bn_aggr(m[:, k, :], st[:, k, :])
                ins_.then_inc(s_ag, 1)

            def normalise(dst, src, m, r, s_ap):
                for k in range(4):
                    ins_ = dve.tensor_scalar(dst[k], src[k], m[:, k, 0:1], r[:, k:k + 1], ALU.subtract, ALU.mult)
                ins_.then_inc(s_ap, 1)

            dve.wait_ge(s["ld_w"], 64)
            dve.tensor_scalar(d_col, d_col, 0.0, 1.0, ALU.max, ALU.min).then_inc(s["p_dve"], 1)
            dve.wait_ge(s["p_act"], 1)
            dve.wait_ge(s["p_dve"], 1)
            dve.tensor_scalar(wTd, wT, d_col, DT, ALU.mult, ALU.mult).then_inc(s["p_dve"], 1)
            dve.wait_ge(s["c_ident"], 2)
            dve.wait_ge(s["c_fzero"], 2)
            dve.tensor_scalar(F[0][:, 0, 0:P], ident[:, :], DT, None, ALU.mult).then_inc(s["p_dve"], 1)
            dve.tensor_scalar(F[1][:, 0, 0:P], ident[:, :], DT, None, ALU.mult).then_inc(s["p_dve"], 1)
            dve.wait_ge(s["m_sig"], 1)
            dve.tensor_scalar(cdt, sig, 0.5 * DT, None, ALU.mult).then_inc(s["m_row"], 1)
            dve.wait_ge(s["m_row"], 1)
            dve.tensor_scalar(dgm, cdt, -1.0, 1.0 - DT, ALU.mult, ALU.add).then_inc(s["m_row"], 1)
            for t in range(NT):
                dve.tensor_scalar(Mn[:, t, :], adj[:, t, :], cdt[:, t:t + 1], None, ALU.mult)\
                   .then_inc(s["m_row"], 1)
            dve.wait_ge(s["m_row"], 6)
            for t in range(NT):
                blk = Mn[:, t, t * P:(t + 1) * P]
                dve.scalar_tensor_tensor(blk, ident[:, :], dgm[:, t:t + 1], blk, ALU.mult, ALU.add)\
                   .then_inc(s["m_row"], 1)

            def f_step(k):
                chunks = (k + 2 + 2) // 3
                dve.wait_ge(s["f_mm"], k + 1)
                if k:
                    dve.wait_ge(s["f_add"], k)
                old, new = F[k % 2], F[(k + 1) % 2]
                dve.tensor_tensor(
                    new[:, 1:1 + 3 * chunks, :].rearrange("p (c i) n -> p c (i n)", c=chunks),
                    ps[:, 2:2 + chunks, 0:3 * FW],
                    old[:, 0:3 * chunks, :].rearrange("p (c i) n -> p c (i n)", c=chunks), ALU.add)\
                    .then_inc(s["f_add"], 1)

            def power_lo(q, t):
                dve.wait_ge(s["m_hi"], NT * q + t + 1)
                sub(Mh[:, q, t, :], Ml[:, q, t, :], ps[:, MBANK[t], :], "m_lo")

            dve.wait_ge(s["p_dve"], 4)
            f_step(0)
            for t in range(NT):
                dve.wait_ge(s["mn_hi"], t + 1)
                sub(Mnh[:, t, :], Mnl[:, t, :], Mn[:, t, :], "mn_lo")
            f_step(1)
            for t in range(NT):
                power_lo(0, t)
            dve.tensor_reduce(urow[:, 0, :], Mn, AX.X, ALU.add).then_inc(s["u_cp"], 1)
            for t in range(NT):
                f_step(2 + t)
                power_lo(1, t)
            dve.wait_ge(s["u_mm"], 1)
            for t in range(NT):
                dve.wait_ge(s["u_cp"], t + 1)
                dve.nop(nofuse=True)
                dve.tensor_tensor_reduce(tsum[:, t % 2, :], Mn[:, t, :], ps[:, 1, :], 1.0, 0.0, ALU.mult, ALU.add,
                                         urow[:, 1, t:t + 1]).then_inc(s["u_cp"], 1)
            dve.wait_ge(s["x_hi"], 1)
            sub(xh[:, 0, :, :], xl[:, 0, :, :], xs[:, 0, :, :], "x_lo")
            for t in range(NT):
                if t < 2:
                    f_step(6 + t)
                if t == 2:
                    dve.wait_ge(s["f_add"], STEPS)
                    dve.tensor_tensor(F[0][:, 1, 0:P], F[0][:, 1, 0:P], ident[:, :], ALU.add)\
                       .then_inc(s["f_add"], 1)
                power_lo(2, t)
            for c in range(3):
                dve.wait_ge(s["e_hi"], c + 1)
                sub(Eh[:, c, :], El[:, c, :], ps[:, 2 + c, 0:GIANT * P], "e_lo")

            def bias_sums():
                dve.wait_ge(s["e_b"], 3)
                dve.wait_ge(s["u_cp"], 1 + NT)
                dve.wait_ge(s["w_cp"], 7)
                for t in range(NT):
                    dve.scalar_tensor_tensor(Cb[:, t, :], Eb[:, 1, :], urow[:, 0, t:t + 1], Eb[:, 0, :],
                                             ALU.mult, ALU.add).then_inc(s["c_b"], 1)
                for t in range(NT):
                    dve.wait_ge(s["c_b"], t + 1)
                    dve.scalar_tensor_tensor(Cb[:, t, :], Eb[:, 2, :], urow[:, 1, t:t + 1], Cb[:, t, :],
                                             ALU.mult, ALU.add).then_inc(s["c_b"], 1)
                dve.wait_ge(s["c_b"], 2 * NT)

            def degrees():
                dve.tensor_reduce(dg[:, 0, :], adj[:, :, :], AX.X, ALU.add).then_inc(s["d_row"], 1)
                for t in range(NT):
                    if t:
                        dve.wait_ge(s["d_dg"], t)
                        dve.nop(nofuse=True)
                    dve.tensor_tensor_reduce(dscr[:, :], adj[:, t, t * P:(t + 1) * P], ident[:, :], 1.0, 0.0,
                                             ALU.mult, ALU.add, dg[:, 1, t:t + 1]).then_inc(s["d_dg"], 1)
                dve.wait_ge(s["d_col"], 1)
                dve.wait_ge(s["d_row"], 1)
                dve.tensor_tensor(dg[:, 2, :], ps[:, 6, 0:NT], dg[:, 0, :], ALU.add).then_inc(s["d_deg"], 1)
                dve.wait_ge(s["d_deg"], 1)
                dve.wait_ge(s["d_dg"], NT)
                dve.tensor_tensor(dg[:, 3, :], dg[:, 2, :], dg[:, 1, :], ALU.subtract).then_inc(s["d_deg"], 1)
                dve.wait_ge(s["d_deg"], 2)
                dve.tensor_scalar(dg[:, 4, :], dg[:, 3, :], 1.0, None, ALU.add).then_inc(s["d_deg"], 1)

            def scaled_adjacency():
                dve.wait_ge(s["d_inv"], 1)
                for t in range(NT):
                    dve.tensor_scalar(A1[:, t, :], adj[:, t, :], dg[:, 5, t:t + 1], None, ALU.mult)\
                       .then_inc(s["d_a1"], 1)
                dve.wait_ge(s["d_a1"], NT)
                for t in range(NT):
                    blk = A1[:, t, t * P:(t + 1) * P]
                    dve.scalar_tensor_tensor(blk, ident[:, :], dg[:, 5, t:t + 1], blk, ALU.mult, ALU.add)\
                       .then_inc(s["d_a1"], 1)

            def euler(g):
                h = g - 1

                def x_lo(u):
                    dve.wait_ge(s["x_hi"], GB * g + u + 1)
                    sub(xh[:, u % 2, :, :], xl[:, u % 2, :, :], xs[:, u, :, :], "x_lo")

                def v_lo(u, r):
                    dve.wait_ge(s["v_hi"], 3 * (GB * g + u) + r + 1)
                    sub(Vh[:, u % 2, r, :], Vl[:, u % 2, r, :], ps[:, r, :], "v_lo")

                def parts(h, u, between=()):
                    n = GB * h + u
                    if not isinstance(h, int) or h:
                        dve.wait_ge(s["eu_sum"], 8 * h - 4)
                    for t in range(NT):
                        dve.wait_ge(s["g_mm"], NT * n + t + 1)
                        bank = 3 + t % 3
                        dve.tensor_tensor(S12[:, t, :, u, :], ps[:, bank, D:3 * D].rearrange("p (j d) -> p j d", j=2),
                                          Cb[:, t, D:3 * D].rearrange("p (j d) -> p j d", j=2), ALU.add)
                        dve.tensor_tensor(xn[:, t, bass.ds(n, 1), :].rearrange("p b d -> p (b d)"),
                                          ps[:, bank, 0:D], Cb[:, t, 0:D], ALU.add).then_inc(s["g_ev"], 1)
                        if t in between:
                            between[t]()

                def s2_lo(h, u):
                    dve.wait_ge(s["s2_hi"], GB * h + u + 1)
                    sub(S2h[:, :, u * D:(u + 1) * D], S2l[:, :, u * D:(u + 1) * D], S12[:, :, 1, u, :], "s2_lo")

                def total(t):
                    dve.wait_ge(s["eu_mm"], 8 * h + t + 1)
                    dve.wait_ge(s["eu_lo"], 4 * h + max(t - 1, 0))
                    dve.tensor_tensor(tsum[:, t % 2, :], ps[:, 6 + t % 2, :],
                                      S12[:, t, 0, :, :].rearrange("p b d -> p (b d)"), ALU.add)\
                       .then_inc(s["eu_sum"], 1)

                def low(t):
                    dve.wait_ge(s["eu_hi"], 4 * h + t + 1)
                    sub(leaph[:, t, :], leapl[:, t, :], tsum[:, t % 2, :], "eu_lo")

                def rows(t):
                    return xn[:, t, bass.ds(h * GB, GB), :].rearrange("p b d -> p (b d)")

                def final(t):
                    dve.wait_ge(s["eu_mm"], 8 * h + 4 + t + 1)
                    dve.tensor_tensor(rows(t), ps[:, 6 + t % 2, :], rows(t), ALU.add).then_inc(s["eu_sum"], 1)

                def ln_a(t):
                    dve.wait_ge(s["eu_sum"], 8 * h + 4 + t + 1)
                    dve.wait_ge(s["ln_ap"], 4 * h)
                    norm_stats(rows4(rows(t)), zst[:, t], zmv[:, t], s["ln_st"], s["ln_ag"], 4 * h + t + 1)

                def ln_b(t, h=h):
                    dve.wait_ge(s["ln_rs"], 4 * h + t + 1)
                    dve.scalar_tensor_tensor(znm[:, t, :], zmv[:, t, :, 0], -1.0, zrs[:, t, :],
                                             ALU.mult, ALU.mult).then_inc(s["ln_nb"], 1)

                now, before = live_group(g), g_before(g)
                tail = isinstance(g, int) and g == GROUPS
                if before:
                    between = {1: lambda: x_lo(0)} if now else {}
                    if g_before(h):
                        between[0] = lambda: ln_b(3, h - 1)
                    parts(h, 2, between)
                if now:
                    v_lo(0, 0)
                if before:
                    s2_lo(h, 2)
                if now:
                    v_lo(0, 1)
                    x_lo(1)
                    v_lo(0, 2)
                if not before:
                    bias_sums()
                if before:
                    parts(h, 3)
                if now:
                    v_lo(1, 0)
                if before:
                    s2_lo(h, 3)
                if tail:
                    scaled_adjacency()
                if now:
                    v_lo(1, 1)
                    x_lo(2)
                    v_lo(1, 2)
                if before:
                    total(0)
                    total(1)
                    low(0)
                    low(1)
                    total(2)
                    low(2)
                    total(3)
                    low(3)
                if now:
                    parts(g, 0)
                    v_lo(2, 0)
                    s2_lo(g, 0)
                    v_lo(2, 1)
                    x_lo(3)
                    v_lo(2, 2)
                    parts(g, 1)
                    v_lo(3, 0)
                    s2_lo(g, 1)
                    v_lo(3, 1)
                    v_lo(3, 2)
                if not before:
                    degrees()
                if tail:
                    for t in range(NT):
                        dve.wait_ge(s["d_hi"], t + 1)
                        dve.scalar_tensor_tensor(Al[:, t, :], ps[:, t, :], dg[:, 5, t:t + 1],
                                                 Ah[:, t, :].bitcast(F32), ALU.mult, ALU.subtract)\
                           .then_inc(s["d_lo"], 1)
                    for b in range(2):
                        dve.wait_ge(s["n_hi"], b + 1)
                        sub(x1h[:, b, :, :], x1l[:, b, :, :], batch(xn, b), "n_lo")
                if before:
                    final(0)
                    ln_a(0)
                    final(1)
                    ln_a(1)
                    ln_b(0)
                    final(2)
                    ln_a(2)
                    ln_b(1)
                    final(3)
                    ln_a(3)
                    ln_b(2)
                if tail:
                    ln_b(3)

            groups(dve, euler)
            def gcn(t, u):
                if live(t) and late(t):
                    dve.wait_ge(s["n_hi"], t + 1)
                    sub(x1h[:, u, :, :], x1l[:, u, :, :],
                        batch(xn, t), "n_lo")
                b = t - 2
                if live(b):
                    dve.wait_ge(s["n_y1"], 2 * (b + 1))
                    dve.nop(nofuse=True)
                    for h in range(HT):
                        dve.bn_stats(bst1[:, h, bass.ds(b, 1), :].rearrange("p b k -> p (b k)"),
                                     y1[:, h, bass.ds(b, 1), :].rearrange("p b n -> p (b n)"))\
                           .then_inc(s["n_st"], 1)

            def fold(a, z, gam, bet, n):
                dve.wait_ge(s["bn_rs"], n)
                dve.tensor_tensor(bsc[:, a:z], brs[:, a:z], gam, ALU.mult).then_inc(s["bn_sc"], 1)
                dve.wait_ge(s["bn_sc"], 2 * n - 1)
                dve.tensor_tensor(bms[:, a:z], bmv[:, a:z, 0], bsc[:, a:z], ALU.mult).then_inc(s["bn_ms"], 1)
                dve.wait_ge(s["bn_ms"], n)
                dve.tensor_tensor(bsh[:, a:z], bet, bms[:, a:z], ALU.subtract).then_inc(s["bn_sc"], 1)

            pipeline(dve, gcn, 2)
            dve.wait_ge(s["n_st"], 2 * B)
            for h in range(HT):
                dve.bn_aggr(bmv[:, h, :], bst1[:, h, :, :].rearrange("p b k -> p (b k)")).then_inc(s["bn_ag"], 1)
            fold(0, 2, g1c, be1c, 1)
            for k, t in enumerate(TBANK):
                dve.wait_ge(s["t_cp"], k + 1)
                sub(Th[:, k, :], Tl[:, k, :], ps[:, t, :], "t_lo")

            def outputs(t, u):
                dve.wait_ge(s["n_w2"], t + 1)
                y2 = y1[:, 0, bass.ds(t, 1), :].rearrange("p b n -> p (b n)")
                dve.tensor_scalar(y2, ps[:, 2 + u, :], b2c, None, ALU.add).then_inc(s["n_y2"], 1)
                dve.wait_ge(s["n_y2"], t + 1)
                dve.nop(nofuse=True)
                dve.bn_stats(bst2[:, bass.ds(t, 1), :].rearrange("p b k -> p (b k)"), y2).then_inc(s["n_st"], 1)

            pipeline(dve, outputs, 0)
            dve.wait_ge(s["n_st"], 3 * B)
            dve.bn_aggr(bmv[:, 2, :], bst2[:, :, :].rearrange("p b k -> p (b k)")).then_inc(s["bn_ag"], 1)
            fold(2, 3, g2c, be2c, 2)
            dve.wait_ge(s["bn_sc"], 4)
            dve.wait_ge(s["t_bmc"], 1)
            dve.wait_ge(s["ld_l3"], 16 * NT)
            dve.wait_ge(s["a_msk"], NT)

            def blocks(t, u):
                if live(t):
                    dve.wait_ge(s["a_t1"], t + 1)
                    dve.wait_ge(s["a_x2"], t)
                    dve.tensor_tensor(yb[:, :, :], ps[:, 6, :].rearrange("p (t d) -> p t d", t=NT), batch(xn, t),
                                      ALU.add).then_inc(s["a_add"], 1)
                    dve.wait_ge(s["a_add"], t + 1)
                    norm_stats([yb[:, k, :] for k in range(4)], stats[:, u], mv[:, u], s["l_st1"], s["l_ag1"],
                               t + 1)
                b, v = t - 1, 1 - u
                if live(b):
                    dve.wait_ge(s["a_pt"], b)
                    for n, k in enumerate(ROWORDER):
                        bank, c = ROWPACK[k]
                        w = (k + 1) * P
                        dve.wait_ge(s["a_sc"], 4 * b + (n + 1 if n < 2 else 4))
                        dve.nop(nofuse=True)
                        dve.tensor_tensor_reduce(S[:, bank, c:c + w], ps[:, bank, c:c + w], adj[:, k, 0:w],
                                                 -1.0, -NEG, ALU.add, ALU.min, nmx[:, v, k:k + 1])\
                           .then_inc(s["a_s"], 1)
                if live(t):
                    dve.wait_ge(s["l_rs1"], t + 1)
                    dve.wait_ge(s["a_t2"], t)
                    dve.wait_ge(s["a_x2c"], t)
                    normalise([x2s[:, k, :] for k in range(4)], [yb[:, k, :] for k in range(4)],
                              mv[:, u], rstd[:, u], s["a_x2"])
                b = t - 4
                if live(b):
                    dve.wait_ge(s["k_w0"], b + 1)
                    dve.wait_ge(s["k_z"], b)
                    dve.tensor_tensor(h1[:, :], ps[:, 5, :], Bm[:, :], ALU.add).then_inc(s["k_add"], 1)
                b = t - 5
                if live(b):
                    dve.wait_ge(s["k_h2h"], b + 1)
                    dve.scalar_tensor_tensor(feat(H3l, b), ps[:, 4, :], 0.0, feat(H3h, b).bitcast(F32),
                                             ALU.max, ALU.subtract).then_inc(s["k_h2l"], 1)
                b, v = t - 2, u
                if live(b):
                    dve.wait_ge(s["a_p"], 4 * (b + 1))
                    dve.reciprocal(rs[:, v, :], es[:, v, :]).then_inc(s["a_ri"], 1)
                    dve.wait_ge(s["a_ri"], b + 1)
                    dve.wait_ge(s["a_pv"], b + 1)
                    dve.wait_ge(s["a_x2c"], b + 1)
                    xb = [xn[:, k, bass.ds(b, 1), :].rearrange("p b d -> p (b d)") for k in range(4)]
                    for k in range(4):
                        dve.scalar_tensor_tensor(xb[k], ps[:, 3, k * P:(k + 1) * P], rs[:, v, k:k + 1], xb[k],
                                                 ALU.mult, ALU.add).then_inc(s["a_y"], 1)
                    dve.wait_ge(s["a_y"], 4 * (b + 1))
                    if late(b):
                        dve.wait_ge(s["a_x3"], b - 1)
                    norm_stats(xb, stats2[:, v], mv2[:, v], s["l_st2"], s["l_ag2"], b + 1)
                b = t - 4
                if live(b):
                    dve.wait_ge(s["k_z"], b + 1)
                    dve.wait_ge(s["k_zl"], b)
                    dve.tensor_tensor(zt[:, :], ps[:, 5, :], bg1r[:, :, :].rearrange("p t d -> p (t d)"),
                                      ALU.add).then_inc(s["k_zt"], 1)
                b, v = t - 2, u
                if live(b):
                    dve.wait_ge(s["l_rs2"], b + 1)
                    normalise(xb, xb, mv2[:, v], rstd2[:, v], s["a_x3"])
                b = t - 4
                if live(b):
                    dve.wait_ge(s["k_zh"], b + 1)
                    sub(zh[:, :], zl[:, :], zt[:, :], "k_zl")
                b, v = t - 2, u
                if live(b):
                    dve.wait_ge(s["k_hi"], b + 1)
                    sub(x3h[:, v, :, :], x3l[:, v, :, :], batch(xn, b), "k_lo")

            def weights(t):
                for j in weights_after(t, B + 2):
                    dve.wait_ge(s["lw_hi"], j + 1)
                    sub(LWh[:, j // 2, j % 2, :], LWl[:, j // 2, j % 2, :], ps[:, WBANK[j], :], "lw_lo")

            pipeline(dve, blocks, 5, weights)
            dve.wait_ge(s["ld_lstm"], 16 * 4 * SKIPS)
            dve.tensor_tensor(lbias[:, :, :], lb[:, 0, :, :], lb[:, 1, :, :], ALU.add).then_inc(s["lw_b"], 1)

            def first_split(i):
                hh, hl = (v[:, bass.ds(2 * i, 2), :] for v in (H3h, H3l))
                dve.wait_ge(lstm["h"][0], i + 1)
                dve.tensor_copy(hh, hb[:, :, :]).then_inc(lstm["hi"][0], 1)
                dve.wait_ge(lstm["hi"][0], i + 1)
                dve.tensor_tensor(hl, hb[:, :, :], hh.bitcast(F32), ALU.subtract).then_inc(lstm["lo"][0], 1)

            def first_lstm(i):
                dve.wait_ge(lstm["act"][0], NG[0] * i + 2)
                dve.tensor_tensor(cc[:, :, :], ga[:, 0, :, :], ga[:, 2, :, :], ALU.mult).then_inc(lstm["c"][0], 1)
                if not isinstance(i, int):
                    first_split(i - 1)
                dve.wait_ge(lstm["tc"][0], i + 1)
                dve.wait_ge(lstm["lo"][0], i)
                dve.tensor_tensor(hb[:, :, :], ga[:, 3, :, :], tc[:, :, :], ALU.mult).then_inc(lstm["h"][0], 1)

            rounds(dve, PAIRS[0], first_lstm)
            first_split(PAIRS[0] - 1)
            dve.wait_ge(lstm["lo"][0], PAIRS[0])
            for p in range(1, SKIPS):
                n = LB[p] * NW[p]

                def chunks_of_two(i):
                    for st in range(p + 1):
                        for u in range(2):
                            step = base_s[u][p] + i * (p + 1) + st
                            rec = base_r[p] + i * p + st - 1
                            acts = base_g[u][p] + i * NG[p] + (0 if st == 0 else 3 + 4 * (st - 1))
                            c, x1, t1, h = (v[:, u, 0:n] for v in (cc, ig, tc, hb))
                            g_i, g_f, g_g, g_o = (ga[:, k, u, 0:n] for k in range(4))
                            dve.wait_ge(lstm["act"][u], acts + 2)
                            if st == 0:
                                dve.tensor_tensor(c, g_i, g_g, ALU.mult).then_inc(lstm["c"][u], 1)
                            else:
                                dve.tensor_tensor(x1, g_i, g_g, ALU.mult).then_inc(lstm["ig"][u], 1)
                                dve.wait_ge(lstm["act"][u], acts + 3)
                                dve.tensor_tensor(c, g_f, c, ALU.mult).then_inc(lstm["fc"][u], 1)
                                dve.wait_ge(lstm["ig"][u], rec + 1)
                                dve.wait_ge(lstm["fc"][u], rec + 1)
                                dve.tensor_tensor(c, c, x1, ALU.add).then_inc(lstm["c"][u], 1)
                            dve.wait_ge(lstm["tc"][u], step + 1)
                            dve.tensor_tensor(h, g_o, t1, ALU.mult).then_inc(lstm["h"][u], 1)
                            if st < p:
                                dh, dl, hv = sth[:, u, 0:n], stl[:, u, 0:n], h
                            else:
                                dh, dl = (v[:, bass.ds((2 * i + u) * LB[p], LB[p]), p:p + (NW[p] - 1) * (p + 1) + 1:p + 1]
                                          for v in (H3h, H3l))
                                hv = h.rearrange("p (b w) -> p b w", b=LB[p])
                            dve.wait_ge(lstm["h"][u], step + 1)
                            dve.tensor_copy(dh, hv).then_inc(lstm["hi"][u], 1)
                            dve.wait_ge(lstm["hi"][u], step + 1)
                            dve.tensor_tensor(dl, hv, dh.bitcast(F32), ALU.subtract).then_inc(lstm["lo"][u], 1)

                rounds(dve, PAIRS[p], chunks_of_two)
            def shift(b, k):
                dve.wait_ge(s["z_rs"], b + 1)
                dve.scalar_tensor_tensor(znm[:, k, :], zmv[:, k, :, 0], -1.0, zrs[:, k, :],
                                         ALU.mult, ALU.mult).then_inc(s["z_nb"], 1)

            def last(q):
                for k in range(4):
                    b = 4 * q + k
                    dve.wait_ge(s["z_tr"], b + 1)
                    norm_stats(rows4(ps[:, k, :]), zst[:, k], zmv[:, k], s["z_st"], s["z_ag"], b + 1)
                    if isinstance(q, int) and k % 2:
                        dve.tensor_tensor(hs[:, b, :], feat(H3h, b + B // 2).bitcast(F32),
                                          feat(H3l, b + B // 2).bitcast(F32), ALU.add).then_inc(s["z_hd"], 1)
                    if k or not isinstance(q, int) or q:
                        shift(b - 1, (k - 1) % 4)

            last(0)
            last(1)
            with dve.Fori(2, B // 4) as q:
                last(q)
            shift(B - 1, 3)

        @block.tensor
        def _(pe):
            def turn(dst, src):
                return pe.transpose(dst, src, ident[:, :])

            def split(dst, pairs):
                for k, (lh, ll, rh, rl) in enumerate(pairs):
                    pe.matmul(dst, lh, rh, start=(k == 0), stop=False)
                    pe.matmul(dst, lh, rl, start=False, stop=False)
                    mm = pe.matmul(dst, ll, rh, start=False, stop=(k == len(pairs) - 1))
                return mm

            pe.wait_ge(s["c_ident"], 2)
            pe.wait_ge(s["ld_w"], 64)
            turn(ps[:, 0, 0:P], w_raw).then_inc(s["p_pe"], 1)
            pe.wait_ge(s["p_dve"], 2)
            pe.matmul(ps[:, 1, 0:P], wTd, wT, start=True, stop=True).then_inc(s["p_pe"], 1)

            def f_step(k):
                chunks = (k + 2 + 2) // 3
                pe.wait_ge(s["f_add"], k)
                for c in range(chunks):
                    mm = pe.matmul(ps[:, 2 + c, 0:3 * FW], W,
                                   F[k % 2][:, 1 + 3 * c:4 + 3 * c, :].rearrange("p i n -> p (i n)"),
                                   start=True, stop=True)
                mm.then_inc(s["f_mm"], 1)

            pe.wait_ge(s["p_act"], 2)
            pe.wait_ge(s["p_dve"], 4)
            f_step(0)
            pe.wait_ge(s["m_row"], 10)
            for m in range(NT):
                for t in range(NT):
                    mm = turn(ps[:, MBANK[m], t * P:(t + 1) * P], Mn[:, t, m * P:(m + 1) * P])
                mm.then_inc(s["m_mm"], 1)
            f_step(1)
            pe.wait_ge(s["mn_lo"], NT)
            for q in (1, 2):
                pe.wait_ge(s["m_lo"], NT * q)
                for m in range(NT):
                    split(ps[:, MBANK[m], :], [(Mnh[:, k, m * P:(m + 1) * P], Mnl[:, k, m * P:(m + 1) * P],
                                                Mh[:, q - 1, k, :], Ml[:, q - 1, k, :]) for k in range(NT)])\
                        .then_inc(s["m_mm"], 1)
                    k = NT * (q - 1) + m + 2
                    if k < STEPS:
                        f_step(k)
                if q == 1:
                    pe.wait_ge(s["u_cp"], 1)
                    for t in range(NT):
                        mm = pe.matmul(ps[:, 1, t * P:(t + 1) * P], urow[:, 0, t:t + 1].to_broadcast([P, P]),
                                       ident[:, :], start=True, stop=True)
                    mm.then_inc(s["u_mm"], 1)
            pe.wait_ge(s["u_cp"], 1 + NT)
            pe.wait_ge(s["ld_late"], 16 * 13)
            for t in range(HT):
                turn(ps[:, 1, t * P:(t + 1) * P], w1_raw[:, t, :])
            for t in range(HT):
                mm = turn(ps[:, 1, HID + t * P:HID + (t + 1) * P], w2_raw[:, t * P:(t + 1) * P])
            mm.then_inc(s["w_tr"], 1)
            pe.wait_ge(s["m_lo"], 3 * NT)
            for k in range(3):
                mm = turn(ps[:, 5, k * P:(k + 1) * P], wqkv_raw[:, k * P:(k + 1) * P])
            mm.then_inc(s["w_tr"], 1)
            pe.wait_ge(s["w_cp"], 5)
            pe.matmul(ps[:, 6, 0:P], wqT, wkT, start=True, stop=True)
            pe.matmul(ps[:, 6, P:2 * P], wvT, wo_raw, start=True, stop=True).then_inc(s["w_mm"], 1)
            pe.wait_ge(s["f_add"], STEPS + 1)
            for k in range(EI):
                mm = turn(ps[:, 2 + k % 3, (k // 3) * P:(k // 3 + 1) * P], F[0][:, 1 + k, 0:P])
            mm.then_inc(s["e_mm"], 1)
            for k in range(EI):
                mm = pe.matmul(ps[:, (7, 0, 1)[k % 3], (k // 3) * P:(k // 3 + 1) * P],
                               F[0][:, 1 + k, P:FW].to_broadcast([P, P]), ident[:, :], start=True, stop=True)
            mm.then_inc(s["e_mm"], 1)
            pe.wait_ge(s["e_lo"], 3)
            pe.wait_ge(s["e_b"], 3)

            def euler(g):
                def powers(u):
                    n = GB * g + u
                    pe.wait_ge(ld_x[u], 16 * (g + 1))
                    if not isinstance(n, int) or n:
                        pe.wait_ge(s["v_lo"], 3 * n)
                    for k in range(NT):
                        mm = turn(ps[:, 0, k * P:(k + 1) * P], xs[:, u, k, :])
                    mm.then_inc(s["v_mm"], 1)
                    pe.wait_ge(s["x_lo"], n + 1)
                    for r in (1, 2):
                        split(ps[:, r, :], [(xh[:, u % 2, k, :], xl[:, u % 2, k, :], Mh[:, r - 1, k, :],
                                             Ml[:, r - 1, k, :]) for k in range(NT)]).then_inc(s["v_mm"], 1)

                def parts(h, u):
                    n = GB * h + u
                    pe.wait_ge(s["v_lo"], 3 * (n + 1))
                    for t in range(NT):
                        if t == 3 or not isinstance(n, int) or n:
                            pe.wait_ge(s["g_ev"], NT * n + (0, -2, -1, 1)[t])
                        split(ps[:, 3 + t % 3, 0:GIANT * P],
                              [(Vh[:, u % 2, r, t * P:(t + 1) * P], Vl[:, u % 2, r, t * P:(t + 1) * P],
                                Eh[:, r, :], El[:, r, :]) for r in range(BABY)]).then_inc(s["g_mm"], 1)

                def leap(h, half, sh, sl):
                    for t in range(NT):
                        at = 8 * h + 4 * half + t
                        if not isinstance(h, int) or at >= 2:
                            pe.wait_ge(s["eu_sum"], at - 1)
                        for k in range(NT):
                            if half and t == 0:
                                pe.wait_ge(s["eu_lo"], 4 * h + k + 1)
                            mh, ml = (v[:, 2, k, t * P:(t + 1) * P] for v in (Mh, Ml))
                            dst = ps[:, 6 + t % 2, :]
                            pe.matmul(dst, mh, sh[:, k, :], start=(k == 0), stop=False)
                            pe.matmul(dst, mh, sl[:, k, :], start=False, stop=False)
                            mm = pe.matmul(dst, ml, sh[:, k, :], start=False, stop=(k == NT - 1))
                        mm.then_inc(s["eu_mm"], 1)

                now, before = live_group(g), g_before(g)
                if now:
                    powers(0)
                if before:
                    parts(g - 1, 3)
                if not g_before(g):
                    pe.wait_ge(s["c_const"], 2)
                    for m in range(NT):
                        for t in range(NT):
                            mm = pe.matmul(ps[:, 6, m:m + 1], adj[:, t, m * P:(m + 1) * P], ones[:, :],
                                           start=(t == 0), stop=(t == NT - 1))
                    mm.then_inc(s["d_col"], 1)
                if now:
                    powers(1)
                if before:
                    pe.wait_ge(s["s2_lo"], GB * g)
                    leap(g - 1, 0, S2h, S2l)
                if isinstance(g, int) and g == GROUPS:
                    pe.wait_ge(s["d_a1"], 2 * NT)
                    for m in range(NT):
                        for t in range(NT):
                            mm = turn(ps[:, m, t * P:(t + 1) * P], A1[:, t, m * P:(m + 1) * P])
                        mm.then_inc(s["d_tr"], 1)
                if now:
                    parts(g, 0)
                    powers(2)
                    parts(g, 1)
                    powers(3)
                if before:
                    leap(g - 1, 1, leaph, leapl)
                if now:
                    parts(g, 2)

            groups(pe, euler)
            pe.wait_ge(s["d_lo"], NT)

            def gcn(t, u):
                if live(t):
                    pe.wait_ge(s["n_lo"], t + 1)
                    if late(t):
                        pe.wait_ge(s["n_cp"], t - 1)
                    split(ps[:, u, :], [(x1h[:, u, k, :], x1l[:, u, k, :], Ah[:, k, :], Al[:, k, :])
                                        for k in range(NT)]).then_inc(s["n_agg"], 1)
                b, v = t - 1, 1 - u
                if live(b):
                    pe.wait_ge(s["n_cp"], b + 1)
                    if late(b):
                        pe.wait_ge(s["n_y1"], 2 * (b - 1))
                    for h in range(HT):
                        mm = pe.matmul(ps[:, 2 + 2 * v + h, :], w1t[:, h * P:(h + 1) * P], agg[:, v, :],
                                       start=True, stop=True)
                    mm.then_inc(s["n_w1"], 1)

            pipeline(pe, gcn, 1)
            pe.wait_ge(s["n_cp"], B)
            for k, b in enumerate(TBANK):
                for t in range(NT):
                    mm = turn(ps[:, b, t * P:(t + 1) * P], adj[:, t, k * P:(k + 1) * P])
                mm.then_inc(s["t_tr"], 1)
            pe.wait_ge(s["n_y1"], 2 * B)
            pe.wait_ge(s["d_row"], 1)
            for t in range(NT):
                mm = pe.matmul(ps[:, 4, t * P:(t + 1) * P], dg[:, 0, t:t + 1].to_broadcast([P, P]), ident[:, :],
                               start=True, stop=True)
            mm.then_inc(s["t_bm"], 1)

            def outputs(t, u):
                pe.wait_ge(s["n_r"], 2 * (t + 1))
                if late(t):
                    pe.wait_ge(s["n_y2"], t - 1)
                for h in range(HT):
                    mm = pe.matmul(ps[:, 2 + u, :], w2t[:, h, :], r1[:, u, h, :], start=(h == 0), stop=(h == HT - 1))
                mm.then_inc(s["n_w2"], 1)

            pipeline(pe, outputs, 0)
            stage_done(pe, 1)
            pe.wait_ge(s["t_lo"], NT)
            pe.wait_ge(s["t_bmc"], 1)

            def blocks(t, u):
                if live(t):
                    pe.wait_ge(s["a_z"], t + 1)
                    pe.wait_ge(s["a_qT"], t)
                    for k in range(NT):
                        mm = turn(ps[:, 6, k * P:(k + 1) * P], zs[:, k * P:(k + 1) * P])
                    mm.then_inc(s["a_t1"], 1)
                b = t - 1
                if live(b):
                    pe.wait_ge(s["a_qT"], b + 1)
                    pe.wait_ge(s["a_pts"], 3 * b)
                    for k in ROWORDER:
                        bank, c = ROWPACK[k]
                        w = (k + 1) * P
                        pe.matmul(ps[:, bank, c:c + w], qT[:, k * P:(k + 1) * P], x2T[:, 0:w],
                                  start=True, stop=True).then_inc(s["a_sc"], 1)
                b = t - 4
                if live(b):
                    pe.wait_ge(s["k_cp"], b + 1)
                    pe.wait_ge(s["k_zt"], b)
                    pe.matmul(ps[:, 5, :], wg0[:, :], a3[:, :], start=True, stop=True).then_inc(s["k_w0"], 1)
                b = t - 5
                if live(b):
                    pe.wait_ge(s["k_zl"], b + 1)
                    pe.wait_ge(s["k_cp"], b + 2 if live(b + 1) else b + 1)
                    pe.wait_ge(s["k_h2l"], b)
                    split(ps[:, 4, :], [(zh[:, k * P:(k + 1) * P], zl[:, k * P:(k + 1) * P], Th[:, k, :], Tl[:, k, :])
                                        for k in range(NT)]).then_inc(s["k_h2"], 1)
                if live(t):
                    pe.wait_ge(s["a_x2"], t + 1)
                    for k in range(NT):
                        mm = turn(ps[:, 6, k * P:(k + 1) * P], x2s[:, k, :])
                    mm.then_inc(s["a_t2"], 1)
                b, v = t - 2, u
                if live(b):
                    pe.wait_ge(s["a_pts"], 3 * (b + 1))
                    pe.wait_ge(s["a_vs"], b + 1)
                    pe.wait_ge(s["a_y"], 4 * b)
                    for k in range(NT):
                        for j in range(k + 1):
                            bank, c = COLPACK[j]
                            c += (k - j) * P
                            mm = pe.matmul(ps[:, 3, k * P:(k + 1) * P], pT[:, bank, c:c + P], vs[:, v, j, :],
                                           start=(j == 0), stop=(j == k))
                    mm.then_inc(s["a_pv"], 1)
                b = t - 4
                if live(b):
                    pe.wait_ge(s["k_h1"], b + 1)
                    for k in range(NT):
                        mm = pe.matmul(ps[:, 5, k * P:(k + 1) * P], h1[:, k * P:(k + 1) * P], wg1[:, :],
                                       start=True, stop=True)
                    mm.then_inc(s["k_z"], 1)
                if live(t):
                    pe.wait_ge(s["a_x2T"], t + 1)
                    pe.matmul(ps[:, 6, :], wqk[:, :], x2T[:, :], start=True, stop=True).then_inc(s["a_q"], 1)
                    pe.wait_ge(s["a_vs"], t)
                    for k in range(NT):
                        mm = pe.matmul(ps[:, 7, k * P:(k + 1) * P], x2T[:, k * P:(k + 1) * P], wvo[:, :],
                                       start=True, stop=True)
                    mm.then_inc(s["a_v"], 1)
                b = t - 1
                if live(b):
                    pe.wait_ge(s["a_p"], 4 * (b + 1))
                    for j in range(NT):
                        ob, oc = COLPACK[j]
                        for k in range(j, NT):
                            ib, ic = ROWPACK[k]
                            mm = turn(ps[:, ob, oc + (k - j) * P:oc + (k - j + 1) * P],
                                      S[:, ib, ic + j * P:ic + (j + 1) * P])
                    mm.then_inc(s["a_pt"], 1)
                b, v = t - 3, 1 - u
                if live(b):
                    pe.wait_ge(s["k_lo"], b + 1)
                    if not isinstance(b, int) or b >= 2:
                        pe.wait_ge(s["k_h2l"], b - 1)
                    split(ps[:, 4, :], [(x3h[:, v, k, :], x3l[:, v, k, :], Th[:, k, :], Tl[:, k, :])
                                        for k in range(NT)]).then_inc(s["k_agg"], 1)

            def weights(t):
                for j in weights_after(t, B + 2):
                    pe.wait_ge(s["ld_lstm"], 16 * 4 * SKIPS)
                    if j >= 5:
                        pe.wait_ge(s["lw_lo"], j - 4)
                    for k in range(GATES):
                        mm = turn(ps[:, WBANK[j], k * P:(k + 1) * P], (wih, whh)[j % 2][:, j // 2, k, :])
                    mm.then_inc(s["lw_tr"], 1)

            pipeline(pe, blocks, 5, weights)
            pe.wait_ge(s["lw_lo"], 2 * SKIPS)

            def first_lstm(i):
                for k, gt in enumerate(FIRST):
                    if not isinstance(i, int):
                        pe.wait_ge(lstm["act"][0], NG[0] * (i - 1) + k + 1)
                    elif k == 2:
                        stage_done(pe, 3)
                    wh, wl = (v[:, 0, 0, gt * P:(gt + 1) * P] for v in (LWh, LWl))
                    for u in range(2):
                        dst, xh, xl = ps[:, 2 * k + u, :], feat(H3h, 2 * i + u), feat(H3l, 2 * i + u)
                        pe.matmul(dst, wh, xh, start=True, stop=False)
                        pe.matmul(dst, wh, xl, start=False, stop=False)
                        mm = pe.matmul(dst, wl, xh, start=False, stop=True)
                    mm.then_inc(lstm["mm"][0], 1)

            rounds(pe, PAIRS[0], first_lstm)
            pe.wait_ge(lstm["act"][0], base_g[0][1])
            for p in range(1, SKIPS):
                n = LB[p] * NW[p]

                def chunks_of_two(i):
                    for u in range(min(p, 2)):
                        pe.wait_ge(lstm["lo"][u], base_s[u][p - 1] + (i + 1) * (LB[p] // LB[p - 1]) * p)
                    for st in range(p + 1):
                        for u in range(2):
                            xh, xl = (v[:, bass.ds((2 * i + u) * LB[p], LB[p]),
                                        st:st + (NW[p] - 1) * (p + 1) + 1:p + 1] for v in (H3h, H3l))
                            before = 0 if st == 0 else 3 + 4 * (st - 1)
                            pe.wait_ge(lstm["act"][u], base_g[u][p] + i * NG[p] + before)
                            gates = FIRST if st == 0 else ORDER
                            for gt in gates:
                                wh, wl = (v[:, p, 0, gt * P:(gt + 1) * P] for v in (LWh, LWl))
                                dst = ps[:, 4 * u + gt, 0:n].rearrange("p (b w) -> p b w", b=LB[p])
                                pe.matmul(dst, wh, xh, start=True, stop=False)
                                pe.matmul(dst, wh, xl, start=False, stop=False)
                                mm = pe.matmul(dst, wl, xh, start=False, stop=(st == 0))
                                if st == 0:
                                    mm.then_inc(lstm["mm"][u], 1)
                            if st:
                                pe.wait_ge(lstm["lo"][u], base_s[u][p] + i * (p + 1) + st)
                                for gt in gates:
                                    wh, wl = (v[:, p, 1, gt * P:(gt + 1) * P] for v in (LWh, LWl))
                                    dst = ps[:, 4 * u + gt, 0:n]
                                    pe.matmul(dst, wh, sth[:, u, 0:n], start=False, stop=False)
                                    pe.matmul(dst, wh, stl[:, u, 0:n], start=False, stop=False)
                                    pe.matmul(dst, wl, sth[:, u, 0:n], start=False, stop=True)\
                                        .then_inc(lstm["mm"][u], 1)

                rounds(pe, PAIRS[p], chunks_of_two)
            pe.wait_ge(lstm["act"][0], base_g[0][SKIPS])
            for b in range(B):
                k = b % (B // 2)
                if b < B // 2:
                    pe.wait_ge(s["z_hs"], b + 1)
                elif k % 2:
                    pe.wait_ge(s["z_hd"], (k + 1) // 2)
                else:
                    pe.wait_ge(s["z_hs"], B // 2 + k // 2 + 1)
                if b >= 4:
                    pe.wait_ge(s["z_ap"], b - 3)
                for t in range(NT):
                    dst = ps[:, b % 4, t * P:(t + 1) * P]
                    pe.matmul(dst, hs[:, k, t * P:(t + 1) * P], ident[:, :], start=True, stop=False)
                    mm = pe.matmul(dst, ident[:, :], xn[:, t, b, :], start=False, stop=True)
                mm.then_inc(s["z_tr"], 1)


_INS = ["x", "adj", "L0_gnn_alpha_train", "L0_gnn_w", "L0_gnn_d", "L0_gnn_fc_in_w", "L0_gnn_fc_in_b",
        "L1_gnn_W1", "L1_gnn_b1", "L1_gnn_g1", "L1_gnn_be1", "L1_gnn_W2", "L1_gnn_b2", "L1_gnn_g2",
        "L1_gnn_be2", "L2_gnn_Wqkv", "L2_gnn_Wo", "L3_gnn_Wg0", "L3_gnn_bg0", "L3_gnn_Wg1", "L3_gnn_bg1",
        "L3_gnn_Wih", "L3_gnn_Whh", "L3_gnn_bih", "L3_gnn_bhh"]


def kernel(**inputs):
    import numpy as _np
    import concourse.bacc as _bacc
    from concourse.bass_utils import run_bass_kernel_spmd as _run

    nc = _bacc.Bacc("TRN2", target_bir_lowering=False, num_devices=1)
    arrays, args = {}, {}
    for name in _INS:
        a = _np.ascontiguousarray(inputs[name])
        arrays[f"in_{name}"] = a
        args[name] = nc.dram_tensor(f"in_{name}", a.shape, mybir.dt.from_np(a.dtype), kind="ExternalInput").ap()
    out = nc.dram_tensor("out_0", (B, N, D), F32, kind="ExternalOutput").ap()
    build(nc, args, out)
    r = _run(nc, [arrays], core_ids=[0])
    return r.results[0]["out_0"]
```
